# Optimizing a Trainium2 kernel written in Bass

```python
import numpy as np
import jax
import jax.numpy as jnp

def _softmax(x, axis=-1):
    return jax.nn.softmax(x, axis=axis)

def _gelu(x):
    return jax.nn.gelu(x, approximate=True)

def _silu(x):
    return jax.nn.silu(x)

def _sigmoid(x):
    return jax.nn.sigmoid(x)

def _layernorm(x, axis=-1, eps=1e-05):
    m = jnp.mean(x, axis=axis, keepdims=True)
    v = jnp.var(x, axis=axis, keepdims=True)
    return (x - m) / jnp.sqrt(v + eps)

def _scatter_add(tgt, idx, src, axis=0):
    return tgt.at[idx].add(src)

def _segment_sum(src, seg, n):
    return jax.ops.segment_sum(src, seg, n)
kernel_name = 'mk_seq_preln_d1_jaxref_r8_7a6895'

def setup_inputs(seed: int=0):
    np.random.seed(seed)
    _w = jnp.asarray

    def _L0_attn_setup():
        import jax, jax.numpy as jnp
        import numpy as np
        HEAD_SIZE = 64
        key = jax.random.key(seed)
        ks = jax.random.split(key, 5)
        B, N, D, H, E, O = (2, 256, 128, 16, HEAD_SIZE, 128)
        return {'query': jax.random.normal(ks[0], (B, N, D), dtype=jnp.float32), 'Wq': jax.random.normal(ks[1], (H, D, E), dtype=jnp.float32) / np.sqrt(D), 'Wk': jax.random.normal(ks[2], (H, D, E), dtype=jnp.float32) / np.sqrt(D), 'Wv': jax.random.normal(ks[3], (H, D, E), dtype=jnp.float32) / np.sqrt(D), 'Wp': jax.random.normal(ks[4], (H * E, O), dtype=jnp.float32) / np.sqrt(H * E), 'bp': jnp.zeros((O,), dtype=jnp.float32)}
    _L0_attn_in = _L0_attn_setup()

    def _L0_ffn_setup():
        import jax, jax.numpy as jnp
        import numpy as np
        EPS = 1e-06
        N_EXPERTS = 8

        def _rms_norm(x, scale, eps=EPS):
            mean_sq = jnp.mean(x.astype(jnp.float32) ** 2, axis=-1, keepdims=True)
            s = scale.astype(jnp.float32) * jax.lax.rsqrt(mean_sq + eps)
            return x * s.astype(x.dtype)

        def _dist2(x, y):
            nx = jnp.sum(x ** 2, axis=-1)[..., :, None]
            ny = jnp.sum(y ** 2, axis=-1)[..., None, :]
            return nx + ny - 2.0 * (x @ y.T)
        key = jax.random.key(seed)
        ks = jax.random.split(key, 5)
        dim, hidden, E = (128, 256, N_EXPERTS)
        x = jax.random.normal(ks[0], (4, 256, dim), dtype=jnp.float32)
        scale = jnp.ones((dim,), dtype=jnp.float32)
        centroids = jax.random.normal(ks[1], (E, dim), dtype=jnp.float32)
        up_w = jax.random.normal(ks[2], (E, dim, hidden * 2), dtype=jnp.float32) * dim ** (-0.5)
        down_w = jax.random.normal(ks[3], (E, hidden, dim), dtype=jnp.float32) * hidden ** (-0.5)
        return {'x': x, 'scale': scale, 'centroids': centroids, 'up_w': up_w, 'down_w': down_w}
    _L0_ffn_in = _L0_ffn_setup()
    _d = {'L0_attn_query': _L0_attn_in['query'], 'L0_attn_Wq': _L0_attn_in['Wq'], 'L0_attn_Wk': _L0_attn_in['Wk'], 'L0_attn_Wv': _L0_attn_in['Wv'], 'L0_attn_Wp': _L0_attn_in['Wp'], 'L0_attn_bp': _L0_attn_in['bp'], 'L0_ffn_scale': _L0_ffn_in['scale'], 'L0_ffn_centroids': _L0_ffn_in['centroids'], 'L0_ffn_up_w': _L0_ffn_in['up_w'], 'L0_ffn_down_w': _L0_ffn_in['down_w']}
    _x0 = _d['L0_attn_query']
    _d['L0_attn_query'] = jax.random.normal(jax.random.fold_in(jax.random.key(seed), 1), (8, 512, 128), dtype=_x0.dtype)
    del _x0
    return _d

def reference(L0_attn_query, L0_attn_Wq, L0_attn_Wk, L0_attn_Wv, L0_attn_Wp, L0_attn_bp, L0_ffn_scale, L0_ffn_centroids, L0_ffn_up_w, L0_ffn_down_w):

    def _L0_attn_ref(query, Wq, Wk, Wv, Wp, bp):
        import jax, jax.numpy as jnp
        import numpy as np
        HEAD_SIZE = 64
        B, N, D = query.shape
        H, _, E = Wq.shape
        scale = 1.0 / jnp.sqrt(jnp.asarray(E, query.dtype))
        q = jnp.einsum('bnd,hde->bhne', query, Wq) * scale
        k = jnp.einsum('bmd,hde->bhme', query, Wk)
        v = jnp.einsum('bmd,hde->bhme', query, Wv)
        logits = jnp.einsum('bhne,bhme->bhnm', q, k)
        attn = jax.nn.softmax(logits, axis=-1)
        out = jnp.einsum('bhnm,bhme->bnhe', attn, v)
        out = jnp.swapaxes(out, -1, -2).reshape(B, N, E * H)
        return jnp.dot(out, Wp) + bp

    def _L0_ffn_ref(x, scale, centroids, up_w, down_w):
        import jax, jax.numpy as jnp
        import numpy as np
        EPS = 1e-06
        N_EXPERTS = 8

        def _rms_norm(x, scale, eps=EPS):
            mean_sq = jnp.mean(x.astype(jnp.float32) ** 2, axis=-1, keepdims=True)
            s = scale.astype(jnp.float32) * jax.lax.rsqrt(mean_sq + eps)
            return x * s.astype(x.dtype)

        def _dist2(x, y):
            nx = jnp.sum(x ** 2, axis=-1)[..., :, None]
            ny = jnp.sum(y ** 2, axis=-1)[..., None, :]
            return nx + ny - 2.0 * (x @ y.T)
        skip = x
        xn = _rms_norm(x, scale)
        ids = jnp.argmin(_dist2(xn, centroids), axis=-1)
        out = jnp.zeros_like(x)
        for e in range(N_EXPERTS):
            h = jnp.einsum('bsd,dh->bsh', xn, up_w[e])
            a, g = jnp.split(h, 2, axis=-1)
            y = jnp.einsum('bsh,hd->bsd', a * jax.nn.silu(g), down_w[e])
            out = jnp.where((ids == e)[..., None], y, out)
        return out + skip
    x = L0_attn_query
    x = x + _L0_attn_ref(_layernorm(x, axis=-1), L0_attn_Wq, L0_attn_Wk, L0_attn_Wv, L0_attn_Wp, L0_attn_bp)
    x = x + _L0_ffn_ref(_layernorm(x, axis=-1), L0_ffn_scale, L0_ffn_centroids, L0_ffn_up_w, L0_ffn_down_w)
    return x

_drawn_inputs = setup_inputs


def setup_inputs(seed=0):
    import zlib

    import numpy as np

    out = dict(_drawn_inputs(seed))
    spreads = {'L0_attn_bp': (0.0, 0.1), 'L0_ffn_scale': (1.0, 0.2)}
    factors = {}
    for name, (base, spread) in spreads.items():
        noise = np.random.default_rng([zlib.crc32(name.encode()), seed]).standard_normal(out[name].shape)
        drawn = base * np.exp(spread * noise) if base else spread * noise
        out[name] = jnp.asarray(drawn.astype(out[name].dtype))
    for name, factor in factors.items():
        out[name] = (out[name] * factor).astype(out[name].dtype)
    return out
```

```python
from contextlib import ExitStack

import concourse.bass as bass
from concourse import mybir

F32 = mybir.dt.float32
F32R = mybir.dt.float32r
BF16 = mybir.dt.bfloat16
ALU = mybir.AluOpType
ACT = mybir.ActivationFunctionType
AX = mybir.AxisListType

P = 128


class Shapes:

    def __init__(self, x, wq, up_w):
        self.B, self.N, self.D = x.shape
        self.H, _, self.E = wq.shape
        self.NE, _, self.F2 = up_w.shape
        self.F = self.F2 // 2
        self.PAIRS = self.H // 2
        self.TILES = self.N // P
        assert self.D == P and self.E == 64 and self.N == 512 and self.PAIRS == 8 and self.F == 256



SLOTS = 3
PRE, LOOP = 5, 34
PROJECT_AT = {0: "q", 2: "k"}
ATTEND_AT = {1: 0, 3: 1, 4: 2, 5: 3}
SUMS_AT = 6
VALUES_AT = {1: (0,), 2: (1,), 4: (2, 3), 5: (4,), 6: (5,), 7: (6, 7)}


def work_order():
    head = [("xT", 0, 0)] + [(w, p, 0) for p in (0, 1) for w in "qk"]
    body = []
    for i in range(8):
        for u in range(8):
            if i <= 5 and u in PROJECT_AT:
                body += [(PROJECT_AT[u], i + 2, 0)]
            if i == 0:
                body += [("v", v, 0) for v in VALUES_AT.get(u, ())]
        if i >= 1:
            body += [("den", i - 1, 0)]
        if i == 6:
            body += [("xT", 0, 1)]
    body += [("q", 0, 1), ("k", 0, 1), ("q", 1, 1), ("den", 7, 0), ("k", 1, 1), ("x1T", 0, 0)]
    assert len(head) == PRE and len(body) == LOOP and LOOP % 2 == 0
    return head, body


def attention(nc, t, dram, sh):
    NB, PAIRS, TILES, N = sh.B, sh.PAIRS, sh.TILES, sh.N
    head_uses, body_uses = work_order()
    bank_of = {("head",) + u[:2]: (1 + i) % 2 for i, u in enumerate(head_uses)}
    bank_of |= {("body",) + u[:2]: (1 + PRE + i) % 2 for i, u in enumerate(body_uses)}

    def use(part, kind, index):
        uses = head_uses if part == "head" else body_uses
        return [u[:2] for u in uses].index((kind, index))

    with ExitStack() as ctx:
        def sb(name, shape, dt=F32):
            return ctx.enter_context(nc.sbuf_tensor(name, shape, dt))

        def pb(name):
            return ctx.enter_context(nc.psum_tensor(name, [P, 512], F32))

        def sem(name):
            return ctx.enter_context(nc.semaphore(name))

        x, ident = t["x"], t["ident"]
        w_raw = sb("w_raw", [P, 3, 1024])
        w_hi = {w: sb(f"W{w}_hi", [P, 1024], F32R) for w in "qkv"}
        w_lo = {w: sb(f"W{w}_lo", [P, 1024], F32R) for w in "qkv"}
        wp = sb("wp", [P, PAIRS, P])
        bp = sb("bp", [P, 1])
        ones = sb("ones", [P, 64])
        stats = sb("stats", [P, TILES, 6])
        pause = sb("pause", [P, 1])
        meanvar = sb("meanvar", [P, TILES, 2])
        varps = sb("varps", [P, TILES])
        rstd = sb("rstd", [P, TILES])
        power = sb("power", [P, TILES])
        xn = sb("xn", [P, TILES, P])
        xT_hi = sb("xT_hi", [P, N], F32R)
        xT_lo = sb("xT_lo", [P, N], F32R)
        V = sb("V", [P, TILES, 1024])
        T1q = sb("T1q", [P, SLOTS, 2, N], F32R)
        T1k = sb("T1k", [P, SLOTS, 2, N], F32R)
        T2q = sb("T2q", [P, SLOTS, 2, N], F32R)
        T2k = sb("T2k", [P, SLOTS, 2, N], F32R)
        negmax = sb("negmax", [P, SLOTS, 2, 4], F32R)
        probs = sb("probs", [P, 2, 2, TILES, N])
        half_sums = sb("half_sums", [P, 2, N])
        prob_sums = sb("prob_sums", [P, 2, 2, N])
        out_T = sb("out_T", [P, PAIRS, N])
        den_rows = sb("den_rows", [P, 2, N])
        den = sb("den", [P, 2, 8])
        rden = sb("rden", [P, 2, 8])
        rden_rows = sb("rden_rows", [P, 2, N])
        last_rden = sb("last_rden", [P, N])
        proj_T = sb("proj_T", [P, N])

        st = [pb("st0"), pb("st1")]
        mx = [pb("mx0"), pb("mx1")]
        ob = [pb("ob0"), pb("ob1")]
        work = [pb("work0"), pb("work1")]

        names = """x_in w_in wp_in w_hi_done w_lo_done setup ln_step ln_done rstd_ready xT_done xT_hi_done xT_lo_done
            qk_done hi_done lo_done v_done v_act v_dve mx_done max_done st_done exp_done av_done o_done
            den_done den_copied rden_done sums_step sums_done scaled proj_done proj_copied x1T_done
            x1_done ident_zero T2k_zero last_rden last_scaled""".split()
        s = {n: sem(n) for n in names}
        s_dup_q = [sem(f"dup_q{i}") for i in range(SLOTS)]
        s_dup_k = [sem(f"dup_k{i}") for i in range(SLOTS)]
        s_c = [[sem(f"max_row{i}{j}") for j in range(2)] for i in range(SLOTS)]
        s_n1 = [sem(f"den_out{i}") for i in range(2)]
        s_n2 = [sem(f"rden_out{i}") for i in range(2)]
        s_n3 = [sem(f"rden_in{i}") for i in range(2)]

        CR = {"st_done": 24, "exp_done": 2, "av_done": 2, "o_done": 2, "sums_done": 4, "rden_done": 2,
              "proj_done": 1, "proj_copied": 1, "den_done": 2, "scaled": 2, "x1_done": 1, "den_copied": 1}

        def v_sum(name, n):
            return n + CR[name]

        def in_slot(p):
            return len(range(p % SLOTS, PAIRS, SLOTS)), p // SLOTS

        def dma_of_slot(b, p):
            a, k = in_slot(p)
            return 16 * a * b + 16 * (k + 1)

        def pair_before_in_slot(b, p):
            return 8 * b + (p - SLOTS if p >= SLOTS else {0: -2, 1: -1, 2: -3}[p])

        def of_parity(p):
            return len(range(p % 2, PAIRS - 1, 2))

        def wait_work_free(eng, part, kind, index, b):
            i = use(part, kind, index)
            if part == "head" and i < 2:
                return
            if i >= 2:
                prev = [(head_uses if part == "head" else body_uses)[i - 2]]
            else:
                eng.wait_ge(s["hi_done"], 32 * b + 8)
                eng.wait_ge(s["lo_done"], 32 * b + 8)
                eng.wait_ge(s["x1_done"], v_sum("x1_done", b))
                return
            for k, n, ahead in prev:
                bb = b + ahead
                if k in "qk":
                    g = 16 * bb + 2 * n + (k == "k")
                    eng.wait_ge(s["hi_done"], 2 * g + 2)
                    eng.wait_ge(s["lo_done"], 2 * g + 2)
                elif k == "xT":
                    eng.wait_ge(s["xT_lo_done"], bb + 1)
                elif k == "v":
                    eng.wait_ge(s["v_act" if n % 2 == 0 else "v_dve"], 4 * bb + n // 2 + 1)
                elif k == "den" and n == PAIRS - 1:
                    eng.wait_ge(s["last_rden"], bb + 1)
                elif k == "den":
                    eng.wait_ge(s["den_copied"], v_sum("den_copied", 7 * bb + n + 1))
                else:
                    eng.wait_ge(s["x1_done"], v_sum("x1_done", bb + 1))

        SETUP = 5

        block = ctx.enter_context(nc.Block())

        @block.sync
        def _(sp):
            rows = dram["x"].rearrange("b (t p) d -> p (b t) d", p=P)
            for b in range(NB):
                tiles = slice(TILES * b, TILES * b + TILES)
                sp.dma_start(x[:, tiles, :], rows[:, tiles, :]).then_inc(s["x_in"], 16)

            def dup(w, p, bb):
                g = 16 * bb + 2 * p + (w == "k")
                sp.wait_ge(s["hi_done"], 2 * g + 2)
                if w == "q":
                    sp.dma_start(T2q[0:64, p % SLOTS].bitcast(F32), T1q[0:64, p % SLOTS].bitcast(F32)).then_inc(s_dup_q[p % SLOTS], 16)
                else:
                    sp.dma_start(T1k[64:P, p % SLOTS].bitcast(F32), T1k[0:64, p % SLOTS].bitcast(F32)).then_inc(s_dup_k[p % SLOTS], 16)

            def max_row(p, hh, bb):
                sp.wait_ge(s["max_done"], 64 * bb + 8 * p + 4 * hh + 4)
                sp.dma_start(T2q[64:65, p % SLOTS, hh, :].bitcast(F32).rearrange("o (p j) -> o p j", j=4),
                             negmax[:, p % SLOTS, hh, :].bitcast(F32)).then_inc(s_c[p % SLOTS][hh], 16)

            def sums_out(p, b):
                sp.wait_ge(s["den_copied"], v_sum("den_copied", 7 * b + p + 1))
                for hh in range(2):
                    sp.dma_start(den[64 * hh:64 * hh + 64, p % 2, :],
                                 den_rows[64 * hh:64 * hh + 1, p % 2, :].rearrange("o (q j) -> o q j", j=8)
                                 ).then_inc(s_n1[p % 2], 16)

            def rden_out(p, b):
                sp.wait_ge(s["rden_done"], v_sum("rden_done", 7 * b + p + 1))
                sp.dma_start(dram["rden"][p % 2].rearrange("(q j) -> q j", j=8), rden[:, p % 2, :]
                             ).then_inc(s_n2[p % 2], 16)

            def rden_in(p, b):
                sp.wait_ge(s_n2[p % 2], 16 * of_parity(p) * b + 16 * (p // 2) + 16)
                for hh in range(2):
                    row = dram["rden"][p % 2:p % 2 + 1, 512 * hh:512 * hh + 512]
                    sp.dma_start(rden_rows[64 * hh:64 * hh + 64, p % 2, :], row.to_broadcast([64, 512])
                                 ).then_inc(s_n3[p % 2], 16)

            for p in (0, 1):
                dup("q", p, 0)
                dup("k", p, 0)
            max_row(0, 0, 0)
            max_row(0, 1, 0)
            with sp.Fori(0, NB) as b:
                for i in range(8):
                    if i >= 2:
                        rden_out(i - 2, b)
                    if i < 7:
                        max_row(i + 1, 0, b)
                    if i <= 5:
                        dup("q", i + 2, b)
                        dup("k", i + 2, b)
                    if i >= 2:
                        rden_in(i - 2, b)
                    if i < 7:
                        max_row(i + 1, 1, b)
                    if i >= 1:
                        sums_out(i - 1, b)
                dup("q", 0, b + 1)
                rden_out(6, b)
                dup("k", 0, b + 1)
                rden_in(6, b)
                dup("q", 1, b + 1)
                dup("k", 1, b + 1)
                max_row(0, 0, b + 1)
                max_row(0, 1, b + 1)

        @block.tensor
        def _(pe):
            pe.wait_ge(s["setup"], SETUP)
            pe.wait_ge(s["w_lo_done"], 3)
            for n in ("st_done", "av_done", "den_done", "proj_done"):
                pe.sem_inc(s[n], CR[n])

            def bank(part, kind, index):
                return work[bank_of[(part, kind, index)]]

            def transpose_x(part, b, bb):
                wait_work_free(pe, part, "xT", 0, b)
                pe.wait_ge(s["ln_done"], TILES * bb + TILES)
                out = bank(part, "xT", 0)
                for tile in range(TILES):
                    mm = pe.transpose(out[:, tile * P:(tile + 1) * P], xn[:, tile, :], ident[:, :])
                mm.then_inc(s["xT_done"], 1)

            def project(part, w, p, b, bb):
                pe.wait_ge(s["xT_hi_done"], bb + 1)
                pe.wait_ge(s["xT_lo_done"], bb + 1)
                wait_work_free(pe, part, w, p, b)
                out, cols = bank(part, w, p), slice(p * P, (p + 1) * P)
                pe.matmul(out[:, :], w_hi[w][:, cols], xT_hi[:, :], start=True, stop=False)
                pe.matmul(out[:, :], w_hi[w][:, cols], xT_lo[:, :], start=False, stop=False)
                pe.matmul(out[:, :], w_lo[w][:, cols], xT_hi[:, :], start=False, stop=True).then_inc(s["qk_done"], 1)

            def values(v, b):
                wait_work_free(pe, "body", "v", v, b)
                out, rows, cols = bank("body", "v", v), slice(v // 2 * P, v // 2 * P + P), slice(v % 2 * 512, v % 2 * 512 + 512)
                pe.matmul(out[:, :], xT_hi[:, rows], w_hi["v"][:, cols], start=True, stop=False)
                pe.matmul(out[:, :], xT_hi[:, rows], w_lo["v"][:, cols], start=False, stop=False)
                pe.matmul(out[:, :], xT_lo[:, rows], w_hi["v"][:, cols], start=False, stop=True).then_inc(s["v_done"], 1)

            def max_scores(p, j, bb, first=False):
                slot, hh = p % SLOTS, j // 4
                if j == 0:
                    g = 16 * bb + 2 * p + 1
                    pe.wait_ge(s["hi_done"], 2 * g + 2)
                    pe.wait_ge(s["lo_done"], 2 * g + 2)
                    pe.wait_ge(s_dup_k[slot], dma_of_slot(bb, p))
                if not (first and j < 2):
                    pe.wait_ge(s["max_done"], 64 * bb + 8 * p + j - 1)
                pe.matmul(mx[j % 2][:, :], T1q[:, slot, hh, j % 4:512:4], T1k[:, slot, hh, :],
                          start=True, stop=True).then_inc(s["mx_done"], 1)

            def scores(p, u, b):
                slot, hh, cols = p % SLOTS, u // 4, slice(u % 4 * P, u % 4 * P + P)
                pe.wait_ge(s["exp_done"], v_sum("exp_done", 64 * b + 8 * p + u - 1))
                pe.matmul(st[u % 2][:, :], T1k[:, slot, hh, cols], T1q[:, slot, hh, :], start=True, stop=False)
                if u == 0:
                    pe.wait_ge(s_dup_q[slot], dma_of_slot(b, p))
                if u % 4 == 0:
                    pe.wait_ge(s_c[slot][hh], dma_of_slot(b, p))
                pe.matmul(st[u % 2][:, :], T2k[:, slot, hh, cols], T2q[:, slot, hh, :],
                          start=False, stop=True).then_inc(s["st_done"], 1)

            def attend(p, blk, b):
                if blk == 0:
                    pe.wait_ge(s["o_done"], v_sum("o_done", 8 * b + p - 1))
                    if p == 0:
                        pe.wait_ge(s["proj_copied"], v_sum("proj_copied", b))
                        pe.wait_ge(s["v_act"], 4 * b + 4)
                        pe.wait_ge(s["v_dve"], 4 * b + 4)
                pe.wait_ge(s["exp_done"], v_sum("exp_done", 64 * b + 8 * p + 4 + blk + 1))
                for hh in range(2):
                    h = 2 * p + hh
                    mm = pe.matmul(ob[p % 2][64 * hh:64 * hh + 64, :], V[:, blk, 64 * h:64 * h + 64],
                                   probs[:, p % 2, hh, blk, :], start=(blk == 0), stop=(blk == TILES - 1))
                if blk == TILES - 1:
                    mm.then_inc(s["av_done"], 1)

            def denominators(p, b):
                pe.wait_ge(s["sums_done"], v_sum("sums_done", 16 * b + 2 * p + 2))
                wait_work_free(pe, "body", "den", p, b)
                for hh in range(2):
                    mm = pe.matmul(bank("body", "den", p)[64 * hh:64 * hh + 64, :], ones[:, :],
                                   prob_sums[:, p % 2, hh, :], start=True, stop=True)
                mm.then_inc(s["den_done"], 1)

            def out_project(p, b):
                if p == 0:
                    pe.wait_ge(s["o_done"], v_sum("o_done", 8 * b + 7))
                if p == PAIRS - 1:
                    pe.wait_ge(s["last_scaled"], b + 1)
                else:
                    pe.wait_ge(s["scaled"], v_sum("scaled", 7 * b + p + 1))
                mm = pe.matmul(ob[0][:, :], wp[:, p, :], out_T[:, p, :], start=(p == 0), stop=(p == PAIRS - 1))
                if p == PAIRS - 1:
                    mm.then_inc(s["proj_done"], 1)

            def transpose_out(b):
                pe.wait_ge(s["proj_copied"], v_sum("proj_copied", b + 1))
                wait_work_free(pe, "body", "x1T", 0, b)
                for tile in range(TILES):
                    mm = pe.transpose(bank("body", "x1T", 0)[:, tile * P:(tile + 1) * P],
                                      proj_T[:, tile * P:(tile + 1) * P], ident[:, :])
                mm.then_inc(s["x1T_done"], 1)

            transpose_x("head", 0, 0)
            for p in (0, 1):
                for w in "qk":
                    project("head", w, p, 0, 0)
            for j in range(8):
                max_scores(0, j, 0, first=True)

            with pe.Fori(0, NB) as b:
                for i in range(8):
                    for u in range(8):
                        scores(i, u, b)
                        if i < 7:
                            max_scores(i + 1, u, b)
                        if i <= 5 and u in PROJECT_AT:
                            project("body", PROJECT_AT[u], i + 2, b, b)
                        if i == 0:
                            for v in VALUES_AT.get(u, ()):
                                values(v, b)
                        if i >= 1 and u in ATTEND_AT:
                            attend(i - 1, ATTEND_AT[u], b)
                        if i >= 1 and u == SUMS_AT:
                            denominators(i - 1, b)
                        if i == 6 and u == 7:
                            transpose_x("body", b, b + 1)
                project("body", "q", 0, b, b + 1)
                attend(7, 0, b)
                project("body", "k", 0, b, b + 1)
                attend(7, 1, b)
                project("body", "q", 1, b, b + 1)
                attend(7, 2, b)
                attend(7, 3, b)
                denominators(7, b)
                project("body", "k", 1, b, b + 1)
                for j in range(6):
                    max_scores(0, j, b + 1)
                    out_project(j, b)
                out_project(6, b)
                out_project(7, b)
                max_scores(0, 6, b + 1)
                max_scores(0, 7, b + 1)
                transpose_out(b)

        @block.scalar
        def _(act):
            for n, w in enumerate("qkv"):
                act.dma_start(w_raw[:, n, :].rearrange("d (h e) -> d h e", h=sh.H),
                              dram["W" + w].rearrange("h d e -> d h e")).then_inc(s["w_in"], 16)
            for hh in range(2):
                act.dma_start(wp[64 * hh:64 * hh + 64, :, :],
                              dram["Wp"].rearrange("(e p hh) o -> hh e p o", p=PAIRS, hh=2)[hh]
                              ).then_inc(s["wp_in"], 16)
            act.dma_start(bp[:, :], dram["bp"].rearrange("(o a) -> o a", a=1)).then_inc(s["wp_in"], 16)
            act.sem_inc(s["exp_done"], CR["exp_done"])
            act.sem_inc(s["o_done"], CR["o_done"])
            act.sem_inc(s["proj_copied"], CR["proj_copied"])
            act.sem_inc(s["den_copied"], CR["den_copied"])
            act.wait_ge(s["w_in"], 48)
            for n, w in enumerate("qkv"):
                nc.scalar.activation(w_hi[w][:, :], w_raw[:, n, :], ACT.Copy).then_inc(s["w_hi_done"], 1)
            act.wait_ge(s["wp_in"], 48)

            def bank(part, kind, index):
                return work[bank_of[(part, kind, index)]]

            def x_hi(part, bb):
                if part == "body":
                    act.wait_ge(s["qk_done"], 16 * bb)
                act.wait_ge(s["xT_done"], bb + 1)
                nc.scalar.activation(xT_hi[:, :], bank(part, "xT", 0)[:, :], ACT.Copy).then_inc(s["xT_hi_done"], 1)

            def hi(part, w, p, bb):
                if part == "body":
                    prev = pair_before_in_slot(bb, p)
                    act.wait_ge(s["st_done"], v_sum("st_done", 8 * prev + 8))
                act.wait_ge(s["qk_done"], 16 * bb + 2 * p + (w == "k") + 1)
                dst = T1q if w == "q" else T1k
                for hh in range(2):
                    nc.scalar.activation(dst[0:64, p % SLOTS, hh, :],
                                         bank(part, w, p)[64 * hh:64 * hh + 64, :], ACT.Copy
                                         ).then_inc(s["hi_done"], 1)

            def value_copy(v, b):
                act.wait_ge(s["av_done"], v_sum("av_done", 8 * b))
                act.wait_ge(s["v_done"], 8 * b + v + 1)
                nc.scalar.activation(V[:, v // 2, v % 2 * 512:v % 2 * 512 + 512], bank("body", "v", v)[:, :],
                                     ACT.Copy).then_inc(s["v_act"], 1)

            def exponentials(p, u, b):
                hh, blk = u // 4, u % 4
                if u == 0:
                    act.wait_ge(s["av_done"], v_sum("av_done", 8 * b + p - 1))
                    act.wait_ge(s["sums_done"], v_sum("sums_done", 16 * b + 2 * p - 2))
                act.wait_ge(s["st_done"], v_sum("st_done", 64 * b + 8 * p + u + 1))
                nc.scalar.activation(probs[:, p % 2, hh, blk, :], st[u % 2][:, :], ACT.Exp,
                                     scale=0.125).then_inc(s["exp_done"], 1)

            def out_copy(p, b):
                if p == 0:
                    act.wait_ge(s["proj_done"], v_sum("proj_done", b))
                act.wait_ge(s["av_done"], v_sum("av_done", 8 * b + p + 1))
                nc.scalar.activation(out_T[:, p, :], ob[p % 2][:, :], ACT.Copy).then_inc(s["o_done"], 1)

            def den_copy(p, b):
                act.wait_ge(s["rden_done"], v_sum("rden_done", 7 * b + max(p - 1, 0)))
                act.wait_ge(s["den_done"], v_sum("den_done", 8 * b + p + 1))
                nc.scalar.activation(den_rows[:, p % 2, :], bank("body", "den", p)[:, :], ACT.Copy
                                     ).then_inc(s["den_copied"], 1)

            x_hi("head", 0)
            for p in (0, 1):
                for w in "qk":
                    hi("head", w, p, 0)
            with act.Fori(0, NB) as b:
                for i in range(8):
                    for u in range(8):
                        exponentials(i, u, b)
                        if i <= 5 and u in PROJECT_AT:
                            hi("body", PROJECT_AT[u], i + 2, b)
                        if i == 0:
                            for v in VALUES_AT.get(u, ()):
                                if v % 2 == 0:
                                    value_copy(v, b)
                        if i >= 1 and u == 6:
                            out_copy(i - 1, b)
                            den_copy(i - 1, b)
                        if i == 7 and u == 1:
                            x_hi("body", b + 1)
                for w in "qk":
                    hi("body", w, 0, b + 1)
                hi("body", "q", 1, b + 1)
                out_copy(7, b)
                hi("body", "k", 1, b + 1)
                act.wait_ge(s["proj_done"], v_sum("proj_done", b + 1))
                nc.scalar.activation(proj_T[:, :], ob[0][:, :], ACT.Identity, bias=bp[:, 0:1]
                                     ).then_inc(s["proj_copied"], 1)

        @block.vector
        def _(dve):
            for n in ("rden_done", "x1_done"):
                dve.sem_inc(s[n], CR[n])
            nc.vector.memset(T2k[64:P].bitcast(F32), 0.0).then_inc(s["T2k_zero"], 1)
            nc.vector.memset(T2q[64:P].bitcast(F32), 0.0).then_inc(s["setup"], 1)
            nc.vector.memset(ones[:, :], 1.0).then_inc(s["setup"], 1)
            dve.wait_ge(s["T2k_zero"], 1)
            nc.vector.memset(T2k[64:65].bitcast(F32), 1.0).then_inc(s["setup"], 1)

            def bank(part, kind, index):
                return work[bank_of[(part, kind, index)]]

            def layer_norm(part, bb, at):
                steps = 3 * bb
                xt = x[:, bass.ds(at, TILES), :]
                for tile in range(TILES):
                    last = nc.vector.bn_stats(stats[:, tile, :], x[:, bass.ds(at + tile, 1), :])
                last.then_inc(s["ln_step"], 1)
                dve.wait_ge(s["ln_step"], steps + 1)
                nc.vector.memset(pause[:, :], 0.0)
                for tile in range(TILES):
                    last = nc.vector.bn_aggr(meanvar[:, tile, :], stats[:, tile, :])
                last.then_inc(s["ln_step"], 1)
                dve.wait_ge(s["ln_step"], steps + 2)
                nc.vector.tensor_scalar(varps[:, :], meanvar[:, :, 1], 1e-5, None, ALU.add).then_inc(s["ln_step"], 1)

            def normalise(part, bb, at):
                dve.wait_ge(s["rstd_ready"], bb + 1)
                if part == "body":
                    dve.wait_ge(s["xT_done"], bb)
                for tile in range(TILES):
                    nc.vector.tensor_scalar(xn[:, tile, :], x[:, bass.ds(at + tile, 1), :], meanvar[:, tile, 0:1],
                                            rstd[:, tile:tile + 1], ALU.subtract, ALU.mult
                                            ).then_inc(s["ln_done"], 1)

            def x_lo(part, bb):
                dve.wait_ge(s["xT_hi_done"], bb + 1)
                nc.vector.tensor_tensor(xT_lo[:, :], bank(part, "xT", 0)[:, :], xT_hi[:, :].bitcast(F32),
                                        ALU.subtract).then_inc(s["xT_lo_done"], 1)

            def lo(part, w, p, bb):
                g = 16 * bb + 2 * p + (w == "k")
                for hh in range(2):
                    dve.wait_ge(s["hi_done"], 2 * g + hh + 1)
                    out = T1q[64:P, p % SLOTS, hh, :] if w == "q" else T2k[0:64, p % SLOTS, hh, :]
                    up = (T1q if w == "q" else T1k)[0:64, p % SLOTS, hh, :]
                    nc.vector.tensor_tensor(out, bank(part, w, p)[64 * hh:64 * hh + 64, :], up.bitcast(F32),
                                            ALU.subtract).then_inc(s["lo_done"], 1)

            def negated_max(p, j, bb):
                dve.wait_ge(s["mx_done"], 64 * bb + 8 * p + j + 1)
                nc.vector.tensor_reduce(negmax[:, p % SLOTS, j // 4, j % 4:j % 4 + 1], mx[j % 2][:, :], AX.X, ALU.max,
                                        negate=True).then_inc(s["max_done"], 1)

            def value_copy(v, b):
                dve.wait_ge(s["av_done"], v_sum("av_done", 8 * b))
                dve.wait_ge(s["v_done"], 8 * b + v + 1)
                nc.vector.tensor_copy(V[:, v // 2, v % 2 * 512:v % 2 * 512 + 512], bank("body", "v", v)[:, :]
                                      ).then_inc(s["v_dve"], 1)

            def reciprocals(p, b):
                dve.wait_ge(s_n1[p % 2], 32 * of_parity(p) * b + 32 * (p // 2) + 32)
                dve.wait_ge(s["scaled"], v_sum("scaled", 7 * b + max(p - 1, 0)))
                nc.vector.reciprocal(rden[:, p % 2, :], den[:, p % 2, :]).then_inc(s["rden_done"], 1)

            def last_reciprocals(b):
                dve.wait_ge(s["den_done"], v_sum("den_done", 8 * b + 8))
                nc.vector.reciprocal(last_rden[:, :], bank("body", "den", 7)[:, :]).then_inc(s["last_rden"], 1)

            def last_scale(b):
                dve.wait_ge(s["o_done"], v_sum("o_done", 8 * b + 8))
                dve.wait_ge(s["last_rden"], b + 1)
                nc.vector.tensor_tensor(out_T[:, 7, :], out_T[:, 7, :], last_rden[:, :], ALU.mult
                                        ).then_inc(s["last_scaled"], 1)

            dve.wait_ge(s["x_in"], 16 * NB)
            layer_norm("head", 0, 0)
            dve.wait_ge(s["w_in"], 48)
            for n, w in enumerate("qkv"):
                dve.wait_ge(s["w_hi_done"], n + 1)
                nc.vector.tensor_tensor(w_lo[w][:, :], w_raw[:, n, :], w_hi[w][:, :].bitcast(F32), ALU.subtract
                                        ).then_inc(s["w_lo_done"], 1)
            normalise("head", 0, 0)
            x_lo("head", 0)
            for p in (0, 1):
                for w in "qk":
                    lo("head", w, p, 0)
            for j in range(8):
                negated_max(0, j, 0)
            with dve.Fori(0, NB) as b:
                nxt = TILES * ((b + 1) % NB)
                for i in range(8):
                    order = {u: [("m", u)] for u in range(8)}
                    for u, w in PROJECT_AT.items():
                        order[u] += [("lo", w)]
                    order[1] += [("r", 0)]
                    for u in range(8):
                        for what, n in order.get(u, []):
                            if what == "m" and i < 7:
                                negated_max(i + 1, n, b)
                            if what == "lo" and i <= 5:
                                lo("body", n, i + 2, b)
                            if what == "r" and i >= 2:
                                reciprocals(i - 2, b)
                        if i == 0:
                            for v in VALUES_AT.get(u, ()):
                                if v % 2 == 1:
                                    value_copy(v, b)
                    if i == 3:
                        layer_norm("body", b + 1, nxt)
                    if i == 5:
                        normalise("body", b + 1, nxt)
                    if i == 7:
                        x_lo("body", b + 1)
                for p in (0, 1):
                    for w in "qk":
                        lo("body", w, p, b + 1)
                    if p == 0:
                        reciprocals(6, b)
                for j in range(8):
                    negated_max(0, j, b + 1)
                    if j == 3:
                        last_reciprocals(b)
                        last_scale(b)
                dve.wait_ge(s["x1T_done"], b + 1)
                xb = x[:, bass.ds(TILES * b, TILES), :].rearrange("p t d -> p (t d)")
                nc.vector.tensor_tensor(xb, xb, bank("body", "x1T", 0)[:, :], ALU.add).then_inc(s["x1_done"], 1)

        @block.gpsimd
        def _(pool):
            for n in ("sums_done", "scaled"):
                pool.sem_inc(s[n], CR[n])
            nc.gpsimd.memset(power[:, :], -0.5).then_inc(s["setup"], 1)
            nc.gpsimd.memset(ident[:, :], 0.0).then_inc(s["ident_zero"], 1)
            pool.wait_ge(s["ident_zero"], 1)
            nc.gpsimd.affine_select(out=ident[:, :], in_=ident[:, :], compare_op=ALU.not_equal, fill=1.0, base=0,
                                    pattern=[[-1, P]], channel_multiplier=1).then_inc(s["setup"], 1)

            def inverse_std(bb):
                pool.wait_ge(s["ln_step"], 3 * bb + 3)
                nc.gpsimd.tensor_tensor(rstd[:, :], varps[:, :], power[:, :], ALU.pow).then_inc(s["rstd_ready"], 1)

            def sums(p, hh, b):
                pool.wait_ge(s["exp_done"], v_sum("exp_done", 64 * b + 8 * p + 4 * hh + 4))
                pool.wait_ge(s["sums_done"], v_sum("sums_done", 16 * b + 2 * p + hh))
                pr = probs[:, p % 2, hh]
                nc.gpsimd.tensor_tensor(half_sums[:, :, :], pr[:, 0:2, :], pr[:, 2:4, :], ALU.add
                                        ).then_inc(s["sums_step"], 1)
                pool.wait_ge(s["sums_step"], 16 * b + 2 * p + hh + 1)
                if hh == 0:
                    pool.wait_ge(s["den_done"], v_sum("den_done", 8 * b + p - 1))
                nc.gpsimd.tensor_tensor(prob_sums[:, p % 2, hh, :], half_sums[:, 0, :], half_sums[:, 1, :], ALU.add
                                        ).then_inc(s["sums_done"], 1)

            def scale(p, b):
                pool.wait_ge(s["o_done"], v_sum("o_done", 8 * b + p + 1))
                pool.wait_ge(s_n3[p % 2], 32 * of_parity(p) * b + 32 * (p // 2) + 32)
                nc.gpsimd.tensor_tensor(out_T[:, p, :], out_T[:, p, :], rden_rows[:, p % 2, :], ALU.mult
                                        ).then_inc(s["scaled"], 1)

            pool.wait_ge(s["setup"], SETUP)
            inverse_std(0)
            with pool.Fori(0, NB) as b:
                for i in range(8):
                    sums(i, 0, b)
                    if i >= 2:
                        scale(i - 2, b)
                    if i == 4:
                        inverse_std(b + 1)
                    sums(i, 1, b)
                scale(6, b)




def feed_forward(nc, t, dram, sh):
    NB, NE, TILES, N = sh.B, sh.NE, sh.TILES, sh.N
    CH = sh.F // P

    with ExitStack() as ctx:
        def sb(name, shape, dt=F32):
            return ctx.enter_context(nc.sbuf_tensor(name, shape, dt))

        def pb(name):
            return ctx.enter_context(nc.psum_tensor(name, [P, 512], F32))

        x, ident = t["x"], t["ident"]
        raw = sb("ffn_raw", [P, 2, 2 * CH * P])
        up_hi = sb("up_hi", [P, NE, sh.F2], F32R)
        up_lo = sb("up_lo", [P, NE, sh.F2], F32R)
        down_hi = sb("down_hi", [P, NE, CH, P], F32R)
        down_lo = sb("down_lo", [P, NE, CH, P], F32R)
        down_raw = sb("down_raw", [P, NE, CH, P])
        cen = sb("cen", [NE, P])
        cenT_hi = sb("cenT_hi", [P, NE], F32R)
        cenT_lo = sb("cenT_lo", [P, NE], F32R)
        cen_row = sb("cen_row", [P, NE, P])
        cen_sq = sb("cen_sq", [P, NE])
        scale_row = sb("scale_row", [P, P])
        rank = sb("rank", [P, TILES, NE])
        power = sb("power2", [P, TILES])
        identb = sb("identb", [P, P], BF16)
        stats = sb("stats2", [P, TILES, 6])
        pause = sb("pause2", [P, 1])
        meanvar = sb("meanvar2", [P, TILES, 2])
        varps = sb("varps2", [P, TILES])
        rstd = sb("rstd2", [P, TILES])
        xn = sb("xn2", [P, TILES, P])
        junk = sb("junk", [P, P])
        square = sb("square", [P, TILES])
        meansq = sb("meansq", [P, TILES])
        rrms = sb("rrms", [P, TILES])
        xr = sb("xr", [P, TILES, P])
        xr_sq = sb("xr_sq", [P, TILES])
        norms = sb("norms", [P, TILES, NE])
        dist = sb("dist", [P, TILES, NE])
        least = sb("least", [P, TILES])
        near = sb("near", [P, TILES, NE])
        first = sb("first", [P, TILES])
        chosen = sb("chosen", [P, TILES, NE], BF16)
        xT_hi = sb("x2T_hi", [P, N], F32R)
        xT_lo = sb("x2T_lo", [P, N], F32R)
        mask = sb("mask", [P, 2, N])
        xm_hi = sb("xm_hi", [P, 2, N], F32R)
        xm_lo = sb("xm_lo", [P, 2, N], F32R)
        gate = sb("gate", [P, CH, N])
        act_f = sb("act_f", [P, CH, N])
        act_hi = sb("act_hi", [P, CH, N], F32R)
        act_lo = sb("act_lo", [P, CH, N], F32R)
        yT = sb("yT", [P, N])
        result = sb("result", [P, N])

        hb = [pb(f"h{i}") for i in range(4)]
        yb = pb("y")
        mb = [pb("mask0"), pb("mask1")]
        tb = pb("turn")

        def sem(name):
            return ctx.enter_context(nc.semaphore(name))

        s_raw = [sem(f"f_raw{i}") for i in range(2)]
        names = """ up_hi_done up_lo_done down_in down_split_hi down_split_lo small_in small_setup
            cenT_done cen_split cen_step pool_setup ident_ready
            dve_step rstd_ready xn_ready square_ready rrms_ready xr_ready xr_sq_ready xT_done xT_hi_done xT_lo_done
            dots_done chosen_ready mask_done mask_copied masked h_done gate_done act_done act_hi_done act_lo_done
            down_done y_done y_copied yT_done result_done stored chain_end""".split()
        s = {n: sem("f_" + n) for n in names}
        CR = {"gate_done": 4, "act_done": 4, "down_done": 2, "masked": 4, "mask_copied": 2, "y_copied": 1,
              "result_done": 1, "stored": 16, "act_hi_done": 4}
        block = ctx.enter_context(nc.Block())

        out_rows = dram["out"].rearrange("b (t p) d -> p (b t) d", p=P)

        @block.sync
        def _(sp):
            sp.sem_inc(s["stored"], CR["stored"])
            sp.dma_start(cen[:, :], dram["centroids"]).then_inc(s["small_in"], 16)
            sp.dma_start(cen_row[:, :, :], dram["centroids"].rearrange("(o e) d -> o e d", o=1).to_broadcast([P, NE, P])
                         ).then_inc(s["small_in"], 16)
            sp.dma_start(scale_row[:, :], dram["scale"].rearrange("(o d) -> o d", o=1).to_broadcast([P, P])
                         ).then_inc(s["small_in"], 16)
            for e in range(NE):
                if e >= 2:
                    sp.wait_ge(s["up_lo_done"], e - 1)
                sp.dma_start(raw[:, e % 2, :], dram["up_w"][e]).then_inc(s_raw[e % 2], 16)
                if e == 0:
                    sp.dma_start(down_raw[:, :, :, :], dram["down_w"].rearrange("e (c f) d -> f e c d", c=CH)
                                 ).then_inc(s["down_in"], 16)
            with sp.Fori(0, NB) as b:
                sp.wait_ge(s["result_done"], b + 2)
                sp.dma_start(out_rows[:, bass.ds(TILES * b, TILES), :], result[:, :].rearrange("p (t d) -> p t d", d=P)
                             ).then_inc(s["stored"], 16)
            sp.wait_ge(s["stored"], 16 * NB + CR["stored"])

        @block.tensor
        def _(pe):
            pe.sem_inc(s["down_done"], CR["down_done"])
            pe.wait_ge(s["small_in"], 48)
            pe.transpose(tb[:, 0:NE], cen[:, :], ident[0:NE, 0:NE]).then_inc(s["cenT_done"], 1)
            pe.wait_ge(s["cen_split"], 2)

            def transpose_x(bb):
                pe.wait_ge(s["xr_ready"], TILES * bb + TILES)
                for tile in range(TILES):
                    mm = pe.transpose(tb[:, tile * P:(tile + 1) * P], xr[:, tile, :], ident[:, :])
                mm.then_inc(s["xT_done"], 1)

            def centroid_products(bb):
                pe.wait_ge(s["xT_lo_done"], bb + 1)
                for tile in range(TILES):
                    out, rows = tb[:, NE * tile:NE * tile + NE], slice(tile * P, (tile + 1) * P)
                    pe.matmul(out, xT_hi[:, rows], cenT_hi[:, :], start=True, stop=False)
                    pe.matmul(out, xT_hi[:, rows], cenT_lo[:, :], start=False, stop=False)
                    mm = pe.matmul(out, xT_lo[:, rows], cenT_hi[:, :], start=False, stop=True)
                mm.then_inc(s["dots_done"], 1)

            def expert_mask(e, bb):
                if e == 0:
                    pe.wait_ge(s["chosen_ready"], bb + 1)
                    pe.wait_ge(s["ident_ready"], 1)
                pe.wait_ge(s["mask_copied"], 8 * bb + e - 1 + CR["mask_copied"])
                for tile in range(TILES):
                    mm = pe.matmul(mb[e % 2][:, tile * P:(tile + 1) * P],
                                   chosen[:, tile, e:e + 1].to_broadcast([P, P]), identb[:, :],
                                   start=True, stop=True)
                mm.then_inc(s["mask_done"], 1)

            def up(e, b):
                pe.wait_ge(s["masked"], 2 * (8 * b + e) + 2 + CR["masked"])
                pe.wait_ge(s["up_lo_done"], e + 1)
                for c in range(CH):
                    for what in (1, 0):
                        out = hb[2 * c + 1 - what]
                        cols = slice((CH * what + c) * P, (CH * what + c + 1) * P)
                        n = CH * (8 * b + e) + c - CH + 1
                        last_reader = "gate_done" if what else "act_done"
                        pe.wait_ge(s[last_reader], n + CR[last_reader])
                        pe.matmul(out[:, :], up_hi[:, e, cols], xm_hi[:, e % 2, :], start=True, stop=False)
                        pe.matmul(out[:, :], up_hi[:, e, cols], xm_lo[:, e % 2, :], start=False, stop=False)
                        pe.matmul(out[:, :], up_lo[:, e, cols], xm_hi[:, e % 2, :], start=False, stop=True
                                  ).then_inc(s["h_done"], 1)

            def down(e, b):
                if e == 0:
                    pe.wait_ge(s["y_copied"], b + CR["y_copied"])
                    pe.wait_ge(s["down_split_lo"], 1)
                for c in range(CH):
                    pe.wait_ge(s["act_lo_done"], CH * (8 * b + e) + c + 1)
                    pe.matmul(yb[:, :], down_hi[:, e, c, :], act_hi[:, c, :], start=(e == 0 and c == 0), stop=False)
                    pe.matmul(yb[:, :], down_hi[:, e, c, :], act_lo[:, c, :], start=False, stop=False)
                    mm = pe.matmul(yb[:, :], down_lo[:, e, c, :], act_hi[:, c, :], start=False,
                                   stop=(e == NE - 1 and c == CH - 1))
                    mm.then_inc(s["down_done"], 1)

            def transpose_y(b):
                pe.wait_ge(s["y_copied"], b + 1 + CR["y_copied"])
                for tile in range(TILES):
                    mm = pe.transpose(tb[:, tile * P:(tile + 1) * P], yT[:, tile * P:(tile + 1) * P], ident[:, :])
                mm.then_inc(s["yT_done"], 1)

            transpose_x(0)
            centroid_products(0)
            expert_mask(0, 0)
            expert_mask(1, 0)
            with pe.Fori(0, NB) as b:
                for e in range(NE):
                    up(e, b)
                    if e + 2 < NE:
                        expert_mask(e + 2, b)
                    if e >= 1:
                        down(e - 1, b)
                    if e == NE - 2:
                        pe.wait_ge(s["result_done"], b + 1)
                        transpose_x(b + 1)
                centroid_products(b + 1)
                down(NE - 1, b)
                expert_mask(0, b + 1)
                expert_mask(1, b + 1)
                transpose_y(b)

        @block.scalar
        def _(act):
            for n in ("gate_done", "mask_copied", "y_copied", "act_hi_done"):
                act.sem_inc(s[n], CR[n])

            def squares(src, dst, done, ready, bb):
                act.wait_ge(s[ready], TILES * bb + TILES)
                for tile in range(TILES):
                    nc.scalar.activation(junk[:, :], src[:, tile, :], ACT.Square, accum_out=dst[:, tile:tile + 1]
                                         ).then_inc(s[done], 1)
                    act.wait_ge(s[done], TILES * bb + tile + 1)

            def x_hi(bb, first=False):
                act.wait_ge(s["xT_done"], bb + 1)
                if not first:
                    act.wait_ge(s["masked"], 16 * bb + CR["masked"])
                nc.scalar.activation(xT_hi[:, :], tb[:, :], ACT.Copy).then_inc(s["xT_hi_done"], 1)

            def mask_copy(e, bb):
                act.wait_ge(s["mask_done"], 8 * bb + e + 1)
                act.wait_ge(s["masked"], 2 * (8 * bb + e - 2) + 2 + CR["masked"])
                nc.scalar.activation(mask[:, e % 2, :], mb[e % 2][:, :], ACT.Copy).then_inc(s["mask_copied"], 1)

            def hidden_hi(c, e, b):
                n = CH * (8 * b + e) + c
                act.wait_ge(s["act_done"], n + 1 + CR["act_done"])
                act.wait_ge(s["down_done"], n + 1 - CH + CR["down_done"])
                nc.scalar.activation(act_hi[:, c, :], act_f[:, c, :], ACT.Copy).then_inc(s["act_hi_done"], 1)

            act.wait_ge(s["cenT_done"], 1)
            nc.scalar.activation(cenT_hi[:, :], tb[:, 0:NE], ACT.Copy).then_inc(s["cen_split"], 1)
            squares(xn, square, "square_ready", "xn_ready", 0)
            squares(xr, xr_sq, "xr_sq_ready", "xr_ready", 0)
            x_hi(0, first=True)
            for e in range(NE):
                act.wait_ge(s_raw[e % 2], 16 * (e // 2) + 16)
                nc.scalar.activation(up_hi[:, e, :], raw[:, e % 2, :], ACT.Copy).then_inc(s["up_hi_done"], 1)
                if e == 0:
                    act.wait_ge(s["down_in"], 16)
                    nc.scalar.activation(down_hi[:, :, :, :], down_raw[:, :, :, :], ACT.Copy
                                         ).then_inc(s["down_split_hi"], 1)
                    mask_copy(0, 0)
                    mask_copy(1, 0)
            with act.Fori(0, NB) as b:
                for e in range(NE):
                    for c in range(CH):
                        act.wait_ge(s["act_done"], CH * (8 * b + e) + c - CH + 1 + CR["act_done"])
                        act.wait_ge(s["h_done"], 4 * (8 * b + e) + 2 * c + 1)
                        nc.scalar.activation(gate[:, c, :], hb[2 * c][:, :], ACT.Silu).then_inc(s["gate_done"], 1)
                        if c == 0 and e + 2 < NE:
                            mask_copy(e + 2, b)
                        if c == 1:
                            hidden_hi(0, e, b)
                    hidden_hi(1, e, b)
                    if e == NE - 4:
                        squares(xn, square, "square_ready", "xn_ready", b + 1)
                    if e == NE - 3:
                        squares(xr, xr_sq, "xr_sq_ready", "xr_ready", b + 1)
                    if e == NE - 2:
                        x_hi(b + 1)
                act.wait_ge(s["down_done"], 2 * 8 * (b + 1) + CR["down_done"])
                act.wait_ge(s["result_done"], b + CR["result_done"])
                nc.scalar.activation(yT[:, :], yb[:, :], ACT.Copy).then_inc(s["y_copied"], 1)
                mask_copy(0, b + 1)
                mask_copy(1, b + 1)

        @block.vector
        def _(dve):
            for n in ("act_done", "result_done"):
                dve.sem_inc(s[n], CR[n])
            STEPS = 10

            def step(ins, bb, n):
                ins.then_inc(s["dve_step"], 1)
                dve.wait_ge(s["dve_step"], STEPS * bb + n)

            def norm_stats(bb, at):
                for tile in range(TILES):
                    last = nc.vector.bn_stats(stats[:, tile, :], x[:, bass.ds(at + tile, 1), :])
                step(last, bb, 1)
                nc.vector.memset(pause[:, :], 0.0)
                for tile in range(TILES):
                    last = nc.vector.bn_aggr(meanvar[:, tile, :], stats[:, tile, :])
                step(last, bb, 2)
                nc.vector.tensor_scalar(varps[:, :], meanvar[:, :, 1], 1e-5, None, ALU.add).then_inc(s["dve_step"], 1)

            def normalise(bb, at):
                dve.wait_ge(s["rstd_ready"], bb + 1)
                for tile in range(TILES):
                    nc.vector.tensor_scalar(xn[:, tile, :], x[:, bass.ds(at + tile, 1), :], meanvar[:, tile, 0:1],
                                            rstd[:, tile:tile + 1], ALU.subtract, ALU.mult).then_inc(s["xn_ready"], 1)
                dve.wait_ge(s["xn_ready"], TILES * bb + TILES)
                xb = x[:, bass.ds(at, TILES), :]
                nc.vector.tensor_tensor(xb, xb, xn[:, :, :], ALU.add).then_inc(s["dve_step"], 1)

            def mean_square(bb):
                dve.wait_ge(s["square_ready"], TILES * bb + TILES)
                nc.vector.tensor_scalar(meansq[:, :], square[:, :], 1.0 / sh.D, 1e-6, ALU.mult, ALU.add
                                        ).then_inc(s["dve_step"], 1)

            def rms_norm(bb):
                dve.wait_ge(s["rrms_ready"], bb + 1)
                for tile in range(TILES):
                    nc.vector.scalar_tensor_tensor(out=xr[:, tile, :], in0=xn[:, tile, :], scalar=rrms[:, tile:tile + 1],
                                                   in1=scale_row[:, :], op0=ALU.mult, op1=ALU.mult
                                                   ).then_inc(s["xr_ready"], 1)

            def x_lo(bb):
                dve.wait_ge(s["xT_hi_done"], bb + 1)
                nc.vector.tensor_tensor(xT_lo[:, :], tb[:, :], xT_hi[:, :].bitcast(F32), ALU.subtract
                                        ).then_inc(s["xT_lo_done"], 1)

            def route(bb):
                dve.wait_ge(s["xr_sq_ready"], TILES * bb + TILES)
                for tile in range(TILES):
                    last = nc.vector.tensor_scalar(norms[:, tile, :], cen_sq[:, :], xr_sq[:, tile:tile + 1], None, ALU.add)
                step(last, bb, 6)
                dve.wait_ge(s["dots_done"], bb + 1)
                flat = "p t e -> p (t e)"
                step(nc.vector.scalar_tensor_tensor(
                    out=dist[:, :, :].rearrange(flat), in0=tb[:, 0:TILES * NE], scalar=-2.0,
                    in1=norms[:, :, :].rearrange(flat), op0=ALU.mult, op1=ALU.add), bb, 7)
                step(nc.vector.tensor_reduce(least[:, :], dist[:, :, :], AX.X, ALU.min), bb, 8)
                wide = lambda a: a.rearrange("p (t o) -> p t o", o=1).to_broadcast([P, TILES, NE])
                nc.vector.tensor_tensor(near[:, :, :], dist[:, :, :], wide(least[:, :]), ALU.is_equal
                                        ).then_inc(s["dve_step"], 1)
                dve.wait_ge(s["dve_step"], STEPS * bb + 9)
                nc.vector.tensor_tensor(near[:, :, :], near[:, :, :], rank[:, :, :], ALU.mult).then_inc(s["dve_step"], 1)
                dve.wait_ge(s["dve_step"], STEPS * bb + 10)
                nc.vector.tensor_reduce(first[:, :], near[:, :, :], AX.X, ALU.max).then_inc(s["chain_end"], 1)
                dve.wait_ge(s["chain_end"], bb + 1)
                nc.vector.tensor_tensor(chosen[:, :, :], near[:, :, :], wide(first[:, :]), ALU.is_equal
                                        ).then_inc(s["chosen_ready"], 1)

            dve.wait_ge(s["small_in"], 48)
            for e in range(NE):
                nc.vector.memset(rank[:, :, e], float(NE - e))
            last = nc.vector.tensor_tensor(cen_row[:, :, :], cen_row[:, :, :], cen_row[:, :, :], ALU.mult)
            last.then_inc(s["cen_step"], 1)
            dve.wait_ge(s["cen_step"], 1)
            nc.vector.tensor_reduce(cen_sq[:, :], cen_row[:, :, :], AX.X, ALU.add).then_inc(s["cen_step"], 1)
            nc.vector.tensor_copy(identb[:, :], ident[:, :]).then_inc(s["ident_ready"], 1)
            dve.wait_ge(s["cen_step"], 2)
            norm_stats(0, 0)
            dve.wait_ge(s["cen_split"], 1)
            nc.vector.tensor_tensor(cenT_lo[:, :], tb[:, 0:NE], cenT_hi[:, :].bitcast(F32), ALU.subtract
                                    ).then_inc(s["cen_split"], 1)
            normalise(0, 0)
            mean_square(0)
            rms_norm(0)
            x_lo(0)
            for e in range(NE):
                dve.wait_ge(s["up_hi_done"], e + 1)
                nc.vector.tensor_tensor(up_lo[:, e, :], raw[:, e % 2, :], up_hi[:, e, :].bitcast(F32), ALU.subtract
                                        ).then_inc(s["up_lo_done"], 1)
                if e == 0:
                    dve.wait_ge(s["down_split_hi"], 1)
                    nc.vector.tensor_tensor(down_lo[:, :, :, :], down_raw[:, :, :, :], down_hi[:, :, :, :].bitcast(F32),
                                            ALU.subtract).then_inc(s["down_split_lo"], 1)
                    route(0)
            with dve.Fori(0, NB) as b:
                nxt = TILES * ((b + 1) % NB)
                for e in range(NE):
                    for c in range(CH):
                        n = CH * (8 * b + e) + c
                        dve.wait_ge(s["gate_done"], n + 1 + CR["gate_done"])
                        dve.wait_ge(s["h_done"], 4 * (8 * b + e) + 2 * c + 2)
                        dve.wait_ge(s["act_hi_done"], n - CH + 1 + CR["act_hi_done"])
                        nc.vector.tensor_tensor(act_f[:, c, :], hb[2 * c + 1][:, :], gate[:, c, :], ALU.mult
                                                ).then_inc(s["act_done"], 1)
                        dve.wait_ge(s["act_hi_done"], n + 1 + CR["act_hi_done"])
                        nc.vector.tensor_tensor(act_lo[:, c, :], act_f[:, c, :], act_hi[:, c, :].bitcast(F32),
                                                ALU.subtract).then_inc(s["act_lo_done"], 1)
                    if e == 1:
                        norm_stats(b + 1, nxt)
                    if e == 2:
                        normalise(b + 1, nxt)
                    if e == NE - 4:
                        mean_square(b + 1)
                    if e == NE - 3:
                        rms_norm(b + 1)
                    if e == NE - 2:
                        x_lo(b + 1)
                route(b + 1)
                dve.wait_ge(s["yT_done"], b + 1)
                dve.wait_ge(s["stored"], 16 * b + CR["stored"])
                xb = x[:, bass.ds(TILES * b, TILES), :].rearrange("p t d -> p (t d)")
                nc.vector.tensor_tensor(result[:, :], xb, tb[:, :], ALU.add).then_inc(s["result_done"], 1)

        @block.gpsimd
        def _(pool):
            pool.sem_inc(s["masked"], CR["masked"])
            nc.gpsimd.memset(power[:, :], -0.5).then_inc(s["pool_setup"], 1)
            pool.wait_ge(s["pool_setup"], 1)

            def inverse_std(bb):
                pool.wait_ge(s["dve_step"], 10 * bb + 3)
                nc.gpsimd.tensor_tensor(rstd[:, :], varps[:, :], power[:, :], ALU.pow).then_inc(s["rstd_ready"], 1)

            def inverse_rms(bb):
                pool.wait_ge(s["dve_step"], 10 * bb + 5)
                nc.gpsimd.tensor_tensor(rrms[:, :], meansq[:, :], power[:, :], ALU.pow).then_inc(s["rrms_ready"], 1)

            def masked(e, b, start=False):
                if e == 0:
                    pool.wait_ge(s["xT_lo_done"], b + 1)
                pool.wait_ge(s["mask_copied"], 8 * b + e + 1 + CR["mask_copied"])
                if not start:
                    pool.wait_ge(s["h_done"], 4 * (8 * b + e - 2) + 4)
                nc.gpsimd.tensor_tensor(xm_hi[:, e % 2, :], xT_hi[:, :].bitcast(F32), mask[:, e % 2, :], ALU.mult
                                        ).then_inc(s["masked"], 1)
                nc.gpsimd.tensor_tensor(xm_lo[:, e % 2, :], xT_lo[:, :].bitcast(F32), mask[:, e % 2, :], ALU.mult
                                        ).then_inc(s["masked"], 1)

            inverse_std(0)
            inverse_rms(0)
            masked(0, 0, start=True)
            masked(1, 0, start=True)
            with pool.Fori(0, NB) as b:
                for e in range(NE):
                    if e + 2 < NE:
                        masked(e + 2, b)
                    if e == 1:
                        inverse_std(b + 1)
                    if e == NE - 4:
                        inverse_rms(b + 1)
                masked(0, b + 1)
                masked(1, b + 1)




def build(nc, dram):
    sh = Shapes(dram["x"], dram["Wq"], dram["up_w"])
    with ExitStack() as ctx:
        x = ctx.enter_context(nc.sbuf_tensor("x_all", [P, sh.B * sh.TILES, P], F32))
        ident = ctx.enter_context(nc.sbuf_tensor("ident", [P, P], F32))
        attention(nc, {"x": x, "ident": ident}, dram, sh)
        feed_forward(nc, {"x": x, "ident": ident}, dram, sh)


_INS = {
    "x": "L0_attn_query", "Wq": "L0_attn_Wq", "Wk": "L0_attn_Wk", "Wv": "L0_attn_Wv", "Wp": "L0_attn_Wp",
    "bp": "L0_attn_bp", "scale": "L0_ffn_scale", "centroids": "L0_ffn_centroids", "up_w": "L0_ffn_up_w",
    "down_w": "L0_ffn_down_w",
}


def kernel(**inputs):
    import numpy as _np
    import concourse.bacc as _bacc
    from concourse.bass_utils import run_bass_kernel_spmd as _run

    nc = _bacc.Bacc("TRN2", target_bir_lowering=False, num_devices=1)
    arrays, dram = {}, {}
    for name, given in _INS.items():
        a = _np.ascontiguousarray(inputs[given])
        arrays[f"in_{name}"] = a
        dram[name] = nc.dram_tensor(f"in_{name}", a.shape, mybir.dt.from_np(a.dtype), kind="ExternalInput").ap()
    shape = arrays["in_x"].shape
    dram["out"] = nc.dram_tensor("out_x", shape, F32, kind="ExternalOutput").ap()
    dram["rden"] = nc.dram_tensor("rden_rows_dram", [2, 2 * shape[1]], F32, kind="Internal").ap()
    build(nc, dram)
    return _run(nc, [arrays], core_ids=[0]).results[0]["out_x"]
```

```python
from contextlib import ExitStack

import concourse.bass as bass
from concourse import mybir

F32 = mybir.dt.float32
F32R = mybir.dt.float32r
BF16 = mybir.dt.bfloat16
ALU = mybir.AluOpType
ACT = mybir.ActivationFunctionType
AX = mybir.AxisListType

P = 128


class Shapes:

    def __init__(self, x, wq, up_w):
        self.B, self.N, self.D = x.shape
        self.H, _, self.E = wq.shape
        self.NE, _, self.F2 = up_w.shape
        self.F = self.F2 // 2
        self.PAIRS = self.H // 2
        self.TILES = self.N // P
        assert self.D == P and self.E == 64 and self.N == 512 and self.PAIRS == 8 and self.F == 256



SLOTS = 3
PRE, LOOP = 5, 34
PROJECT_AT = {0: "q", 2: "k"}
ATTEND_AT = {1: 0, 3: 1, 4: 2, 5: 3}
SUMS_AT = 6
VALUES_AT = {1: (0,), 2: (1,), 4: (2, 3), 5: (4,), 6: (5,), 7: (6, 7)}


def work_order():
    head = [("xT", 0, 0)] + [(w, p, 0) for p in (0, 1) for w in "qk"]
    body = []
    for i in range(8):
        for u in range(8):
            if i <= 5 and u in PROJECT_AT:
                body += [(PROJECT_AT[u], i + 2, 0)]
            if i == 0:
                body += [("v", v, 0) for v in VALUES_AT.get(u, ())]
        if i >= 1:
            body += [("den", i - 1, 0)]
        if i == 6:
            body += [("xT", 0, 1)]
    body += [("q", 0, 1), ("k", 0, 1), ("q", 1, 1), ("den", 7, 0), ("k", 1, 1), ("x1T", 0, 0)]
    assert len(head) == PRE and len(body) == LOOP and LOOP % 2 == 0
    return head, body


def attention(nc, t, dram, sh):
    NB, PAIRS, TILES, N = sh.B, sh.PAIRS, sh.TILES, sh.N
    head_uses, body_uses = work_order()
    bank_of = {("head",) + u[:2]: (1 + i) % 2 for i, u in enumerate(head_uses)}
    bank_of |= {("body",) + u[:2]: (1 + PRE + i) % 2 for i, u in enumerate(body_uses)}

    def use(part, kind, index):
        uses = head_uses if part == "head" else body_uses
        return [u[:2] for u in uses].index((kind, index))

    with ExitStack() as ctx:
        def sb(name, shape, dt=F32):
            return ctx.enter_context(nc.sbuf_tensor(name, shape, dt))

        def pb(name):
            return ctx.enter_context(nc.psum_tensor(name, [P, 512], F32))

        def sem(name):
            return ctx.enter_context(nc.semaphore(name))

        x, ident = t["x"], t["ident"]
        w_raw = sb("w_raw", [P, 3, 1024])
        w_hi = {w: sb(f"W{w}_hi", [P, 1024], F32R) for w in "qkv"}
        w_lo = {w: sb(f"W{w}_lo", [P, 1024], F32R) for w in "qkv"}
        wp = sb("wp", [P, PAIRS, P])
        bp = sb("bp", [P, 1])
        ones = sb("ones", [P, 64])
        stats = sb("stats", [P, TILES, 6])
        pause = sb("pause", [P, 1])
        meanvar = sb("meanvar", [P, TILES, 2])
        varps = sb("varps", [P, TILES])
        rstd = sb("rstd", [P, TILES])
        power = sb("power", [P, TILES])
        xn = sb("xn", [P, TILES, P])
        xT_hi = sb("xT_hi", [P, N], F32R)
        xT_lo = sb("xT_lo", [P, N], F32R)
        V = sb("V", [P, TILES, 1024])
        T1q = sb("T1q", [P, SLOTS, 2, N], F32R)
        T1k = sb("T1k", [P, SLOTS, 2, N], F32R)
        T2q = sb("T2q", [P, SLOTS, 2, N], F32R)
        T2k = sb("T2k", [P, SLOTS, 2, N], F32R)
        negmax = sb("negmax", [P, SLOTS, 2, 4], F32R)
        probs = sb("probs", [P, 2, 2, TILES, N])
        half_sums = sb("half_sums", [P, 2, N])
        prob_sums = sb("prob_sums", [P, 2, 2, N])
        out_T = sb("out_T", [P, PAIRS, N])
        den_rows = sb("den_rows", [P, 2, N])
        den = sb("den", [P, 2, 8])
        rden = sb("rden", [P, 2, 8])
        rden_rows = sb("rden_rows", [P, 2, N])
        last_rden = sb("last_rden", [P, N])
        proj_T = sb("proj_T", [P, N])

        st = [pb("st0"), pb("st1")]
        mx = [pb("mx0"), pb("mx1")]
        ob = [pb("ob0"), pb("ob1")]
        work = [pb("work0"), pb("work1")]

        names = """x_in w_in wp_in w_hi_done w_lo_done setup ln_step ln_done rstd_ready xT_done xT_hi_done xT_lo_done
            qk_done hi_done lo_done v_done v_act v_dve mx_done max_done st_done exp_done av_done o_done
            den_done den_copied rden_done sums_step sums_done scaled proj_done proj_copied x1T_done
            x1_done ident_zero T2k_zero last_rden last_scaled""".split()
        s = {n: sem(n) for n in names}
        s_dup_q = [sem(f"dup_q{i}") for i in range(SLOTS)]
        s_dup_k = [sem(f"dup_k{i}") for i in range(SLOTS)]
        s_c = [[sem(f"max_row{i}{j}") for j in range(2)] for i in range(SLOTS)]
        s_n1 = [sem(f"den_out{i}") for i in range(2)]
        s_n2 = [sem(f"rden_out{i}") for i in range(2)]
        s_n3 = [sem(f"rden_in{i}") for i in range(2)]

        CR = {"st_done": 24, "exp_done": 2, "av_done": 2, "o_done": 2, "sums_done": 4, "rden_done": 2,
              "proj_done": 1, "proj_copied": 1, "den_done": 2, "scaled": 2, "x1_done": 1, "den_copied": 1}

        def v_sum(name, n):
            return n + CR[name]

        def in_slot(p):
            return len(range(p % SLOTS, PAIRS, SLOTS)), p // SLOTS

        def dma_of_slot(b, p):
            a, k = in_slot(p)
            return 16 * a * b + 16 * (k + 1)

        def pair_before_in_slot(b, p):
            return 8 * b + (p - SLOTS if p >= SLOTS else {0: -2, 1: -1, 2: -3}[p])

        def of_parity(p):
            return len(range(p % 2, PAIRS - 1, 2))

        def wait_work_free(eng, part, kind, index, b):
            i = use(part, kind, index)
            if part == "head" and i < 2:
                return
            if i >= 2:
                prev = [(head_uses if part == "head" else body_uses)[i - 2]]
            else:
                eng.wait_ge(s["hi_done"], 32 * b + 8)
                eng.wait_ge(s["lo_done"], 32 * b + 8)
                eng.wait_ge(s["x1_done"], v_sum("x1_done", b))
                return
            for k, n, ahead in prev:
                bb = b + ahead
                if k in "qk":
                    g = 16 * bb + 2 * n + (k == "k")
                    eng.wait_ge(s["hi_done"], 2 * g + 2)
                    eng.wait_ge(s["lo_done"], 2 * g + 2)
                elif k == "xT":
                    eng.wait_ge(s["xT_lo_done"], bb + 1)
                elif k == "v":
                    eng.wait_ge(s["v_act" if n % 2 == 0 else "v_dve"], 4 * bb + n // 2 + 1)
                elif k == "den" and n == PAIRS - 1:
                    eng.wait_ge(s["last_rden"], bb + 1)
                elif k == "den":
                    eng.wait_ge(s["den_copied"], v_sum("den_copied", 7 * bb + n + 1))
                else:
                    eng.wait_ge(s["x1_done"], v_sum("x1_done", bb + 1))

        SETUP = 5

        block = ctx.enter_context(nc.Block())

        @block.sync
        def _(sp):
            rows = dram["x"].rearrange("b (t p) d -> p (b t) d", p=P)
            for b in range(NB):
                tiles = slice(TILES * b, TILES * b + TILES)
                sp.dma_start(x[:, tiles, :], rows[:, tiles, :]).then_inc(s["x_in"], 16)

            def dup(w, p, bb):
                g = 16 * bb + 2 * p + (w == "k")
                sp.wait_ge(s["hi_done"], 2 * g + 2)
                if w == "q":
                    sp.dma_start(T2q[0:64, p % SLOTS].bitcast(F32), T1q[0:64, p % SLOTS].bitcast(F32)).then_inc(s_dup_q[p % SLOTS], 16)
                else:
                    sp.dma_start(T1k[64:P, p % SLOTS].bitcast(F32), T1k[0:64, p % SLOTS].bitcast(F32)).then_inc(s_dup_k[p % SLOTS], 16)

            def max_row(p, hh, bb):
                sp.wait_ge(s["max_done"], 64 * bb + 8 * p + 4 * hh + 4)
                sp.dma_start(T2q[64:65, p % SLOTS, hh, :].bitcast(F32).rearrange("o (p j) -> o p j", j=4),
                             negmax[:, p % SLOTS, hh, :].bitcast(F32)).then_inc(s_c[p % SLOTS][hh], 16)

            def sums_out(p, b):
                sp.wait_ge(s["den_copied"], v_sum("den_copied", 7 * b + p + 1))
                for hh in range(2):
                    sp.dma_start(den[64 * hh:64 * hh + 64, p % 2, :],
                                 den_rows[64 * hh:64 * hh + 1, p % 2, :].rearrange("o (q j) -> o q j", j=8)
                                 ).then_inc(s_n1[p % 2], 16)

            def rden_out(p, b):
                sp.wait_ge(s["rden_done"], v_sum("rden_done", 7 * b + p + 1))
                sp.dma_start(dram["rden"][p % 2].rearrange("(q j) -> q j", j=8), rden[:, p % 2, :]
                             ).then_inc(s_n2[p % 2], 16)

            def rden_in(p, b):
                sp.wait_ge(s_n2[p % 2], 16 * of_parity(p) * b + 16 * (p // 2) + 16)
                for hh in range(2):
                    row = dram["rden"][p % 2:p % 2 + 1, 512 * hh:512 * hh + 512]
                    sp.dma_start(rden_rows[64 * hh:64 * hh + 64, p % 2, :], row.to_broadcast([64, 512])
                                 ).then_inc(s_n3[p % 2], 16)

            for p in (0, 1):
                dup("q", p, 0)
                dup("k", p, 0)
            max_row(0, 0, 0)
            max_row(0, 1, 0)
            with sp.Fori(0, NB) as b:
                for i in range(8):
                    if i >= 2:
                        rden_out(i - 2, b)
                    if i < 7:
                        max_row(i + 1, 0, b)
                    if i <= 5:
                        dup("q", i + 2, b)
                        dup("k", i + 2, b)
                    if i >= 2:
                        rden_in(i - 2, b)
                    if i < 7:
                        max_row(i + 1, 1, b)
                    if i >= 1:
                        sums_out(i - 1, b)
                dup("q", 0, b + 1)
                rden_out(6, b)
                dup("k", 0, b + 1)
                rden_in(6, b)
                dup("q", 1, b + 1)
                dup("k", 1, b + 1)
                max_row(0, 0, b + 1)
                max_row(0, 1, b + 1)
            for p in (0, 1):
                sp.wait_ge(s_dup_q[p], dma_of_slot(NB, p))
                sp.wait_ge(s_dup_k[p], dma_of_slot(NB, p))
            for hh in range(2):
                sp.wait_ge(s_c[0][hh], dma_of_slot(NB, 0))

        @block.tensor
        def _(pe):
            pe.wait_ge(s["setup"], SETUP)
            pe.wait_ge(s["w_lo_done"], 3)
            for n in ("st_done", "av_done", "den_done", "proj_done"):
                pe.sem_inc(s[n], CR[n])

            def bank(part, kind, index):
                return work[bank_of[(part, kind, index)]]

            def transpose_x(part, b, bb):
                wait_work_free(pe, part, "xT", 0, b)
                pe.wait_ge(s["ln_done"], TILES * bb + TILES)
                out = bank(part, "xT", 0)
                for tile in range(TILES):
                    mm = pe.transpose(out[:, tile * P:(tile + 1) * P], xn[:, tile, :], ident[:, :])
                mm.then_inc(s["xT_done"], 1)

            def project(part, w, p, b, bb):
                pe.wait_ge(s["xT_hi_done"], bb + 1)
                pe.wait_ge(s["xT_lo_done"], bb + 1)
                wait_work_free(pe, part, w, p, b)
                out, cols = bank(part, w, p), slice(p * P, (p + 1) * P)
                pe.matmul(out[:, :], w_hi[w][:, cols], xT_hi[:, :], start=True, stop=False)
                pe.matmul(out[:, :], w_hi[w][:, cols], xT_lo[:, :], start=False, stop=False)
                pe.matmul(out[:, :], w_lo[w][:, cols], xT_hi[:, :], start=False, stop=True).then_inc(s["qk_done"], 1)

            def values(v, b):
                wait_work_free(pe, "body", "v", v, b)
                out, rows, cols = bank("body", "v", v), slice(v // 2 * P, v // 2 * P + P), slice(v % 2 * 512, v % 2 * 512 + 512)
                pe.matmul(out[:, :], xT_hi[:, rows], w_hi["v"][:, cols], start=True, stop=False)
                pe.matmul(out[:, :], xT_hi[:, rows], w_lo["v"][:, cols], start=False, stop=False)
                pe.matmul(out[:, :], xT_lo[:, rows], w_hi["v"][:, cols], start=False, stop=True).then_inc(s["v_done"], 1)

            def max_scores(p, j, bb, first=False):
                slot, hh = p % SLOTS, j // 4
                if j == 0:
                    g = 16 * bb + 2 * p + 1
                    pe.wait_ge(s["hi_done"], 2 * g + 2)
                    pe.wait_ge(s["lo_done"], 2 * g + 2)
                    pe.wait_ge(s_dup_k[slot], dma_of_slot(bb, p))
                if not (first and j < 2):
                    pe.wait_ge(s["max_done"], 64 * bb + 8 * p + j - 1)
                pe.matmul(mx[j % 2][:, :], T1q[:, slot, hh, j % 4:512:4], T1k[:, slot, hh, :],
                          start=True, stop=True).then_inc(s["mx_done"], 1)

            def scores(p, u, b):
                slot, hh, cols = p % SLOTS, u // 4, slice(u % 4 * P, u % 4 * P + P)
                pe.wait_ge(s["exp_done"], v_sum("exp_done", 64 * b + 8 * p + u - 1))
                pe.matmul(st[u % 2][:, :], T1k[:, slot, hh, cols], T1q[:, slot, hh, :], start=True, stop=False)
                if u == 0:
                    pe.wait_ge(s_dup_q[slot], dma_of_slot(b, p))
                if u % 4 == 0:
                    pe.wait_ge(s_c[slot][hh], dma_of_slot(b, p))
                pe.matmul(st[u % 2][:, :], T2k[:, slot, hh, cols], T2q[:, slot, hh, :],
                          start=False, stop=True).then_inc(s["st_done"], 1)

            def attend(p, blk, b):
                if blk == 0:
                    pe.wait_ge(s["o_done"], v_sum("o_done", 8 * b + p - 1))
                    if p == 0:
                        pe.wait_ge(s["proj_copied"], v_sum("proj_copied", b))
                        pe.wait_ge(s["v_act"], 4 * b + 4)
                        pe.wait_ge(s["v_dve"], 4 * b + 4)
                pe.wait_ge(s["exp_done"], v_sum("exp_done", 64 * b + 8 * p + 4 + blk + 1))
                for hh in range(2):
                    h = 2 * p + hh
                    mm = pe.matmul(ob[p % 2][64 * hh:64 * hh + 64, :], V[:, blk, 64 * h:64 * h + 64],
                                   probs[:, p % 2, hh, blk, :], start=(blk == 0), stop=(blk == TILES - 1))
                if blk == TILES - 1:
                    mm.then_inc(s["av_done"], 1)

            def denominators(p, b):
                pe.wait_ge(s["sums_done"], v_sum("sums_done", 16 * b + 2 * p + 2))
                wait_work_free(pe, "body", "den", p, b)
                for hh in range(2):
                    mm = pe.matmul(bank("body", "den", p)[64 * hh:64 * hh + 64, :], ones[:, :],
                                   prob_sums[:, p % 2, hh, :], start=True, stop=True)
                mm.then_inc(s["den_done"], 1)

            def out_project(p, b):
                if p == 0:
                    pe.wait_ge(s["o_done"], v_sum("o_done", 8 * b + 7))
                if p == PAIRS - 1:
                    pe.wait_ge(s["last_scaled"], b + 1)
                else:
                    pe.wait_ge(s["scaled"], v_sum("scaled", 7 * b + p + 1))
                mm = pe.matmul(ob[0][:, :], wp[:, p, :], out_T[:, p, :], start=(p == 0), stop=(p == PAIRS - 1))
                if p == PAIRS - 1:
                    mm.then_inc(s["proj_done"], 1)

            def transpose_out(b):
                pe.wait_ge(s["proj_copied"], v_sum("proj_copied", b + 1))
                wait_work_free(pe, "body", "x1T", 0, b)
                for tile in range(TILES):
                    mm = pe.transpose(bank("body", "x1T", 0)[:, tile * P:(tile + 1) * P],
                                      proj_T[:, tile * P:(tile + 1) * P], ident[:, :])
                mm.then_inc(s["x1T_done"], 1)

            transpose_x("head", 0, 0)
            for p in (0, 1):
                for w in "qk":
                    project("head", w, p, 0, 0)
            for j in range(8):
                max_scores(0, j, 0, first=True)

            with pe.Fori(0, NB) as b:
                for i in range(8):
                    for u in range(8):
                        scores(i, u, b)
                        if i < 7:
                            max_scores(i + 1, u, b)
                        if i <= 5 and u in PROJECT_AT:
                            project("body", PROJECT_AT[u], i + 2, b, b)
                        if i == 0:
                            for v in VALUES_AT.get(u, ()):
                                values(v, b)
                        if i >= 1 and u in ATTEND_AT:
                            attend(i - 1, ATTEND_AT[u], b)
                        if i >= 1 and u == SUMS_AT:
                            denominators(i - 1, b)
                        if i == 6 and u == 7:
                            transpose_x("body", b, b + 1)
                project("body", "q", 0, b, b + 1)
                attend(7, 0, b)
                project("body", "k", 0, b, b + 1)
                attend(7, 1, b)
                project("body", "q", 1, b, b + 1)
                attend(7, 2, b)
                attend(7, 3, b)
                denominators(7, b)
                project("body", "k", 1, b, b + 1)
                for j in range(6):
                    max_scores(0, j, b + 1)
                    out_project(j, b)
                out_project(6, b)
                out_project(7, b)
                max_scores(0, 6, b + 1)
                max_scores(0, 7, b + 1)
                transpose_out(b)

        @block.scalar
        def _(act):
            for n, w in enumerate("qkv"):
                act.dma_start(w_raw[:, n, :].rearrange("d (h e) -> d h e", h=sh.H),
                              dram["W" + w].rearrange("h d e -> d h e")).then_inc(s["w_in"], 16)
            for hh in range(2):
                act.dma_start(wp[64 * hh:64 * hh + 64, :, :],
                              dram["Wp"].rearrange("(e p hh) o -> hh e p o", p=PAIRS, hh=2)[hh]
                              ).then_inc(s["wp_in"], 16)
            act.dma_start(bp[:, :], dram["bp"].rearrange("(o a) -> o a", a=1)).then_inc(s["wp_in"], 16)
            act.sem_inc(s["exp_done"], CR["exp_done"])
            act.sem_inc(s["o_done"], CR["o_done"])
            act.sem_inc(s["proj_copied"], CR["proj_copied"])
            act.sem_inc(s["den_copied"], CR["den_copied"])
            act.wait_ge(s["w_in"], 48)
            for n, w in enumerate("qkv"):
                nc.scalar.activation(w_hi[w][:, :], w_raw[:, n, :], ACT.Copy).then_inc(s["w_hi_done"], 1)
            act.wait_ge(s["wp_in"], 48)

            def bank(part, kind, index):
                return work[bank_of[(part, kind, index)]]

            def x_hi(part, bb):
                if part == "body":
                    act.wait_ge(s["qk_done"], 16 * bb)
                act.wait_ge(s["xT_done"], bb + 1)
                nc.scalar.activation(xT_hi[:, :], bank(part, "xT", 0)[:, :], ACT.Copy).then_inc(s["xT_hi_done"], 1)

            def hi(part, w, p, bb):
                if part == "body":
                    prev = pair_before_in_slot(bb, p)
                    act.wait_ge(s["st_done"], v_sum("st_done", 8 * prev + 8))
                act.wait_ge(s["qk_done"], 16 * bb + 2 * p + (w == "k") + 1)
                dst = T1q if w == "q" else T1k
                for hh in range(2):
                    nc.scalar.activation(dst[0:64, p % SLOTS, hh, :],
                                         bank(part, w, p)[64 * hh:64 * hh + 64, :], ACT.Copy
                                         ).then_inc(s["hi_done"], 1)

            def value_copy(v, b):
                act.wait_ge(s["av_done"], v_sum("av_done", 8 * b))
                act.wait_ge(s["v_done"], 8 * b + v + 1)
                nc.scalar.activation(V[:, v // 2, v % 2 * 512:v % 2 * 512 + 512], bank("body", "v", v)[:, :],
                                     ACT.Copy).then_inc(s["v_act"], 1)

            def exponentials(p, u, b):
                hh, blk = u // 4, u % 4
                if u == 0:
                    act.wait_ge(s["av_done"], v_sum("av_done", 8 * b + p - 1))
                    act.wait_ge(s["sums_done"], v_sum("sums_done", 16 * b + 2 * p - 2))
                act.wait_ge(s["st_done"], v_sum("st_done", 64 * b + 8 * p + u + 1))
                nc.scalar.activation(probs[:, p % 2, hh, blk, :], st[u % 2][:, :], ACT.Exp,
                                     scale=0.125).then_inc(s["exp_done"], 1)

            def out_copy(p, b):
                if p == 0:
                    act.wait_ge(s["proj_done"], v_sum("proj_done", b))
                act.wait_ge(s["av_done"], v_sum("av_done", 8 * b + p + 1))
                nc.scalar.activation(out_T[:, p, :], ob[p % 2][:, :], ACT.Copy).then_inc(s["o_done"], 1)

            def den_copy(p, b):
                act.wait_ge(s["rden_done"], v_sum("rden_done", 7 * b + max(p - 1, 0)))
                act.wait_ge(s["den_done"], v_sum("den_done", 8 * b + p + 1))
                nc.scalar.activation(den_rows[:, p % 2, :], bank("body", "den", p)[:, :], ACT.Copy
                                     ).then_inc(s["den_copied"], 1)

            x_hi("head", 0)
            for p in (0, 1):
                for w in "qk":
                    hi("head", w, p, 0)
            with act.Fori(0, NB) as b:
                for i in range(8):
                    for u in range(8):
                        exponentials(i, u, b)
                        if i <= 5 and u in PROJECT_AT:
                            hi("body", PROJECT_AT[u], i + 2, b)
                        if i == 0:
                            for v in VALUES_AT.get(u, ()):
                                if v % 2 == 0:
                                    value_copy(v, b)
                        if i >= 1 and u == 6:
                            out_copy(i - 1, b)
                            den_copy(i - 1, b)
                        if i == 7 and u == 1:
                            x_hi("body", b + 1)
                for w in "qk":
                    hi("body", w, 0, b + 1)
                hi("body", "q", 1, b + 1)
                out_copy(7, b)
                hi("body", "k", 1, b + 1)
                act.wait_ge(s["proj_done"], v_sum("proj_done", b + 1))
                nc.scalar.activation(proj_T[:, :], ob[0][:, :], ACT.Identity, bias=bp[:, 0:1]
                                     ).then_inc(s["proj_copied"], 1)

        @block.vector
        def _(dve):
            for n in ("rden_done", "x1_done"):
                dve.sem_inc(s[n], CR[n])
            nc.vector.memset(T2k[64:P].bitcast(F32), 0.0).then_inc(s["T2k_zero"], 1)
            nc.vector.memset(T2q[64:P].bitcast(F32), 0.0).then_inc(s["setup"], 1)
            nc.vector.memset(ones[:, :], 1.0).then_inc(s["setup"], 1)
            dve.wait_ge(s["T2k_zero"], 1)
            nc.vector.memset(T2k[64:65].bitcast(F32), 1.0).then_inc(s["setup"], 1)

            def bank(part, kind, index):
                return work[bank_of[(part, kind, index)]]

            def layer_norm(part, bb, at):
                steps = 3 * bb
                xt = x[:, bass.ds(at, TILES), :]
                for tile in range(TILES):
                    last = nc.vector.bn_stats(stats[:, tile, :], x[:, bass.ds(at + tile, 1), :])
                last.then_inc(s["ln_step"], 1)
                dve.wait_ge(s["ln_step"], steps + 1)
                nc.vector.memset(pause[:, :], 0.0)
                for tile in range(TILES):
                    last = nc.vector.bn_aggr(meanvar[:, tile, :], stats[:, tile, :])
                last.then_inc(s["ln_step"], 1)
                dve.wait_ge(s["ln_step"], steps + 2)
                nc.vector.tensor_scalar(varps[:, :], meanvar[:, :, 1], 1e-5, None, ALU.add).then_inc(s["ln_step"], 1)

            def normalise(part, bb, at):
                dve.wait_ge(s["rstd_ready"], bb + 1)
                if part == "body":
                    dve.wait_ge(s["xT_done"], bb)
                for tile in range(TILES):
                    nc.vector.tensor_scalar(xn[:, tile, :], x[:, bass.ds(at + tile, 1), :], meanvar[:, tile, 0:1],
                                            rstd[:, tile:tile + 1], ALU.subtract, ALU.mult
                                            ).then_inc(s["ln_done"], 1)

            def x_lo(part, bb):
                dve.wait_ge(s["xT_hi_done"], bb + 1)
                nc.vector.tensor_tensor(xT_lo[:, :], bank(part, "xT", 0)[:, :], xT_hi[:, :].bitcast(F32),
                                        ALU.subtract).then_inc(s["xT_lo_done"], 1)

            def lo(part, w, p, bb):
                g = 16 * bb + 2 * p + (w == "k")
                for hh in range(2):
                    dve.wait_ge(s["hi_done"], 2 * g + hh + 1)
                    out = T1q[64:P, p % SLOTS, hh, :] if w == "q" else T2k[0:64, p % SLOTS, hh, :]
                    up = (T1q if w == "q" else T1k)[0:64, p % SLOTS, hh, :]
                    nc.vector.tensor_tensor(out, bank(part, w, p)[64 * hh:64 * hh + 64, :], up.bitcast(F32),
                                            ALU.subtract).then_inc(s["lo_done"], 1)

            def negated_max(p, j, bb):
                dve.wait_ge(s["mx_done"], 64 * bb + 8 * p + j + 1)
                nc.vector.tensor_reduce(negmax[:, p % SLOTS, j // 4, j % 4:j % 4 + 1], mx[j % 2][:, :], AX.X, ALU.max,
                                        negate=True).then_inc(s["max_done"], 1)

            def value_copy(v, b):
                dve.wait_ge(s["av_done"], v_sum("av_done", 8 * b))
                dve.wait_ge(s["v_done"], 8 * b + v + 1)
                nc.vector.tensor_copy(V[:, v // 2, v % 2 * 512:v % 2 * 512 + 512], bank("body", "v", v)[:, :]
                                      ).then_inc(s["v_dve"], 1)

            def reciprocals(p, b):
                dve.wait_ge(s_n1[p % 2], 32 * of_parity(p) * b + 32 * (p // 2) + 32)
                dve.wait_ge(s["scaled"], v_sum("scaled", 7 * b + max(p - 1, 0)))
                nc.vector.reciprocal(rden[:, p % 2, :], den[:, p % 2, :]).then_inc(s["rden_done"], 1)

            def last_reciprocals(b):
                dve.wait_ge(s["den_done"], v_sum("den_done", 8 * b + 8))
                nc.vector.reciprocal(last_rden[:, :], bank("body", "den", 7)[:, :]).then_inc(s["last_rden"], 1)

            def last_scale(b):
                dve.wait_ge(s["o_done"], v_sum("o_done", 8 * b + 8))
                dve.wait_ge(s["last_rden"], b + 1)
                nc.vector.tensor_tensor(out_T[:, 7, :], out_T[:, 7, :], last_rden[:, :], ALU.mult
                                        ).then_inc(s["last_scaled"], 1)

            dve.wait_ge(s["x_in"], 16 * NB)
            layer_norm("head", 0, 0)
            dve.wait_ge(s["w_in"], 48)
            for n, w in enumerate("qkv"):
                dve.wait_ge(s["w_hi_done"], n + 1)
                nc.vector.tensor_tensor(w_lo[w][:, :], w_raw[:, n, :], w_hi[w][:, :].bitcast(F32), ALU.subtract
                                        ).then_inc(s["w_lo_done"], 1)
            normalise("head", 0, 0)
            x_lo("head", 0)
            for p in (0, 1):
                for w in "qk":
                    lo("head", w, p, 0)
            for j in range(8):
                negated_max(0, j, 0)
            with dve.Fori(0, NB) as b:
                nxt = TILES * ((b + 1) % NB)
                for i in range(8):
                    order = {u: [("m", u)] for u in range(8)}
                    for u, w in PROJECT_AT.items():
                        order[u] += [("lo", w)]
                    order[1] += [("r", 0)]
                    for u in range(8):
                        for what, n in order.get(u, []):
                            if what == "m" and i < 7:
                                negated_max(i + 1, n, b)
                            if what == "lo" and i <= 5:
                                lo("body", n, i + 2, b)
                            if what == "r" and i >= 2:
                                reciprocals(i - 2, b)
                        if i == 0:
                            for v in VALUES_AT.get(u, ()):
                                if v % 2 == 1:
                                    value_copy(v, b)
                    if i == 3:
                        layer_norm("body", b + 1, nxt)
                    if i == 5:
                        normalise("body", b + 1, nxt)
                    if i == 7:
                        x_lo("body", b + 1)
                for p in (0, 1):
                    for w in "qk":
                        lo("body", w, p, b + 1)
                    if p == 0:
                        reciprocals(6, b)
                for j in range(8):
                    negated_max(0, j, b + 1)
                    if j == 3:
                        last_reciprocals(b)
                        last_scale(b)
                dve.wait_ge(s["x1T_done"], b + 1)
                xb = x[:, bass.ds(TILES * b, TILES), :].rearrange("p t d -> p (t d)")
                nc.vector.tensor_tensor(xb, xb, bank("body", "x1T", 0)[:, :], ALU.add).then_inc(s["x1_done"], 1)

        @block.gpsimd
        def _(pool):
            for n in ("sums_done", "scaled"):
                pool.sem_inc(s[n], CR[n])
            nc.gpsimd.memset(power[:, :], -0.5).then_inc(s["setup"], 1)
            nc.gpsimd.memset(ident[:, :], 0.0).then_inc(s["ident_zero"], 1)
            pool.wait_ge(s["ident_zero"], 1)
            nc.gpsimd.affine_select(out=ident[:, :], in_=ident[:, :], compare_op=ALU.not_equal, fill=1.0, base=0,
                                    pattern=[[-1, P]], channel_multiplier=1).then_inc(s["setup"], 1)

            def inverse_std(bb):
                pool.wait_ge(s["ln_step"], 3 * bb + 3)
                nc.gpsimd.tensor_tensor(rstd[:, :], varps[:, :], power[:, :], ALU.pow).then_inc(s["rstd_ready"], 1)

            def sums(p, hh, b):
                pool.wait_ge(s["exp_done"], v_sum("exp_done", 64 * b + 8 * p + 4 * hh + 4))
                pool.wait_ge(s["sums_done"], v_sum("sums_done", 16 * b + 2 * p + hh))
                pr = probs[:, p % 2, hh]
                nc.gpsimd.tensor_tensor(half_sums[:, :, :], pr[:, 0:2, :], pr[:, 2:4, :], ALU.add
                                        ).then_inc(s["sums_step"], 1)
                pool.wait_ge(s["sums_step"], 16 * b + 2 * p + hh + 1)
                if hh == 0:
                    pool.wait_ge(s["den_done"], v_sum("den_done", 8 * b + p - 1))
                nc.gpsimd.tensor_tensor(prob_sums[:, p % 2, hh, :], half_sums[:, 0, :], half_sums[:, 1, :], ALU.add
                                        ).then_inc(s["sums_done"], 1)

            def scale(p, b):
                pool.wait_ge(s["o_done"], v_sum("o_done", 8 * b + p + 1))
                pool.wait_ge(s_n3[p % 2], 32 * of_parity(p) * b + 32 * (p // 2) + 32)
                nc.gpsimd.tensor_tensor(out_T[:, p, :], out_T[:, p, :], rden_rows[:, p % 2, :], ALU.mult
                                        ).then_inc(s["scaled"], 1)

            pool.wait_ge(s["setup"], SETUP)
            inverse_std(0)
            with pool.Fori(0, NB) as b:
                for i in range(8):
                    sums(i, 0, b)
                    if i >= 2:
                        scale(i - 2, b)
                    if i == 4:
                        inverse_std(b + 1)
                    sums(i, 1, b)
                scale(6, b)



RUN = 4


class Blocks:

    def __init__(self, sh):
        self.TOKEN_TILES = sh.B * sh.TILES
        self.COUNT = -(-(self.TOKEN_TILES + sh.NE - 1) // RUN) * RUN
        self.REGION_BLOCKS = self.TOKEN_TILES + 1
        self.EMPTY = self.COUNT - self.TOKEN_TILES
        self.ROWS = (sh.NE * self.REGION_BLOCKS + self.EMPTY) * P
        self.WIDTH = 2 * sh.D + 1


def feed_forward(nc, t, dram, sh):
    NB, NE, TILES, N, D = sh.B, sh.NE, sh.TILES, sh.N, sh.D
    CH = sh.F // P
    bl = Blocks(sh)
    RUNS = bl.COUNT // RUN
    I32 = mybir.dt.int32

    with ExitStack() as ctx:
        def sb(name, shape, dt=F32):
            return ctx.enter_context(nc.sbuf_tensor(name, shape, dt))

        def pb(name):
            return ctx.enter_context(nc.psum_tensor(name, [P, 512], F32))

        def sem(name):
            return ctx.enter_context(nc.semaphore(name))

        x, ident = t["x"], t["ident"]
        up_raw = sb("up_raw", [P, NE * sh.F2])
        up_hi = sb("up_hi", [P, NE * sh.F2], F32R)
        up_lo = sb("up_lo", [P, NE * sh.F2], F32R)
        down_raw = sb("down_raw", [P, NE * CH * P])
        down_hi = sb("down_hi", [P, NE * CH * P], F32R)
        down_lo = sb("down_lo", [P, NE * CH * P], F32R)
        cen = sb("cen", [NE, P])
        cenT_hi = sb("cenT_hi", [P, NE], F32R)
        cenT_lo = sb("cenT_lo", [P, NE], F32R)
        cen_row = sb("cen_row", [P, NE, P])
        cen_sq = sb("cen_sq", [P, NE])
        scale_row = sb("scale_row", [P, P])
        rank = sb("rank", [P, TILES, NE])
        power = sb("power2", [P, TILES])
        earlier_f = sb("earlier_f", [P, P])
        earlier = sb("earlier", [P, P], BF16)
        ones = sb("ones_bf16", [P, P], BF16)
        token = sb("token", [P, bl.TOKEN_TILES], I32)
        block_no_int = sb("block_no_int", [P, bl.COUNT], I32)
        block_no = sb("block_no", [P, bl.COUNT])
        filling = sb("filling", [P, bl.WIDTH])
        stats = sb("stats2", [P, TILES, 6])
        pause = sb("pause2", [P, 1])
        meanvar = sb("meanvar2", [P, TILES, 2])
        varps = sb("varps2", [P, TILES])
        rstd = sb("rstd2", [P, TILES])
        xn = sb("xn2", [P, TILES, P])
        hold = sb("hold", [P, 1])
        junk = sb("junk", [P, P])
        square = sb("square", [P, TILES])
        meansq = sb("meansq", [P, TILES])
        rrms = sb("rrms", [P, TILES])
        xr = sb("xr", [P, TILES, P])
        xr_sq = sb("xr_sq", [P, TILES])
        xT_hi = sb("x2T_hi", [P, N], F32R)
        xT_lo = sb("x2T_lo", [P, N], F32R)
        norms = sb("norms", [P, TILES, NE])
        dist = sb("dist", [P, TILES, NE])
        least = sb("least", [P, TILES])
        near = sb("near", [P, TILES, NE])
        first = sb("first", [P, TILES])
        chosen = sb("chosen", [P, TILES, NE], BF16)
        place = sb("place", [P, TILES, NE])
        mine = sb("mine", [P, TILES, NE])
        row_f = sb("row_f", [P, TILES])
        next_row = sb("next_row", [P, NE])
        rows = sb("rows", [P, TILES, bl.WIDTH])
        row_of = sb("row_of", [P, TILES], I32)
        next_row_int = sb("next_row_int", [P, NE], I32)
        region = sb("region", [P, NE])
        tokens = sb("tokens", [P, NE])
        over = sb("over", [P, NE, bl.TOKEN_TILES])
        PAD = NE
        ends = [sb(f"ends{i}", [P, PAD + NE]) for i in range(4)]
        skip = sb("skip", [P, NE])
        past = sb("past", [P, bl.COUNT, NE])
        skipped = sb("skipped", [P, bl.COUNT, NE])
        BEHIND = 2
        expert_f = sb("expert_f", [P, bl.COUNT])
        expert = sb("expert", [P, BEHIND + bl.COUNT + RUN - BEHIND])
        weights_at = sb("weights_at", [P, RUNS + 1, 2 * RUN], I32)
        start_f = sb("start_f", [P, bl.COUNT])
        start = sb("start", [P, bl.COUNT], I32)
        xb = sb("xb", [P, RUN, P])
        rest = sb("rest", [P, RUN, P + 1])
        xbT_hi = sb("xbT_hi", [P, 2, P], F32R)
        xbT_lo = sb("xbT_lo", [P, 2, P], F32R)
        gate = sb("gate", [P, 2, sh.F])
        act_f = sb("act_f", [P, 2, sh.F])
        act_hi = sb("act_hi", [P, 2, sh.F], F32R)
        act_lo = sb("act_lo", [P, 2, sh.F], F32R)

        turn = [pb("turn0"), pb("turn1")]
        hidden = [pb("hidden0"), pb("hidden1")]
        actT = [pb("actT0"), pb("actT1")]
        yb = [pb("y0"), pb("y1")]

        names = """small_in up_in down_in up_hi_done down_hi_done weights_split earlier_step power_ready cenT_done cen_split cen_step iota_done const_done rows_x held meansq_ready stats_step route_step place_step
            fill_done empty_out pool_setup ones_done next_done step rstd_ready xn_ready base_ready square_ready
            rrms_ready xr_ready xr_sq_ready xT_done xT_hi_done xT_lo_done dots_done chosen_ready place_done row_ready
            scattered tables_step tables_ready fill_out
            xbT_done xbT_hi_done xbT_lo_done up_done gate_done act_done actT_done act_hi_done act_lo_done down_done
            result_ready""".split()
        s = {n: sem("f_" + n) for n in names}
        s_xb = [sem(f"f_xb{i}") for i in range(RUN)]
        s_rest = [sem(f"f_rest{i}") for i in range(RUN)]
        s_out = [sem(f"f_out{i}") for i in range(RUN)]
        CR = {"row_ready": 1, "xbT_done": RUN, "down_done": 2, "xbT_lo_done": 2, "act_done": 2, "act_lo_done": 2,
              "result_ready": 2, "chosen_ready": 1, "xr_ready": TILES, "held": 1}
        block = ctx.enter_context(nc.Block())
        out_rows = dram["out"].rearrange("b n d -> (b n) d")
        sorted_rows = dram["sorted"]

        @block.sync
        def _(sp):
            sp.dma_start(cen[:, :], dram["centroids"]).then_inc(s["small_in"], 16)
            sp.dma_start(cen_row[:, :, :], dram["centroids"].rearrange("(o e) d -> o e d", o=1).to_broadcast([P, NE, P])
                         ).then_inc(s["small_in"], 16)
            sp.dma_start(scale_row[:, :], dram["scale"].rearrange("(o d) -> o d", o=1).to_broadcast([P, P])
                         ).then_inc(s["small_in"], 16)
            sp.dma_start(up_raw[:, :].rearrange("d (e f) -> d e f", e=NE), dram["up_w"].rearrange("e d f -> d e f")
                         ).then_inc(s["up_in"], 16)
            sp.dma_start(down_raw[:, :].rearrange("f (c d) -> f c d", d=D),
                         dram["down_w"].rearrange("e (c f) d -> f (e c) d", c=CH)).then_inc(s["down_in"], 16)
            sp.wait_ge(s["fill_done"], 2)
            for i in range(bl.EMPTY):
                at = (NE * bl.REGION_BLOCKS + i) * P
                sp.dma_start(sorted_rows[at:at + P, :], filling[:, :]).then_inc(s["empty_out"], 16)
            sp.wait_ge(s["tables_ready"], 5)
            for e in range(NE):
                at = sp.value_load(next_row_int[0:1, e:e + 1], min_val=0, max_val=NE * bl.REGION_BLOCKS * P - P)
                sp.dma_start(sorted_rows[bass.ds(at, P), :], filling[:, :]).then_inc(s["fill_out"], 16)
            sp.wait_ge(s["empty_out"], 16 * bl.EMPTY)
            sp.wait_ge(s["fill_out"], 16 * NE)
            sp.wait_ge(s["scattered"], 16 * bl.TOKEN_TILES)

            def row_of_block(r, u):
                return sp.value_load(start[0:1, bass.ds(RUN * r + u, 1)], min_val=0, max_val=bl.ROWS - P)

            def load_x(r, u, first=False):
                at = row_of_block(r, u)
                if not first:
                    sp.wait_ge(s["xbT_done"], RUN * r + u - RUN + 1 + CR["xbT_done"])
                sp.dma_start(xb[:, u, :], sorted_rows[bass.ds(at, P), 0:P]).then_inc(s_xb[u], 16)

            def load_rest(r, u, first=False):
                at = row_of_block(r, u)
                if not first:
                    sp.wait_ge(s_out[u], 16 * r)
                sp.dma_start(rest[:, u, :], sorted_rows[bass.ds(at, P), P:bl.WIDTH]).then_inc(s_rest[u], 16)

            for u in range(RUN):
                load_x(0, u, first=True)
            for u in range(RUN):
                load_rest(0, u, first=True)
                load_x(1, u)
            with sp.Fori(2, RUNS) as r:
                for u in range(RUN):
                    load_rest(r - 1, u)
                    load_x(r, u)
            for u in range(RUN):
                load_rest(RUNS - 1, u)

        @block.tensor
        def _(pe):
            for n in ("xbT_done", "down_done"):
                pe.sem_inc(s[n], CR[n])
            pe.wait_ge(s["small_in"], 48)
            pe.transpose(turn[0][:, 0:NE], cen[:, :], ident[0:NE, 0:NE]).then_inc(s["cenT_done"], 1)
            pe.wait_ge(s["cen_split"], 2)
            pe.wait_ge(s["const_done"], 1)
            pe.wait_ge(s["ones_done"], 1)

            def transpose_x(bb):
                pe.wait_ge(s["xr_ready"], TILES * bb + TILES + CR["xr_ready"])
                if not isinstance(bb, int):
                    pe.wait_ge(s["xT_lo_done"], bb)
                for tile in range(TILES):
                    mm = pe.transpose(turn[0][:, tile * P:(tile + 1) * P], xr[:, tile, :], ident[:, :])
                mm.then_inc(s["xT_done"], 1)

            def centroid_products(bb):
                pe.wait_ge(s["xT_lo_done"], bb + 1)
                for tile in range(TILES):
                    out, cols = turn[1][:, NE * tile:NE * tile + NE], slice(tile * P, (tile + 1) * P)
                    pe.matmul(out, xT_hi[:, cols], cenT_hi[:, :], start=True, stop=False)
                    pe.matmul(out, xT_hi[:, cols], cenT_lo[:, :], start=False, stop=False)
                    mm = pe.matmul(out, xT_lo[:, cols], cenT_hi[:, :], start=False, stop=True)
                mm.then_inc(s["dots_done"], 1)

            def places(bb):
                pe.wait_ge(s["chosen_ready"], bb + 1 + CR["chosen_ready"])
                flat = chosen[:, :, :].rearrange("p t e -> p (t e)")
                pe.matmul(hidden[0][:, 0:TILES * NE], earlier[:, :], flat, start=True, stop=False)
                for tile in range(TILES - 1):
                    left = TILES - 1 - tile
                    pe.matmul(hidden[0][:, (tile + 1) * NE:TILES * NE], ones[:, :],
                              chosen[:, tile:tile + 1, :].to_broadcast([P, left, NE]), start=False,
                              stop=(left == 1))
                for tile in range(TILES):
                    mm = pe.matmul(hidden[1][:, 0:NE], ones[:, :], chosen[:, tile, :],
                                   start=(tile == 0), stop=(tile == TILES - 1))
                mm.then_inc(s["place_done"], 1)

            transpose_x(0)
            centroid_products(0)
            with pe.Fori(0, NB) as b:
                places(b)
                transpose_x(b + 1)
                centroid_products(b + 1)

            pe.wait_ge(s["weights_split"], 2 * NE)
            pe.wait_ge(s["tables_ready"], 5)

            def transpose_block(r, u):
                q, u = u // RUN, u % RUN
                j = RUN * (r + q) + u
                pe.wait_ge(s_xb[u], 16 * (r + q) + 16)
                pe.wait_ge(s["xbT_lo_done"], j - 1 + CR["xbT_lo_done"])
                pe.transpose(turn[u % 2][:, 0:P], xb[:, u, :], ident[:, :]).then_inc(s["xbT_done"], 1)

            def up(r, u):
                j = RUN * r + u
                pe.wait_ge(s["xbT_lo_done"], j + 1 + CR["xbT_lo_done"])
                pe.wait_ge(s["act_done"], j - 1 + CR["act_done"])
                w = bass.ds(place(RUN + u), sh.F2)
                pe.matmul(hidden[u % 2][:, :], xbT_hi[:, u % 2, :], up_hi[:, w], start=True, stop=False)
                pe.matmul(hidden[u % 2][:, :], xbT_hi[:, u % 2, :], up_lo[:, w], start=False, stop=False)
                pe.matmul(hidden[u % 2][:, :], xbT_lo[:, u % 2, :], up_hi[:, w], start=False, stop=True
                          ).then_inc(s["up_done"], 1)

            def transpose_hidden(r, u):
                j = RUN * r + u
                pe.wait_ge(s["act_done"], j + 1 + CR["act_done"])
                pe.wait_ge(s["act_lo_done"], j - 1 + CR["act_lo_done"])
                for c in range(CH):
                    mm = pe.transpose(actT[u % 2][:, c * P:(c + 1) * P], act_f[:, u % 2, c * P:(c + 1) * P], ident[:, :])
                mm.then_inc(s["actT_done"], 1)

            def down(r, u):
                j = RUN * r + u - BEHIND
                first = place(u)
                pe.wait_ge(s["act_lo_done"], j + 1 + CR["act_lo_done"])
                pe.wait_ge(s["result_ready"], j - 1 + CR["result_ready"])
                for c in range(CH):
                    rows_c, w = slice(c * P, (c + 1) * P), bass.ds(first + c * P, P)
                    pe.matmul(yb[u % 2][:, 0:P], act_hi[:, u % 2, rows_c], down_hi[:, w], start=(c == 0), stop=False)
                    pe.matmul(yb[u % 2][:, 0:P], act_hi[:, u % 2, rows_c], down_lo[:, w], start=False, stop=False)
                    mm = pe.matmul(yb[u % 2][:, 0:P], act_lo[:, u % 2, rows_c], down_hi[:, w], start=False,
                                   stop=(c == CH - 1))
                mm.then_inc(s["down_done"], 1)

            at = [pe.alloc_register(f"weights_at{i}") for i in range(2 * RUN)]

            def load_places(r):
                pe.load(at, weights_at[0:1, bass.ds(r, 1), :].rearrange("p o n -> p (o n)"))

            def place(i):
                most = (NE - 1) * (CH * P if i < RUN else sh.F2)
                return pe.snap(at[i], min_val=0, max_val=most)

            def run(r, first=False, last=False):
                load_places(r)
                for u in range(RUN):
                    up(r, u)
                    if not (first and u < BEHIND):
                        down(r, u)
                    if not (first and u < 1):
                        transpose_hidden(r, u - 1)
                    if not (last and u >= RUN - 2):
                        transpose_block(r, u + 2)

            transpose_block(0, 0)
            transpose_block(0, 1)
            run(0, first=True)
            with pe.Fori(1, RUNS - 1) as r:
                run(r)
            run(RUNS - 1, last=True)
            load_places(RUNS)
            down(RUNS, 0)
            transpose_hidden(RUNS - 1, RUN - 1)
            down(RUNS, 1)

        @block.scalar
        def _(act):
            act.wait_ge(s["cenT_done"], 1)
            nc.scalar.activation(cenT_hi[:, :], turn[0][:, 0:NE], ACT.Copy).then_inc(s["cen_split"], 1)

            def squares(src, dst, done, ready, bb, credit=0):
                act.wait_ge(s[ready], TILES * bb + TILES + credit)
                for tile in range(TILES):
                    nc.scalar.activation(junk[:, :], src[:, tile, :], ACT.Square, accum_out=dst[:, tile:tile + 1]
                                         ).then_inc(s[done], 1)
                    act.wait_ge(s[done], TILES * bb + tile + 1)

            def x_hi(bb):
                act.wait_ge(s["xT_done"], bb + 1)
                nc.scalar.activation(xT_hi[:, :], turn[0][:, :], ACT.Copy).then_inc(s["xT_hi_done"], 1)

            def rows_x(bb):
                act.wait_ge(s["base_ready"], 2 * bb + 1)
                nc.scalar.activation(rows[:, :, 0:D], xr[:, :, :], ACT.Copy).then_inc(s["rows_x"], 1)

            squares(xn, square, "square_ready", "xn_ready", 0)
            x_hi(0)
            squares(xr, xr_sq, "xr_sq_ready", "xr_ready", 0, CR["xr_ready"])
            rows_x(0)
            act.wait_ge(s["up_in"], 16)
            act.wait_ge(s["down_in"], 16)
            with act.Fori(0, NB) as b:
                w = bass.ds(b * sh.F2, sh.F2)
                nc.scalar.activation(up_hi[:, w], up_raw[:, w], ACT.Copy).then_inc(s["up_hi_done"], 1)
                squares(xn, square, "square_ready", "xn_ready", b + 1)
                w = bass.ds(b * (CH * P), CH * P)
                nc.scalar.activation(down_hi[:, w], down_raw[:, w], ACT.Copy).then_inc(s["down_hi_done"], 1)
                x_hi(b + 1)
                squares(xr, xr_sq, "xr_sq_ready", "xr_ready", b + 1, CR["xr_ready"])
                rows_x(b + 1)

            act.sem_inc(s["act_hi_done"], 1)

            def xb_hi(r, u):
                q, u = u // RUN, u % RUN
                act.wait_ge(s["xbT_done"], RUN * (r + q) + u + 1 + CR["xbT_done"])
                nc.scalar.activation(xbT_hi[:, u % 2, :], turn[u % 2][:, 0:P], ACT.Copy).then_inc(s["xbT_hi_done"], 1)

            def gates(r, u):
                j = RUN * r + u
                act.wait_ge(s["act_done"], j - 1 + CR["act_done"])
                act.wait_ge(s["up_done"], j + 1)
                nc.scalar.activation(gate[:, u % 2, :], hidden[u % 2][:, sh.F:sh.F2], ACT.Silu).then_inc(s["gate_done"], 1)

            def hidden_hi(r, u):
                act.wait_ge(s["actT_done"], RUN * r + u + 1)
                nc.scalar.activation(act_hi[:, u % 2, :], actT[u % 2][:, 0:sh.F], ACT.Copy).then_inc(s["act_hi_done"], 1)

            def run(r, first=False, last=False):
                for u in range(RUN):
                    gates(r, u)
                    if not (first and u < 1):
                        hidden_hi(r, u - 1)
                    if not (last and u >= RUN - 2):
                        xb_hi(r, u + 2)

            xb_hi(0, 0)
            xb_hi(0, 1)
            run(0, first=True)
            with act.Fori(1, RUNS - 1) as r:
                run(r)
            run(RUNS - 1, last=True)
            hidden_hi(RUNS - 1, RUN - 1)

        @block.vector
        def _(dve):
            for n in ("xbT_lo_done", "act_done", "act_lo_done", "result_ready", "chosen_ready", "xr_ready"):
                dve.sem_inc(s[n], CR[n])

            def step(ins, name, n):
                ins.then_inc(s[name], 1)
                dve.wait_ge(s[name], n)

            def along_tile(a, n):
                return a.rearrange("p (k o) -> p k o", o=1).to_broadcast([P, a.shape[1], n])

            def across(a, n):
                return a.rearrange("p (o k) -> p o k", o=1).to_broadcast([P, n, a.shape[1]])

            nc.vector.memset(filling[:, 0:2 * D], 0.0).then_inc(s["fill_done"], 1)
            nc.vector.memset(filling[:, 2 * D:bl.WIDTH].bitcast(I32), 2 * bl.TOKEN_TILES * P).then_inc(s["fill_done"], 1)
            nc.vector.memset(ones[:, :], 1.0).then_inc(s["ones_done"], 1)
            for e in range(NE):
                nc.vector.memset(rank[:, :, e], float(NE - e))
                nc.vector.memset(region[:, e:e + 1], float(e * bl.REGION_BLOCKS * P))
                nc.vector.memset(next_row[:, e:e + 1], float(e * bl.REGION_BLOCKS * P))
            for table in ends:
                nc.vector.memset(table[:, 0:PAD], 0.0)
            nc.vector.memset(expert[:, 0:BEHIND], 0.0)
            nc.vector.memset(expert[:, BEHIND + bl.COUNT:], 0.0)
            dve.wait_ge(s["small_in"], 48)
            step(nc.vector.tensor_tensor(cen_row[:, :, :], cen_row[:, :, :], cen_row[:, :, :], ALU.mult), "cen_step", 1)
            step(nc.vector.tensor_reduce(cen_sq[:, :], cen_row[:, :, :], AX.X, ALU.add), "cen_step", 2)
            dve.wait_ge(s["iota_done"], 3)
            nc.vector.tensor_copy(block_no[:, :], block_no_int[:, :]).then_inc(s["cen_step"], 1)
            nc.vector.tensor_copy(earlier[:, :], earlier_f[:, :]).then_inc(s["const_done"], 1)

            STATS = 3

            def norm_stats(bb, at):
                for tile in range(TILES):
                    last = nc.vector.bn_stats(stats[:, tile, :], x[:, bass.ds(at + tile, 1), :])
                step(last, "stats_step", STATS * bb + 1)
                nc.vector.memset(pause[:, :], 0.0)
                for tile in range(TILES):
                    last = nc.vector.bn_aggr(meanvar[:, tile, :], stats[:, tile, :])
                step(last, "stats_step", STATS * bb + 2)
                nc.vector.tensor_scalar(varps[:, :], meanvar[:, :, 1], 1e-5, None, ALU.add).then_inc(s["stats_step"], 1)

            def normalise(bb, at):
                dve.wait_ge(s["rstd_ready"], bb + 1)
                if not isinstance(bb, int):
                    dve.wait_ge(s["base_ready"], 2 * bb)
                for tile in range(TILES):
                    nc.vector.tensor_scalar(xn[:, tile, :], x[:, bass.ds(at + tile, 1), :], meanvar[:, tile, 0:1],
                                            rstd[:, tile:tile + 1], ALU.subtract, ALU.mult).then_inc(s["xn_ready"], 1)

            def mean_square(bb):
                dve.wait_ge(s["square_ready"], TILES * bb + TILES)
                nc.vector.tensor_scalar(meansq[:, :], square[:, :], 1.0 / D, 1e-6, ALU.mult, ALU.add
                                        ).then_inc(s["meansq_ready"], 1)

            def rms_norm(bb):
                dve.wait_ge(s["rrms_ready"], bb + 1)
                if not isinstance(bb, int):
                    dve.wait_ge(s["rows_x"], bb)
                for tile in range(TILES):
                    nc.vector.scalar_tensor_tensor(out=xr[:, tile, :], in0=xn[:, tile, :], scalar=rrms[:, tile:tile + 1],
                                                   in1=scale_row[:, :], op0=ALU.mult, op1=ALU.mult
                                                   ).then_inc(s["xr_ready"], 1)

            def x_lo(bb):
                dve.wait_ge(s["xT_hi_done"], bb + 1)
                nc.vector.tensor_tensor(xT_lo[:, :], turn[0][:, :], xT_hi[:, :].bitcast(F32), ALU.subtract
                                        ).then_inc(s["xT_lo_done"], 1)

            ROUTE = 6

            def route(b):
                at = ROUTE * b
                dve.wait_ge(s["xr_sq_ready"], TILES * b + TILES)
                for tile in range(TILES):
                    last = nc.vector.tensor_scalar(norms[:, tile, :], cen_sq[:, :], xr_sq[:, tile:tile + 1], None, ALU.add)
                step(last, "route_step", at + 1)
                dve.wait_ge(s["dots_done"], b + 1)
                flat = "p t e -> p (t e)"
                step(nc.vector.scalar_tensor_tensor(
                    out=dist[:, :, :].rearrange(flat), in0=turn[1][:, 0:TILES * NE], scalar=-2.0,
                    in1=norms[:, :, :].rearrange(flat), op0=ALU.mult, op1=ALU.add), "route_step", at + 2)
                step(nc.vector.tensor_reduce(least[:, :], dist[:, :, :], AX.X, ALU.min), "route_step", at + 3)
                step(nc.vector.tensor_tensor(near[:, :, :], dist[:, :, :], along_tile(least[:, :], NE), ALU.is_equal),
                     "route_step", at + 4)
                step(nc.vector.tensor_tensor(near[:, :, :], near[:, :, :], rank[:, :, :], ALU.mult), "route_step", at + 5)
                step(nc.vector.tensor_reduce(first[:, :], near[:, :, :], AX.X, ALU.max), "route_step", at + 6)
                nc.vector.tensor_tensor(chosen[:, :, :], near[:, :, :], along_tile(first[:, :], NE), ALU.is_equal
                                        ).then_inc(s["chosen_ready"], 1)

            PLACES = 3

            def rows_of_tokens(b):
                at = PLACES * b
                dve.wait_ge(s["place_done"], b + 1)
                step(nc.vector.tensor_tensor(place[:, :, :], hidden[0][:, 0:TILES * NE].rearrange("p (t e) -> p t e", e=NE),
                                             across(next_row[:, :], TILES), ALU.add), "place_step", at + 1)
                step(nc.vector.tensor_tensor(mine[:, :, :], place[:, :, :], chosen[:, :, :], ALU.mult), "place_step", at + 2)
                nc.vector.tensor_tensor(next_row[:, :], next_row[:, :], hidden[1][:, 0:NE], ALU.add
                                        ).then_inc(s["next_done"], 1)
                step(nc.vector.tensor_reduce(row_f[:, :], mine[:, :, :], AX.X, ALU.add), "place_step", at + 3)
                dve.wait_ge(s["base_ready"], 2 * b + 1)
                nc.vector.tensor_copy(row_of[:, :], row_f[:, :]).then_inc(s["row_ready"], 1)
                dve.wait_ge(s["next_done"], b + 1)

            norm_stats(0, 0)
            dve.wait_ge(s["cen_split"], 1)
            nc.vector.tensor_tensor(cenT_lo[:, :], turn[0][:, 0:NE], cenT_hi[:, :].bitcast(F32), ALU.subtract
                                    ).then_inc(s["cen_split"], 1)
            normalise(0, 0)
            mean_square(0)
            rms_norm(0)
            x_lo(0)
            with dve.Fori(0, NB) as b:
                nxt = TILES * ((b + 1) % NB)
                norm_stats(b + 1, nxt)
                normalise(b + 1, nxt)
                route(b)
                mean_square(b + 1)
                rows_of_tokens(b)
                rms_norm(b + 1)
                x_lo(b + 1)

            n = 0

            def table(ins):
                nonlocal n
                n += 1
                step(ins, "tables_step", n)

            table(nc.vector.tensor_tensor(tokens[:, :], next_row[:, :], region[:, :], ALU.subtract))
            nc.vector.tensor_copy(next_row_int[:, :], next_row[:, :]).then_inc(s["tables_ready"], 1)
            table(nc.vector.tensor_scalar(tokens[:, :], tokens[:, :], 1.0 / P, None, ALU.mult))
            table(nc.vector.tensor_tensor(over[:, :, :], along_tile(tokens[:, :], bl.TOKEN_TILES),
                                          across(block_no[:, 0:bl.TOKEN_TILES], NE), ALU.is_gt))
            table(nc.vector.tensor_reduce(ends[0][:, PAD:PAD + NE], over[:, :, :], AX.X, ALU.add))
            nc.vector.tensor_scalar(skip[:, :], ends[0][:, PAD:PAD + NE], -1.0, float(bl.REGION_BLOCKS), ALU.mult, ALU.add)
            for i in range(3):
                back = PAD - 2 ** i
                table(nc.vector.tensor_tensor(ends[i + 1][:, PAD:PAD + NE], ends[i][:, PAD:PAD + NE],
                                              ends[i][:, back:back + NE], ALU.add))
            table(nc.vector.tensor_tensor(past[:, :, :], along_tile(block_no[:, :], NE),
                                          across(ends[3][:, PAD:PAD + NE], bl.COUNT), ALU.is_ge))
            table(nc.vector.tensor_reduce(expert_f[:, :], past[:, :, :], AX.X, ALU.add))
            table(nc.vector.tensor_scalar(expert[:, BEHIND:BEHIND + bl.COUNT], expert_f[:, :], float(NE - 1), None, ALU.min))
            for part, (back, size) in enumerate(((0, CH * P), (BEHIND, sh.F2))):
                runs = RUNS + 1 - part
                nc.vector.tensor_scalar(weights_at[:, 0:runs, part * RUN:(part + 1) * RUN],
                                        expert[:, back:back + runs * RUN].rearrange("p (r u) -> p r u", u=RUN),
                                        float(size), None, ALU.mult).then_inc(s["tables_ready"], 1)
            nc.vector.memset(weights_at[:, RUNS, RUN:2 * RUN], 0).then_inc(s["tables_ready"], 1)
            table(nc.vector.tensor_tensor(skipped[:, :, :], past[:, :, :], across(skip[:, :], bl.COUNT), ALU.mult))
            table(nc.vector.tensor_reduce(start_f[:, :], skipped[:, :, :], AX.X, ALU.add))
            table(nc.vector.tensor_tensor(start_f[:, :], start_f[:, :], block_no[:, :], ALU.add))
            nc.vector.tensor_scalar(start[:, :], start_f[:, :], float(P), None, ALU.mult).then_inc(s["tables_ready"], 1)

            def xb_lo(r, u):
                q, u = u // RUN, u % RUN
                dve.wait_ge(s["xbT_hi_done"], RUN * (r + q) + u + 1)
                nc.vector.tensor_tensor(xbT_lo[:, u % 2, :], turn[u % 2][:, 0:P], xbT_hi[:, u % 2, :].bitcast(F32),
                                        ALU.subtract).then_inc(s["xbT_lo_done"], 1)

            def gated(r, u):
                dve.wait_ge(s["gate_done"], RUN * r + u + 1)
                nc.vector.tensor_tensor(act_f[:, u % 2, :], hidden[u % 2][:, 0:sh.F], gate[:, u % 2, :], ALU.mult
                                        ).then_inc(s["act_done"], 1)

            def hidden_lo(r, u):
                dve.wait_ge(s["act_hi_done"], RUN * r + u + 1 + 1)
                nc.vector.tensor_tensor(act_lo[:, u % 2, :], actT[u % 2][:, 0:sh.F], act_hi[:, u % 2, :].bitcast(F32),
                                        ALU.subtract).then_inc(s["act_lo_done"], 1)

            def result(r, u):
                q, u = u // RUN, u % RUN
                dve.wait_ge(s_rest[u], 16 * (r + q) + 16)
                dve.wait_ge(s["down_done"], RUN * (r + q) + u + 1 + CR["down_done"])
                nc.vector.tensor_tensor(rest[:, u, 0:D], rest[:, u, 0:D], yb[u % 2][:, 0:D], ALU.add
                                        ).then_inc(s["result_ready"], 1)

            def run(r, first=False, last=False):
                for u in range(RUN):
                    if not (first and u < 2):
                        result(r, u - 2)
                    gated(r, u)
                    if not (first and u < 1):
                        hidden_lo(r, u - 1)
                    if not (last and u >= RUN - 2):
                        xb_lo(r, u + 2)

            xb_lo(0, 0)
            xb_lo(0, 1)
            run(0, first=True)
            with dve.Fori(1, RUNS - 1) as r:
                run(r)
            run(RUNS - 1, last=True)
            result(RUNS - 1, RUN - 2)
            hidden_lo(RUNS - 1, RUN - 1)
            result(RUNS - 1, RUN - 1)

        @block.gpsimd
        def _(pool):
            pool.sem_inc(s["row_ready"], CR["row_ready"])
            nc.gpsimd.memset(power[:, :], -0.5).then_inc(s["pool_setup"], 1)
            nc.gpsimd.memset(earlier_f[:, :], 1.0).then_inc(s["pool_setup"], 1)
            nc.gpsimd.iota(token[:, :], pattern=[[P, bl.TOKEN_TILES]], base=0, channel_multiplier=1
                           ).then_inc(s["iota_done"], 1)
            nc.gpsimd.iota(block_no_int[:, :], pattern=[[1, bl.COUNT]], base=0, channel_multiplier=0
                           ).then_inc(s["iota_done"], 1)
            pool.wait_ge(s["pool_setup"], 2)
            nc.gpsimd.affine_select(out=earlier_f[:, :], in_=earlier_f[:, :], compare_op=ALU.is_gt, fill=0.0, base=0,
                                    pattern=[[1, P]], channel_multiplier=-1).then_inc(s["iota_done"], 1)
            pool.wait_ge(s["iota_done"], 3)

            def inverse_std(bb):
                pool.wait_ge(s["stats_step"], 3 * bb + 3)
                nc.gpsimd.tensor_tensor(rstd[:, :], varps[:, :], power[:, :], ALU.pow).then_inc(s["rstd_ready"], 1)

            def inverse_rms(bb):
                pool.wait_ge(s["meansq_ready"], bb + 1)
                nc.gpsimd.tensor_tensor(rrms[:, :], meansq[:, :], power[:, :], ALU.pow).then_inc(s["rrms_ready"], 1)

            def residual(bb, at, start=False):
                pool.wait_ge(s["xn_ready"], TILES * bb + TILES)
                if not start:
                    pool.wait_ge(s["scattered"], 16 * TILES * bb)
                nc.gpsimd.tensor_copy(rows[:, :, 2 * D:bl.WIDTH].rearrange("p t o -> p (t o)").bitcast(I32),
                                      token[:, bass.ds(at, TILES)]).then_inc(s["base_ready"], 1)
                nc.gpsimd.tensor_tensor(rows[:, :, D:2 * D], x[:, bass.ds(at, TILES), :], xn[:, :, :], ALU.add
                                        ).then_inc(s["base_ready"], 1)

            def split_weights(b):
                w = bass.ds(b * sh.F2, sh.F2)
                pool.wait_ge(s["up_hi_done"], b + 1)
                nc.gpsimd.tensor_tensor(up_lo[:, w], up_raw[:, w], up_hi[:, w].bitcast(F32), ALU.subtract
                                        ).then_inc(s["weights_split"], 1)
                w = bass.ds(b * (CH * P), CH * P)
                pool.wait_ge(s["down_hi_done"], b + 1)
                nc.gpsimd.tensor_tensor(down_lo[:, w], down_raw[:, w], down_hi[:, w].bitcast(F32), ALU.subtract
                                        ).then_inc(s["weights_split"], 1)

            def send(b):
                pool.wait_ge(s["rows_x"], b + 1)
                pool.wait_ge(s["base_ready"], 2 * b + 2)
                pool.wait_ge(s["row_ready"], b + 1 + CR["row_ready"])
                nc.gpsimd.tensor_tensor(hold[:, :], power[:, 0:1], power[:, 0:1], ALU.add)
                for tile in range(TILES):
                    nc.gpsimd.indirect_dma_start(
                        sorted_rows[:, :], bass.IndirectOffsetOnAxis(ap=row_of[:, tile:tile + 1], axis=0),
                        rows[:, tile, :], None
                    ).then_inc(s["scattered"], 16)

            inverse_std(0)
            residual(0, 0, start=True)
            inverse_rms(0)
            with pool.Fori(0, NB) as b:
                inverse_std(b + 1)
                inverse_rms(b + 1)
                send(b)
                split_weights(b)
                residual(b + 1, TILES * ((b + 1) % NB))

            pool.sem_inc(s["held"], CR["held"])
            last_token = pool.to_reg(bl.TOKEN_TILES * P - 1)
            with pool.Fori(0, RUNS) as r:
                for u in range(RUN):
                    pool.wait_ge(s["result_ready"], RUN * r + u + 1 + CR["result_ready"])
                    pool.wait_ge(s["held"], RUN * r + u + CR["held"])
                    nc.gpsimd.tensor_tensor(hold[:, :], power[:, 0:1], power[:, 0:1], ALU.add).then_inc(s["held"], 1)
                    nc.gpsimd.indirect_dma_start(
                        out_rows, bass.IndirectOffsetOnAxis(ap=rest[:, u, D:D + 1].bitcast(I32), axis=0),
                        rest[:, u, 0:D], None, bounds_check=last_token, oob_is_err=False
                    ).then_inc(s_out[u], 16)
            for u in range(RUN):
                pool.wait_ge(s_out[u], 16 * RUNS)




def _sorted_shape(dram):
    bl = Blocks(Shapes(dram["x"], dram["Wq"], dram["up_w"]))
    return [bl.ROWS, bl.WIDTH]


def build(nc, dram):
    sh = Shapes(dram["x"], dram["Wq"], dram["up_w"])
    with ExitStack() as ctx:
        x = ctx.enter_context(nc.sbuf_tensor("x_all", [P, sh.B * sh.TILES, P], F32))
        ident = ctx.enter_context(nc.sbuf_tensor("ident", [P, P], F32))
        attention(nc, {"x": x, "ident": ident}, dram, sh)
        feed_forward(nc, {"x": x, "ident": ident}, dram, sh)


_INS = {
    "x": "L0_attn_query", "Wq": "L0_attn_Wq", "Wk": "L0_attn_Wk", "Wv": "L0_attn_Wv", "Wp": "L0_attn_Wp",
    "bp": "L0_attn_bp", "scale": "L0_ffn_scale", "centroids": "L0_ffn_centroids", "up_w": "L0_ffn_up_w",
    "down_w": "L0_ffn_down_w",
}


def kernel(**inputs):
    import numpy as _np
    import concourse.bacc as _bacc
    from concourse.bass_utils import run_bass_kernel_spmd as _run

    nc = _bacc.Bacc("TRN2", target_bir_lowering=False, num_devices=1)
    arrays, dram = {}, {}
    for name, given in _INS.items():
        a = _np.ascontiguousarray(inputs[given])
        arrays[f"in_{name}"] = a
        dram[name] = nc.dram_tensor(f"in_{name}", a.shape, mybir.dt.from_np(a.dtype), kind="ExternalInput").ap()
    shape = arrays["in_x"].shape
    dram["out"] = nc.dram_tensor("out_x", shape, F32, kind="ExternalOutput").ap()
    dram["rden"] = nc.dram_tensor("rden_rows_dram", [2, 2 * shape[1]], F32, kind="Internal").ap()
    sorted_shape = _sorted_shape(dram)
    dram["sorted"] = nc.dram_tensor("sorted_rows_dram", sorted_shape, F32, kind="Internal").ap()
    build(nc, dram)
    return _run(nc, [arrays], core_ids=[0]).results[0]["out_x"]
```

```python
from contextlib import ExitStack

import concourse.bass as bass
from concourse import mybir

F32 = mybir.dt.float32
F32R = mybir.dt.float32r
BF16 = mybir.dt.bfloat16
ALU = mybir.AluOpType
ACT = mybir.ActivationFunctionType
AX = mybir.AxisListType

P = 128


class Shapes:

    def __init__(self, x, wq, up_w):
        self.B, self.N, self.D = x.shape
        self.H, _, self.E = wq.shape
        self.NE, _, self.F2 = up_w.shape
        self.F = self.F2 // 2
        self.PAIRS = self.H // 2
        self.TILES = self.N // P
        assert self.D == P and self.E == 64 and self.N == 512 and self.PAIRS == 8 and self.F == 256



RUN = 8


class Blocks:

    def __init__(self, sh):
        self.TOKEN_TILES = sh.B * sh.TILES
        self.COUNT = -(-(self.TOKEN_TILES + sh.NE - 1) // RUN) * RUN
        self.REGION_BLOCKS = self.TOKEN_TILES + 1
        self.EMPTY = self.COUNT - self.TOKEN_TILES
        self.ROWS = (sh.NE * self.REGION_BLOCKS + self.EMPTY) * P
        self.WIDTH = 2 * sh.D + 1


class Routing:
    pass


def make_routing(nc, ctx, t, dram, sh):
    NE, TILES, N, D = sh.NE, sh.TILES, sh.N, sh.D
    bl = Blocks(sh)
    I32 = mybir.dt.int32
    x, ident, staging = t["x"], t["ident"], t["staging"]

    def sb(name, shape, dt=F32):
        return ctx.enter_context(nc.sbuf_tensor(name, shape, dt))

    def piece(n, half):
        return staging[:, n, 512 * half:512 * half + 512]

    def tiles_of(a):
        return a.rearrange("p (t d) -> p t d", d=D)

    xn, xr = tiles_of(piece(0, 0)), tiles_of(piece(0, 1))
    junk_n, junk_r = tiles_of(piece(2, 0)), tiles_of(piece(2, 1))
    cen_row = staging[:, 2, :].rearrange("p (e d) -> p e d", d=D)
    cenT = staging[:, 1, 0:NE]
    earlier_f = staging[:, 0, 0:P]

    cenT_hi = sb("cenT_hi", [P, NE], F32R)
    cenT_lo = sb("cenT_lo", [P, NE], F32R)
    cen_sq = sb("cen_sq", [P, NE])
    scale_row = sb("scale_row", [P, P])
    rank = sb("rank", [P, TILES, NE])
    power = sb("power2", [P, TILES])
    earlier = sb("earlier", [P, P], BF16)
    ones = sb("ones_bf16", [P, P], BF16)
    token = sb("token", [P, bl.TOKEN_TILES], I32)
    stats = sb("stats2", [P, TILES, 6])
    pause = sb("pause2", [P, 1])
    meanvar = sb("meanvar2", [P, TILES, 2])
    varps = sb("varps2", [P, TILES])
    rstd = sb("rstd2", [P, TILES])
    hold = sb("hold", [P, 1])
    square = sb("square", [P, TILES])
    meansq = sb("meansq", [P, TILES])
    rrms = sb("rrms", [P, TILES])
    xr_sq = sb("xr_sq", [P, TILES])
    norms = sb("norms", [P, TILES, NE])
    dist = sb("dist", [P, TILES, NE])
    least = sb("least", [P, TILES])
    near = sb("near", [P, TILES, NE])
    first = sb("first", [P, TILES])
    chosen = sb("chosen", [P, TILES, NE], BF16)
    place = sb("place", [P, TILES, NE])
    mine = sb("mine", [P, TILES, NE])
    row_f = sb("row_f", [P, TILES])
    region = sb("region", [P, NE])
    next_row = sb("next_row", [P, NE])
    rows = sb("rows", [P, TILES, bl.WIDTH])
    row_of = sb("row_of", [P, TILES], I32)

    names = """small_in cen_split cen_step iota_done const_done pool_setup ones_done
        stats_step rstd_ready xn_ready base_ready square_ready meansq_ready rrms_ready xr_ready rows_x xr_sq_ready
        xT_done xT_hi_done xT_lo_done dots_done route_step chosen_ready place_done place_step next_done row_ready
        sent""".split()
    s = {n: ctx.enter_context(nc.semaphore("r_" + n)) for n in names}
    STATS, ROUTE, PLACES = 3, 6, 3
    sorted_rows = dram["sorted"]

    def bank_read(kind, g):
        return {"rT": (s["xT_lo_done"], g + 1), "dots": (s["route_step"], ROUTE * g + 2),
                "places": (s["place_step"], PLACES * g + 1), "totals": (s["next_done"], g + 1)}[kind]

    def along_tile(a, n):
        return a.rearrange("p (k o) -> p k o", o=1).to_broadcast([P, a.shape[1], n])

    def across(a, n):
        return a.rearrange("p (o k) -> p o k", o=1).to_broadcast([P, n, a.shape[1]])

    def load_constants(sp):
        sp.dma_start(cenT, dram["centroids"].rearrange("e d -> d e"), allow_slow_non_contiguous=True
                     ).then_inc(s["small_in"], 16)
        sp.dma_start(cen_row, dram["centroids"].rearrange("(o e) d -> o e d", o=1).to_broadcast([P, NE, P])
                     ).then_inc(s["small_in"], 16)
        sp.dma_start(scale_row[:, :], dram["scale"].rearrange("(o d) -> o d", o=1).to_broadcast([P, P])
                     ).then_inc(s["small_in"], 16)

    def patterns(pool):
        nc.gpsimd.memset(power[:, :], -0.5).then_inc(s["pool_setup"], 1)
        nc.gpsimd.memset(earlier_f, 1.0).then_inc(s["pool_setup"], 1)
        nc.gpsimd.iota(token[:, :], pattern=[[P, bl.TOKEN_TILES]], base=0, channel_multiplier=1
                       ).then_inc(s["iota_done"], 1)
        pool.wait_ge(s["pool_setup"], 2)
        nc.gpsimd.affine_select(out=earlier_f, in_=earlier_f, compare_op=ALU.is_gt, fill=0.0, base=0,
                                pattern=[[1, P]], channel_multiplier=-1).then_inc(s["iota_done"], 1)
        pool.wait_ge(s["iota_done"], 2)

    def centroids_hi(act):
        act.wait_ge(s["small_in"], 48)
        nc.scalar.activation(cenT_hi[:, :], cenT, ACT.Copy).then_inc(s["cen_split"], 1)

    def constants(dve):
        for e in range(NE):
            nc.vector.memset(rank[:, :, e], float(NE - e))
            nc.vector.memset(region[:, e:e + 1], float(e * bl.REGION_BLOCKS * P))
            nc.vector.memset(next_row[:, e:e + 1], float(e * bl.REGION_BLOCKS * P))
        nc.vector.memset(ones[:, :], 1.0).then_inc(s["ones_done"], 1)
        dve.wait_ge(s["small_in"], 48)
        nc.vector.tensor_tensor(cen_row, cen_row, cen_row, ALU.mult).then_inc(s["cen_step"], 1)
        dve.wait_ge(s["cen_step"], 1)
        nc.vector.tensor_reduce(cen_sq[:, :], cen_row, AX.X, ALU.add).then_inc(s["cen_step"], 1)
        dve.wait_ge(s["cen_split"], 1)
        nc.vector.tensor_tensor(cenT_lo[:, :], cenT, cenT_hi[:, :].bitcast(F32), ALU.subtract
                                ).then_inc(s["cen_split"], 1)
        dve.wait_ge(s["iota_done"], 2)
        nc.vector.tensor_copy(earlier[:, :], earlier_f).then_inc(s["const_done"], 1)
        dve.wait_ge(s["const_done"], 1)

    def step(dve, ins, name, n):
        ins.then_inc(s[name], 1)
        dve.wait_ge(s[name], n)

    def norm_stats(dve, g, at):
        for tile in range(TILES):
            last = nc.vector.bn_stats(stats[:, tile, :], x[:, bass.ds(at + tile, 1), :])
        step(dve, last, "stats_step", STATS * g + 1)
        nc.vector.memset(pause[:, :], 0.0)
        for tile in range(TILES):
            last = nc.vector.bn_aggr(meanvar[:, tile, :], stats[:, tile, :])
        step(dve, last, "stats_step", STATS * g + 2)
        nc.vector.tensor_scalar(varps[:, :], meanvar[:, :, 1], 1e-5, None, ALU.add).then_inc(s["stats_step"], 1)

    def inverse_std(pool, g):
        pool.wait_ge(s["stats_step"], STATS * g + STATS)
        nc.gpsimd.tensor_tensor(rstd[:, :], varps[:, :], power[:, :], ALU.pow).then_inc(s["rstd_ready"], 1)

    def normalise(dve, g, at):
        dve.wait_ge(s["rstd_ready"], g + 1)
        for tile in range(TILES):
            nc.vector.tensor_scalar(xn[:, tile, :], x[:, bass.ds(at + tile, 1), :], meanvar[:, tile, 0:1],
                                    rstd[:, tile:tile + 1], ALU.subtract, ALU.mult).then_inc(s["xn_ready"], 1)

    def squares(act, junk, src, dst, done, ready, g):
        act.wait_ge(s[ready], TILES * g + TILES)
        for tile in range(TILES):
            nc.scalar.activation(junk[:, tile, :], src[:, tile, :], ACT.Square, accum_out=dst[:, tile:tile + 1]
                                 ).then_inc(s[done], 1)

    def squares_n(act, g):
        squares(act, junk_n, xn, square, "square_ready", "xn_ready", g)

    def residual(pool, g, at):
        pool.wait_ge(s["xn_ready"], TILES * g + TILES)
        nc.gpsimd.tensor_copy(rows[:, :, 2 * D:bl.WIDTH].rearrange("p t o -> p (t o)").bitcast(I32),
                              token[:, bass.ds(at, TILES)]).then_inc(s["base_ready"], 1)
        nc.gpsimd.tensor_tensor(rows[:, :, D:2 * D], x[:, bass.ds(at, TILES), :], xn, ALU.add
                                ).then_inc(s["base_ready"], 1)

    def mean_square(dve, g):
        dve.wait_ge(s["square_ready"], TILES * g + TILES)
        nc.vector.tensor_scalar(meansq[:, :], square[:, :], 1.0 / D, 1e-6, ALU.mult, ALU.add
                                ).then_inc(s["meansq_ready"], 1)

    def inverse_rms(pool, g):
        pool.wait_ge(s["meansq_ready"], g + 1)
        nc.gpsimd.tensor_tensor(rrms[:, :], meansq[:, :], power[:, :], ALU.pow).then_inc(s["rrms_ready"], 1)

    def rms_norm(dve, g):
        dve.wait_ge(s["rrms_ready"], g + 1)
        for tile in range(TILES):
            nc.vector.scalar_tensor_tensor(out=xr[:, tile, :], in0=xn[:, tile, :], scalar=rrms[:, tile:tile + 1],
                                           in1=scale_row[:, :], op0=ALU.mult, op1=ALU.mult
                                           ).then_inc(s["xr_ready"], 1)

    def transpose_rows(pe, bank, g):
        pe.wait_ge(s["xr_ready"], TILES * g + TILES)
        for tile in range(TILES):
            mm = pe.transpose(bank[:, tile * P:(tile + 1) * P], xr[:, tile, :], ident[:, :])
        mm.then_inc(s["xT_done"], 1)

    def rows_hi(act, bank, xT, g):
        act.wait_ge(s["xT_done"], g + 1)
        nc.scalar.activation(xT[0][:, :], bank[:, :], ACT.Copy).then_inc(s["xT_hi_done"], 1)

    def rows_lo(dve, bank, xT, g):
        dve.wait_ge(s["xT_hi_done"], g + 1)
        nc.vector.tensor_tensor(xT[1][:, :], bank[:, :], xT[0][:, :].bitcast(F32), ALU.subtract
                                ).then_inc(s["xT_lo_done"], 1)

    def squares_r(act, g):
        squares(act, junk_r, xr, xr_sq, "xr_sq_ready", "xr_ready", g)

    def rows_x(act, g):
        act.wait_ge(s["base_ready"], 2 * g + 1)
        nc.scalar.activation(rows[:, :, 0:D], xr, ACT.Copy).then_inc(s["rows_x"], 1)

    def centroid_products(pe, bank, xT, g):
        pe.wait_ge(s["xT_lo_done"], g + 1)
        pe.wait_ge(s["cen_split"], 2)
        for tile in range(TILES):
            out, cols = bank[:, NE * tile:NE * tile + NE], slice(tile * P, (tile + 1) * P)
            pe.matmul(out, xT[0][:, cols], cenT_hi[:, :], start=True, stop=False)
            pe.matmul(out, xT[0][:, cols], cenT_lo[:, :], start=False, stop=False)
            mm = pe.matmul(out, xT[1][:, cols], cenT_hi[:, :], start=False, stop=True)
        mm.then_inc(s["dots_done"], 1)

    def sum_norms(dve, g):
        dve.wait_ge(s["xr_sq_ready"], TILES * g + TILES)
        for tile in range(TILES):
            last = nc.vector.tensor_scalar(norms[:, tile, :], cen_sq[:, :], xr_sq[:, tile:tile + 1], None, ALU.add)
        last.then_inc(s["route_step"], 1)

    def route(dve, bank, g):
        sum_norms(dve, g)
        at = ROUTE * g
        dve.wait_ge(s["route_step"], at + 1)
        dve.wait_ge(s["dots_done"], g + 1)
        flat = "p t e -> p (t e)"
        step(dve, nc.vector.scalar_tensor_tensor(
            out=dist[:, :, :].rearrange(flat), in0=bank[:, 0:TILES * NE], scalar=-2.0,
            in1=norms[:, :, :].rearrange(flat), op0=ALU.mult, op1=ALU.add), "route_step", at + 2)
        step(dve, nc.vector.tensor_reduce(least[:, :], dist[:, :, :], AX.X, ALU.min), "route_step", at + 3)
        step(dve, nc.vector.tensor_tensor(near[:, :, :], dist[:, :, :], along_tile(least[:, :], NE), ALU.is_equal),
             "route_step", at + 4)
        step(dve, nc.vector.tensor_tensor(near[:, :, :], near[:, :, :], rank[:, :, :], ALU.mult), "route_step", at + 5)
        step(dve, nc.vector.tensor_reduce(first[:, :], near[:, :, :], AX.X, ALU.max), "route_step", at + 6)
        nc.vector.tensor_tensor(chosen[:, :, :], near[:, :, :], along_tile(first[:, :], NE), ALU.is_equal
                                ).then_inc(s["chosen_ready"], 1)

    def places(pe, bank, totals, g):
        pe.wait_ge(s["chosen_ready"], g + 1)
        pe.wait_ge(s["ones_done"], 1)
        pe.wait_ge(s["const_done"], 1)
        flat = chosen[:, :, :].rearrange("p t e -> p (t e)")
        pe.matmul(bank[:, 0:TILES * NE], earlier[:, :], flat, start=True, stop=False)
        for tile in range(TILES - 1):
            left = TILES - 1 - tile
            pe.matmul(bank[:, (tile + 1) * NE:TILES * NE], ones[:, :],
                      chosen[:, tile:tile + 1, :].to_broadcast([P, left, NE]), start=False,
                      stop=(left == 1))
        for tile in range(TILES):
            mm = pe.matmul(totals[:, 0:NE], ones[:, :], chosen[:, tile, :],
                           start=(tile == 0), stop=(tile == TILES - 1))
        mm.then_inc(s["place_done"], 1)

    def rows_of_tokens(dve, bank, totals, g):
        at = PLACES * g
        dve.wait_ge(s["place_done"], g + 1)
        step(dve, nc.vector.tensor_tensor(place[:, :, :], bank[:, 0:TILES * NE].rearrange("p (t e) -> p t e", e=NE),
                                     across(next_row[:, :], TILES), ALU.add), "place_step", at + 1)
        step(dve, nc.vector.tensor_tensor(mine[:, :, :], place[:, :, :], chosen[:, :, :], ALU.mult), "place_step", at + 2)
        nc.vector.tensor_tensor(next_row[:, :], next_row[:, :], totals[:, 0:NE], ALU.add
                                ).then_inc(s["next_done"], 1)
        step(dve, nc.vector.tensor_reduce(row_f[:, :], mine[:, :, :], AX.X, ALU.add), "place_step", at + 3)
        dve.wait_ge(s["base_ready"], 2 * g + 1)
        nc.vector.tensor_copy(row_of[:, :], row_f[:, :]).then_inc(s["row_ready"], 1)
        dve.wait_ge(s["next_done"], g + 1)

    def send(pool, g):
        pool.wait_ge(s["rows_x"], g + 1)
        pool.wait_ge(s["base_ready"], 2 * g + 2)
        pool.wait_ge(s["row_ready"], g + 1)
        nc.gpsimd.tensor_tensor(hold[:, :], power[:, 0:1], power[:, 0:1], ALU.add)
        for tile in range(TILES):
            nc.gpsimd.indirect_dma_start(
                sorted_rows[:, :], bass.IndirectOffsetOnAxis(ap=row_of[:, tile:tile + 1], axis=0),
                rows[:, tile, :], None).then_inc(s["sent"], 16)

    def sent(pool, g):
        pool.wait_ge(s["sent"], 16 * TILES * g + 16 * TILES)

    r = Routing()
    r.load_constants = load_constants
    r.patterns = patterns
    r.centroids_hi = centroids_hi
    r.constants = constants
    r.norm_stats = norm_stats
    r.inverse_std = inverse_std
    r.normalise = normalise
    r.squares_n = squares_n
    r.residual = residual
    r.mean_square = mean_square
    r.inverse_rms = inverse_rms
    r.rms_norm = rms_norm
    r.transpose_rows = transpose_rows
    r.rows_hi = rows_hi
    r.rows_lo = rows_lo
    r.squares_r = squares_r
    r.rows_x = rows_x
    r.centroid_products = centroid_products
    r.route = route
    r.places = places
    r.rows_of_tokens = rows_of_tokens
    r.send = send
    r.sent = sent
    r.bank_read = bank_read
    r.along_tile = along_tile
    r.across = across
    r.next_row, r.region = next_row, region
    return r



SLOTS = 3
PRE, LOOP, FIRST = 5, 38, 34
PROJECT_AT = {0: "q", 2: "k"}
ATTEND_AT = {1: 0, 2: 1, 4: 2, 5: 3}
SUMS_AT = 6
VALUES_AT = {1: (0,), 2: (1,), 4: (2, 3), 5: (4,), 6: (5,), 7: (6, 7)}


def work_order():
    head = [("xT", 0, 0)] + [(w, p, 0) for p in (0, 1) for w in "qk"]
    body = []
    routed = {(5, 4): ["rT"], (6, 1): ["dots"], (7, 3): ["places", "totals"]}
    for i in range(8):
        for u in range(8):
            if i <= 5 and u in PROJECT_AT:
                body += [(PROJECT_AT[u], i + 2, 0)]
            if i == 0:
                body += [("v", v, 0) for v in VALUES_AT.get(u, ())]
            body += [(kind, 0, -1) for kind in routed.get((i, u), ())]
        if i >= 1:
            body += [("den", i - 1, 0)]
        if i == 6:
            body += [("xT", 0, 1)]
    body += [("q", 0, 1), ("k", 0, 1), ("q", 1, 1), ("den", 7, 0), ("k", 1, 1), ("x1T", 0, 0)]
    first = [use for use in body if use[2] >= 0]
    assert len(head) == PRE and len(body) == LOOP and LOOP % 2 == 0
    assert len(first) == FIRST and FIRST % 2 == 0
    return {"head": head, "first": first, "body": body}


def attention(nc, t, dram, sh, routing):
    NB, PAIRS, TILES, N = sh.B, sh.PAIRS, sh.TILES, sh.N
    uses = work_order()
    bank_of = {(part,) + u[:2]: ((1 if part == "head" else 1 + PRE) + i) % 2
               for part in uses for i, u in enumerate(uses[part])}

    def part_of(part, b):
        return "first" if part == "body" and isinstance(b, int) else part

    with ExitStack() as ctx:
        def sb(name, shape, dt=F32):
            return ctx.enter_context(nc.sbuf_tensor(name, shape, dt))

        def pb(name):
            return ctx.enter_context(nc.psum_tensor(name, [P, 512], F32))

        def sem(name):
            return ctx.enter_context(nc.semaphore(name))

        x, ident = t["x"], t["ident"]
        w_raw = t["staging"]
        w_hi = {w: sb(f"W{w}_hi", [P, 1024], F32R) for w in "qkv"}
        w_lo = {w: sb(f"W{w}_lo", [P, 1024], F32R) for w in "qkv"}
        wp = sb("wp", [P, PAIRS, P])
        bp = sb("bp", [P, 1])
        ones = sb("ones", [P, 64])
        stats = sb("stats", [P, TILES, 6])
        pause = sb("pause", [P, 1])
        meanvar = sb("meanvar", [P, TILES, 2])
        varps = sb("varps", [P, TILES])
        rstd = sb("rstd", [P, TILES])
        power = sb("power", [P, TILES])
        xn = sb("xn", [P, TILES, P])
        xT_hi = sb("xT_hi", [P, N], F32R)
        xT_lo = sb("xT_lo", [P, N], F32R)
        V = sb("V", [P, TILES, 1024])
        T1q = sb("T1q", [P, SLOTS, 2, N], F32R)
        T1k = sb("T1k", [P, SLOTS, 2, N], F32R)
        T2q = sb("T2q", [P, SLOTS, 2, N], F32R)
        T2k = sb("T2k", [P, SLOTS, 2, N], F32R)
        negmax = sb("negmax", [P, SLOTS, 2, 4], F32R)
        probs = sb("probs", [P, 2, 2, TILES, N])
        half_sums = sb("half_sums", [P, 2, N])
        prob_sums = sb("prob_sums", [P, 2, 2, N])
        out_T = sb("out_T", [P, PAIRS, N])
        den_rows = sb("den_rows", [P, 2, N])
        den = sb("den", [P, 2, 8])
        rden = sb("rden", [P, 2, 8])
        rden_rows = sb("rden_rows", [P, 2, N])
        last_rden = sb("last_rden", [P, N])
        proj_T = sb("proj_T", [P, N])

        st = [pb("st0"), pb("st1")]
        mx = [pb("mx0"), pb("mx1")]
        ob = [pb("ob0"), pb("ob1")]
        work = [pb("work0"), pb("work1")]

        names = """x0_in x_in wp_in w_hi_done w_lo_done setup ln_step ln_done rstd_ready xT_done xT_hi_done xT_lo_done
            qk_done hi_done lo_done v_done v_act v_dve mx_done max_done st_done exp_done av_done o_done
            den_done den_copied rden_done sums_step sums_done scaled proj_done proj_copied x1T_done
            x1_done ident_step T2k_zero last_rden last_scaled""".split()
        s = {n: sem(n) for n in names}
        s_w = {w: sem(f"w{w}_in") for w in "qkv"}
        s_dup_q = [sem(f"dup_q{i}") for i in range(SLOTS)]
        s_dup_k = [sem(f"dup_k{i}") for i in range(SLOTS)]
        s_c = [[sem(f"max_row{i}{j}") for j in range(2)] for i in range(SLOTS)]
        s_n1 = [sem(f"den_out{i}") for i in range(2)]
        s_n2 = [sem(f"rden_out{i}") for i in range(2)]
        s_n3 = [sem(f"rden_in{i}") for i in range(2)]

        CR = {"st_done": 24, "exp_done": 2, "av_done": 2, "o_done": 2, "sums_done": 4, "rden_done": 2,
              "proj_done": 1, "proj_copied": 1, "den_done": 2, "scaled": 2, "x1_done": 1, "den_copied": 1}

        def v_sum(name, n):
            return n + CR[name]

        def in_slot(p):
            return len(range(p % SLOTS, PAIRS, SLOTS)), p // SLOTS

        def dma_of_slot(b, p):
            a, k = in_slot(p)
            return 16 * a * b + 16 * (k + 1)

        def pair_before_in_slot(b, p):
            return 8 * b + (p - SLOTS if p >= SLOTS else {0: -2, 1: -1, 2: -3}[p])

        def of_parity(p):
            return len(range(p % 2, PAIRS - 1, 2))

        def wait_work_free(eng, part, kind, index, b):
            part = part_of(part, b)
            i = [u[:2] for u in uses[part]].index((kind, index))
            if part == "head" and i < 2:
                return
            if i >= 2:
                prev = [uses[part][i - 2]]
            else:
                eng.wait_ge(s["hi_done"], 32 * b + 8)
                eng.wait_ge(s["lo_done"], 32 * b + 8)
                eng.wait_ge(s["x1_done"], v_sum("x1_done", b))
                return
            for k, n, ahead in prev:
                bb = b + ahead
                if k in "qk":
                    g = 16 * bb + 2 * n + (k == "k")
                    eng.wait_ge(s["hi_done"], 2 * g + 2)
                    eng.wait_ge(s["lo_done"], 2 * g + 2)
                elif k == "xT":
                    eng.wait_ge(s["xT_lo_done"], bb + 1)
                elif k in ("rT", "dots", "places", "totals"):
                    eng.wait_ge(*routing.bank_read(k, bb))
                elif k == "v":
                    eng.wait_ge(s["v_act" if n % 2 == 0 else "v_dve"], 4 * bb + n // 2 + 1)
                elif k == "den" and n == PAIRS - 1:
                    eng.wait_ge(s["last_rden"], bb + 1)
                elif k == "den":
                    eng.wait_ge(s["den_copied"], v_sum("den_copied", 7 * bb + n + 1))
                else:
                    eng.wait_ge(s["x1_done"], v_sum("x1_done", bb + 1))

        SETUP = 4

        block = ctx.enter_context(nc.Block())

        @block.sync
        def _(sp):
            rows = dram["x"].rearrange("b (t p) d -> p (b t) d", p=P)
            for b in range(NB):
                tiles = slice(TILES * b, TILES * b + TILES)
                sp.dma_start(x[:, tiles, :], rows[:, tiles, :]).then_inc(s["x_in" if b else "x0_in"], 16)

            def dup(w, p, bb):
                g = 16 * bb + 2 * p + (w == "k")
                sp.wait_ge(s["hi_done"], 2 * g + 2)
                if w == "q":
                    sp.dma_start(T2q[0:64, p % SLOTS].bitcast(F32), T1q[0:64, p % SLOTS].bitcast(F32)
                                 ).then_inc(s_dup_q[p % SLOTS], 16)
                else:
                    sp.dma_start(T1k[64:P, p % SLOTS].bitcast(F32), T1k[0:64, p % SLOTS].bitcast(F32)
                                 ).then_inc(s_dup_k[p % SLOTS], 16)

            def max_row(p, hh, bb):
                sp.wait_ge(s["max_done"], 64 * bb + 8 * p + 4 * hh + 4)
                sp.dma_start(T2q[64:65, p % SLOTS, hh, :].bitcast(F32).rearrange("o (p j) -> o p j", j=4),
                             negmax[:, p % SLOTS, hh, :].bitcast(F32)).then_inc(s_c[p % SLOTS][hh], 16)

            def sums_out(p, b):
                sp.wait_ge(s["den_copied"], v_sum("den_copied", 7 * b + p + 1))
                for hh in range(2):
                    sp.dma_start(den[64 * hh:64 * hh + 64, p % 2, :],
                                 den_rows[64 * hh:64 * hh + 1, p % 2, :].rearrange("o (q j) -> o q j", j=8)
                                 ).then_inc(s_n1[p % 2], 16)

            def rden_out(p, b):
                sp.wait_ge(s["rden_done"], v_sum("rden_done", 7 * b + p + 1))
                sp.dma_start(dram["rden"][p % 2].rearrange("(q j) -> q j", j=8), rden[:, p % 2, :]
                             ).then_inc(s_n2[p % 2], 16)

            def rden_in(p, b):
                sp.wait_ge(s_n2[p % 2], 16 * of_parity(p) * b + 16 * (p // 2) + 16)
                for hh in range(2):
                    row = dram["rden"][p % 2:p % 2 + 1, 512 * hh:512 * hh + 512]
                    sp.dma_start(rden_rows[64 * hh:64 * hh + 64, p % 2, :], row.to_broadcast([64, 512])
                                 ).then_inc(s_n3[p % 2], 16)

            for p in (0, 1):
                dup("q", p, 0)
                dup("k", p, 0)
            max_row(0, 0, 0)
            max_row(0, 1, 0)
            def batch(b, first=False):
                for i in range(8):
                    if first and i == 1:
                        sp.wait_ge(s["w_lo_done"], 3)
                        routing.load_constants(sp)
                    if i >= 2:
                        rden_out(i - 2, b)
                    if i < 7:
                        max_row(i + 1, 0, b)
                    if i <= 5:
                        dup("q", i + 2, b)
                        dup("k", i + 2, b)
                    if i >= 2:
                        rden_in(i - 2, b)
                    if i < 7:
                        max_row(i + 1, 1, b)
                    if i >= 1:
                        sums_out(i - 1, b)
                dup("q", 0, b + 1)
                rden_out(6, b)
                dup("k", 0, b + 1)
                rden_in(6, b)
                dup("q", 1, b + 1)
                dup("k", 1, b + 1)
                max_row(0, 0, b + 1)
                max_row(0, 1, b + 1)

            batch(0, first=True)
            with sp.Fori(1, NB) as b:
                batch(b)
            for p in (0, 1):
                sp.wait_ge(s_dup_q[p], dma_of_slot(NB, p))
                sp.wait_ge(s_dup_k[p], dma_of_slot(NB, p))
            for hh in range(2):
                sp.wait_ge(s_c[0][hh], dma_of_slot(NB, 0))

        @block.tensor
        def _(pe):
            pe.wait_ge(s["setup"], SETUP)
            for n in ("st_done", "av_done", "den_done", "proj_done"):
                pe.sem_inc(s[n], CR[n])

            def bank(part, kind, index, b):
                return work[bank_of[(part_of(part, b), kind, index)]]

            def transpose_x(part, b, bb):
                wait_work_free(pe, part, "xT", 0, b)
                pe.wait_ge(s["ln_done"], TILES * bb + TILES)
                out = bank(part, "xT", 0, bb)
                for tile in range(TILES):
                    mm = pe.transpose(out[:, tile * P:(tile + 1) * P], xn[:, tile, :], ident[:, :])
                mm.then_inc(s["xT_done"], 1)

            def project(part, w, p, b, bb):
                pe.wait_ge(s["xT_hi_done"], bb + 1)
                pe.wait_ge(s["xT_lo_done"], bb + 1)
                wait_work_free(pe, part, w, p, b)
                out, cols = bank(part, w, p, bb), slice(p * P, (p + 1) * P)
                pe.matmul(out[:, :], w_hi[w][:, cols], xT_hi[:, :], start=True, stop=False)
                pe.matmul(out[:, :], w_hi[w][:, cols], xT_lo[:, :], start=False, stop=False)
                pe.matmul(out[:, :], w_lo[w][:, cols], xT_hi[:, :], start=False, stop=True).then_inc(s["qk_done"], 1)

            def values(v, b):
                wait_work_free(pe, "body", "v", v, b)
                out, rows, cols = bank("body", "v", v, b), slice(v // 2 * P, v // 2 * P + P), slice(v % 2 * 512, v % 2 * 512 + 512)
                pe.matmul(out[:, :], xT_hi[:, rows], w_hi["v"][:, cols], start=True, stop=False)
                pe.matmul(out[:, :], xT_hi[:, rows], w_lo["v"][:, cols], start=False, stop=False)
                pe.matmul(out[:, :], xT_lo[:, rows], w_hi["v"][:, cols], start=False, stop=True).then_inc(s["v_done"], 1)

            def max_scores(p, j, bb, first=False):
                slot, hh = p % SLOTS, j // 4
                if j == 0:
                    g = 16 * bb + 2 * p + 1
                    pe.wait_ge(s["hi_done"], 2 * g + 2)
                    pe.wait_ge(s["lo_done"], 2 * g + 2)
                    pe.wait_ge(s_dup_k[slot], dma_of_slot(bb, p))
                if not (first and j < 2):
                    pe.wait_ge(s["max_done"], 64 * bb + 8 * p + j - 1)
                pe.matmul(mx[j % 2][:, :], T1q[:, slot, hh, j % 4:512:4], T1k[:, slot, hh, :],
                          start=True, stop=True).then_inc(s["mx_done"], 1)

            def scores(p, u, b):
                slot, hh, cols = p % SLOTS, u // 4, slice(u % 4 * P, u % 4 * P + P)
                pe.wait_ge(s["exp_done"], v_sum("exp_done", 64 * b + 8 * p + u - 1))
                pe.matmul(st[u % 2][:, :], T1k[:, slot, hh, cols], T1q[:, slot, hh, :], start=True, stop=False)
                if u == 0:
                    pe.wait_ge(s_dup_q[slot], dma_of_slot(b, p))
                if u % 4 == 0:
                    pe.wait_ge(s_c[slot][hh], dma_of_slot(b, p))
                pe.matmul(st[u % 2][:, :], T2k[:, slot, hh, cols], T2q[:, slot, hh, :],
                          start=False, stop=True).then_inc(s["st_done"], 1)

            def attend(p, blk, b):
                if blk == 0:
                    pe.wait_ge(s["o_done"], v_sum("o_done", 8 * b + p - 1))
                    if p == 0:
                        pe.wait_ge(s["proj_copied"], v_sum("proj_copied", b))
                        pe.wait_ge(s["v_act"], 4 * b + 4)
                        pe.wait_ge(s["v_dve"], 4 * b + 4)
                pe.wait_ge(s["exp_done"], v_sum("exp_done", 64 * b + 8 * p + 4 + blk + 1))
                for hh in range(2):
                    h = 2 * p + hh
                    mm = pe.matmul(ob[p % 2][64 * hh:64 * hh + 64, :], V[:, blk, 64 * h:64 * h + 64],
                                   probs[:, p % 2, hh, blk, :], start=(blk == 0), stop=(blk == TILES - 1))
                if blk == TILES - 1:
                    mm.then_inc(s["av_done"], 1)

            def denominators(p, b):
                pe.wait_ge(s["sums_done"], v_sum("sums_done", 16 * b + 2 * p + 2))
                wait_work_free(pe, "body", "den", p, b)
                for hh in range(2):
                    mm = pe.matmul(bank("body", "den", p, b)[64 * hh:64 * hh + 64, :], ones[:, :],
                                   prob_sums[:, p % 2, hh, :], start=True, stop=True)
                mm.then_inc(s["den_done"], 1)

            def out_project(p, b):
                if p == 0:
                    pe.wait_ge(s["o_done"], v_sum("o_done", 8 * b + 7))
                if p == PAIRS - 1:
                    pe.wait_ge(s["last_scaled"], b + 1)
                else:
                    pe.wait_ge(s["scaled"], v_sum("scaled", 7 * b + p + 1))
                mm = pe.matmul(ob[0][:, :], wp[:, p, :], out_T[:, p, :], start=(p == 0), stop=(p == PAIRS - 1))
                if p == PAIRS - 1:
                    mm.then_inc(s["proj_done"], 1)

            def transpose_out(b):
                pe.wait_ge(s["proj_copied"], v_sum("proj_copied", b + 1))
                wait_work_free(pe, "body", "x1T", 0, b)
                for tile in range(TILES):
                    mm = pe.transpose(bank("body", "x1T", 0, b)[:, tile * P:(tile + 1) * P],
                                      proj_T[:, tile * P:(tile + 1) * P], ident[:, :])
                mm.then_inc(s["x1T_done"], 1)

            transpose_x("head", 0, 0)
            for p in (0, 1):
                for w in "qk":
                    if p == 0:
                        pe.wait_ge(s["w_lo_done"], "qkv".index(w) + 1)
                    project("head", w, p, 0, 0)
            for j in range(8):
                max_scores(0, j, 0, first=True)
            pe.wait_ge(s["w_lo_done"], 3)
            pe.wait_ge(s["wp_in"], 48)

            def batch(b, first=False):
                for i in range(8):
                    for u in range(8):
                        scores(i, u, b)
                        if i < 7:
                            max_scores(i + 1, u, b)
                        if i <= 5 and u in PROJECT_AT:
                            project("body", PROJECT_AT[u], i + 2, b, b)
                        if i == 0:
                            for v in VALUES_AT.get(u, ()):
                                values(v, b)
                        if not first and (i, u) == (5, 4):
                            wait_work_free(pe, "body", "rT", 0, b)
                            routing.transpose_rows(pe, bank("body", "rT", 0, b), b - 1)
                        if not first and (i, u) == (6, 1):
                            wait_work_free(pe, "body", "dots", 0, b)
                            routing.centroid_products(pe, bank("body", "dots", 0, b), (xT_hi, xT_lo), b - 1)
                        if not first and (i, u) == (7, 3):
                            wait_work_free(pe, "body", "places", 0, b)
                            wait_work_free(pe, "body", "totals", 0, b)
                            routing.places(pe, bank("body", "places", 0, b), bank("body", "totals", 0, b), b - 1)
                        if i >= 1 and u in ATTEND_AT:
                            attend(i - 1, ATTEND_AT[u], b)
                        if i >= 1 and u == SUMS_AT:
                            denominators(i - 1, b)
                        if i == 6 and u == 7:
                            transpose_x("body", b, b + 1)
                project("body", "q", 0, b, b + 1)
                attend(7, 0, b)
                project("body", "k", 0, b, b + 1)
                attend(7, 1, b)
                project("body", "q", 1, b, b + 1)
                attend(7, 2, b)
                attend(7, 3, b)
                denominators(7, b)
                project("body", "k", 1, b, b + 1)
                for j in range(6):
                    max_scores(0, j, b + 1)
                    out_project(j, b)
                out_project(6, b)
                out_project(7, b)
                max_scores(0, 6, b + 1)
                max_scores(0, 7, b + 1)
                transpose_out(b)

            batch(0, first=True)
            with pe.Fori(1, NB) as b:
                batch(b)

        @block.scalar
        def _(act):
            for n, w in enumerate("qkv"):
                act.dma_start(w_raw[:, n, :].rearrange("d (h e) -> d h e", h=sh.H),
                              dram["W" + w].rearrange("h d e -> d h e")).then_inc(s_w[w], 16)
            for hh in range(2):
                act.dma_start(wp[64 * hh:64 * hh + 64, :, :],
                              dram["Wp"].rearrange("(e p hh) o -> hh e p o", p=PAIRS, hh=2)[hh]
                              ).then_inc(s["wp_in"], 16)
            act.dma_start(bp[:, :], dram["bp"].rearrange("(o a) -> o a", a=1)).then_inc(s["wp_in"], 16)
            act.sem_inc(s["exp_done"], CR["exp_done"])
            act.sem_inc(s["o_done"], CR["o_done"])
            act.sem_inc(s["proj_copied"], CR["proj_copied"])
            act.sem_inc(s["den_copied"], CR["den_copied"])

            def weights_hi(w):
                act.wait_ge(s_w[w], 16)
                nc.scalar.activation(w_hi[w][:, :], w_raw[:, "qkv".index(w), :], ACT.Copy).then_inc(s["w_hi_done"], 1)

            def bank(part, kind, index, b):
                return work[bank_of[(part_of(part, b), kind, index)]]

            def x_hi(part, bb):
                if part == "body":
                    act.wait_ge(s["qk_done"], 16 * bb)
                act.wait_ge(s["xT_done"], bb + 1)
                nc.scalar.activation(xT_hi[:, :], bank(part, "xT", 0, bb)[:, :], ACT.Copy).then_inc(s["xT_hi_done"], 1)

            def hi(part, w, p, bb):
                if part == "body":
                    prev = pair_before_in_slot(bb, p)
                    act.wait_ge(s["st_done"], v_sum("st_done", 8 * prev + 8))
                act.wait_ge(s["qk_done"], 16 * bb + 2 * p + (w == "k") + 1)
                dst = T1q if w == "q" else T1k
                for hh in range(2):
                    nc.scalar.activation(dst[0:64, p % SLOTS, hh, :],
                                         bank(part, w, p, bb)[64 * hh:64 * hh + 64, :], ACT.Copy
                                         ).then_inc(s["hi_done"], 1)

            def value_copy(v, b):
                act.wait_ge(s["av_done"], v_sum("av_done", 8 * b))
                act.wait_ge(s["v_done"], 8 * b + v + 1)
                nc.scalar.activation(V[:, v // 2, v % 2 * 512:v % 2 * 512 + 512], bank("body", "v", v, b)[:, :],
                                     ACT.Copy).then_inc(s["v_act"], 1)

            def exponentials(p, u, b):
                hh, blk = u // 4, u % 4
                if u == 0:
                    act.wait_ge(s["av_done"], v_sum("av_done", 8 * b + p - 1))
                    act.wait_ge(s["sums_done"], v_sum("sums_done", 16 * b + 2 * p - 2))
                act.wait_ge(s["st_done"], v_sum("st_done", 64 * b + 8 * p + u + 1))
                nc.scalar.activation(probs[:, p % 2, hh, blk, :], st[u % 2][:, :], ACT.Exp,
                                     scale=0.125).then_inc(s["exp_done"], 1)

            def out_copy(p, b):
                if p == 0:
                    act.wait_ge(s["proj_done"], v_sum("proj_done", b))
                act.wait_ge(s["av_done"], v_sum("av_done", 8 * b + p + 1))
                nc.scalar.activation(out_T[:, p, :], ob[p % 2][:, :], ACT.Copy).then_inc(s["o_done"], 1)

            def den_copy(p, b):
                act.wait_ge(s["rden_done"], v_sum("rden_done", 7 * b + max(p - 1, 0)))
                act.wait_ge(s["den_done"], v_sum("den_done", 8 * b + p + 1))
                nc.scalar.activation(den_rows[:, p % 2, :], bank("body", "den", p, b)[:, :], ACT.Copy
                                     ).then_inc(s["den_copied"], 1)

            weights_hi("q")
            x_hi("head", 0)
            weights_hi("k")
            for p in (0, 1):
                for w in "qk":
                    hi("head", w, p, 0)
            weights_hi("v")
            act.wait_ge(s["wp_in"], 48)
            def batch(b, first=False):
                for i in range(8):
                    for u in range(8):
                        exponentials(i, u, b)
                        if i <= 5 and u in PROJECT_AT:
                            hi("body", PROJECT_AT[u], i + 2, b)
                        if i == 0:
                            for v in VALUES_AT.get(u, ()):
                                if v % 2 == 0:
                                    value_copy(v, b)
                        if i >= 1 and u == 6:
                            out_copy(i - 1, b)
                            den_copy(i - 1, b)
                        if i == 7 and u == 0:
                            x_hi("body", b + 1)
                        if first and (i, u) == (2, 7):
                            routing.centroids_hi(act)
                        if not first and (i, u) == (2, 5):
                            routing.squares_n(act, b - 1)
                        if not first and (i, u) == (5, 5):
                            routing.rows_hi(act, bank("body", "rT", 0, b), (xT_hi, xT_lo), b - 1)
                        if not first and (i, u) == (5, 7):
                            routing.squares_r(act, b - 1)
                            routing.rows_x(act, b - 1)
                for w in "qk":
                    hi("body", w, 0, b + 1)
                hi("body", "q", 1, b + 1)
                out_copy(7, b)
                hi("body", "k", 1, b + 1)
                act.wait_ge(s["proj_done"], v_sum("proj_done", b + 1))
                nc.scalar.activation(proj_T[:, :], ob[0][:, :], ACT.Identity, bias=bp[:, 0:1]
                                     ).then_inc(s["proj_copied"], 1)

            batch(0, first=True)
            with act.Fori(1, NB) as b:
                batch(b)

        @block.vector
        def _(dve):
            for n in ("rden_done", "x1_done"):
                dve.sem_inc(s[n], CR[n])
            nc.vector.memset(T2k[64:P].bitcast(F32), 0.0).then_inc(s["T2k_zero"], 1)
            nc.vector.memset(ones[:, :], 1.0).then_inc(s["setup"], 1)
            dve.wait_ge(s["T2k_zero"], 1)
            nc.vector.memset(T2k[64:65].bitcast(F32), 1.0).then_inc(s["setup"], 1)

            def bank(part, kind, index, b):
                return work[bank_of[(part_of(part, b), kind, index)]]

            def layer_norm(part, bb, at):
                steps = 3 * bb
                for tile in range(TILES):
                    last = nc.vector.bn_stats(stats[:, tile, :], x[:, bass.ds(at + tile, 1), :])
                last.then_inc(s["ln_step"], 1)
                dve.wait_ge(s["ln_step"], steps + 1)
                nc.vector.memset(pause[:, :], 0.0)
                for tile in range(TILES):
                    last = nc.vector.bn_aggr(meanvar[:, tile, :], stats[:, tile, :])
                last.then_inc(s["ln_step"], 1)
                dve.wait_ge(s["ln_step"], steps + 2)
                nc.vector.tensor_scalar(varps[:, :], meanvar[:, :, 1], 1e-5, None, ALU.add).then_inc(s["ln_step"], 1)

            def normalise(part, bb, at):
                dve.wait_ge(s["rstd_ready"], bb + 1)
                if part == "body":
                    dve.wait_ge(s["xT_done"], bb)
                for tile in range(TILES):
                    nc.vector.tensor_scalar(xn[:, tile, :], x[:, bass.ds(at + tile, 1), :], meanvar[:, tile, 0:1],
                                            rstd[:, tile:tile + 1], ALU.subtract, ALU.mult
                                            ).then_inc(s["ln_done"], 1)

            def x_lo(part, bb):
                dve.wait_ge(s["xT_hi_done"], bb + 1)
                nc.vector.tensor_tensor(xT_lo[:, :], bank(part, "xT", 0, bb)[:, :], xT_hi[:, :].bitcast(F32),
                                        ALU.subtract).then_inc(s["xT_lo_done"], 1)

            def lo(part, w, p, bb):
                g = 16 * bb + 2 * p + (w == "k")
                for hh in range(2):
                    dve.wait_ge(s["hi_done"], 2 * g + hh + 1)
                    out = T1q[64:P, p % SLOTS, hh, :] if w == "q" else T2k[0:64, p % SLOTS, hh, :]
                    up = (T1q if w == "q" else T1k)[0:64, p % SLOTS, hh, :]
                    nc.vector.tensor_tensor(out, bank(part, w, p, bb)[64 * hh:64 * hh + 64, :], up.bitcast(F32),
                                            ALU.subtract).then_inc(s["lo_done"], 1)

            def negated_max(p, j, bb):
                dve.wait_ge(s["mx_done"], 64 * bb + 8 * p + j + 1)
                nc.vector.tensor_reduce(negmax[:, p % SLOTS, j // 4, j % 4:j % 4 + 1], mx[j % 2][:, :], AX.X, ALU.max,
                                        negate=True).then_inc(s["max_done"], 1)

            def value_copy(v, b):
                dve.wait_ge(s["av_done"], v_sum("av_done", 8 * b))
                dve.wait_ge(s["v_done"], 8 * b + v + 1)
                nc.vector.tensor_copy(V[:, v // 2, v % 2 * 512:v % 2 * 512 + 512], bank("body", "v", v, b)[:, :]
                                      ).then_inc(s["v_dve"], 1)

            def reciprocals(p, b):
                dve.wait_ge(s_n1[p % 2], 32 * of_parity(p) * b + 32 * (p // 2) + 32)
                dve.wait_ge(s["scaled"], v_sum("scaled", 7 * b + max(p - 1, 0)))
                nc.vector.reciprocal(rden[:, p % 2, :], den[:, p % 2, :]).then_inc(s["rden_done"], 1)

            def last_reciprocals(b):
                dve.wait_ge(s["den_done"], v_sum("den_done", 8 * b + 8))
                nc.vector.reciprocal(last_rden[:, :], bank("body", "den", 7, b)[:, :]).then_inc(s["last_rden"], 1)

            def last_scale(b):
                dve.wait_ge(s["o_done"], v_sum("o_done", 8 * b + 8))
                dve.wait_ge(s["last_rden"], b + 1)
                nc.vector.tensor_tensor(out_T[:, 7, :], out_T[:, 7, :], last_rden[:, :], ALU.mult
                                        ).then_inc(s["last_scaled"], 1)

            def weights_lo(w):
                n = "qkv".index(w)
                dve.wait_ge(s["w_hi_done"], n + 1)
                nc.vector.tensor_tensor(w_lo[w][:, :], w_raw[:, n, :], w_hi[w][:, :].bitcast(F32), ALU.subtract
                                        ).then_inc(s["w_lo_done"], 1)

            dve.wait_ge(s["x0_in"], 16)
            layer_norm("head", 0, 0)
            normalise("head", 0, 0)
            weights_lo("q")
            x_lo("head", 0)
            weights_lo("k")
            for p in (0, 1):
                for w in "qk":
                    lo("head", w, p, 0)
            weights_lo("v")
            dve.wait_ge(s["x_in"], 16 * (NB - 1))
            for j in range(8):
                negated_max(0, j, 0)
            def batch(b, first=False):
                nxt = TILES * ((b + 1) % NB)
                for i in range(8):
                    order = {u: [("m", u)] for u in range(8)}
                    for u, w in PROJECT_AT.items():
                        order[u] += [("lo", w)]
                    order[1] += [("r", 0)]
                    for u in range(8):
                        if (i, u) == (7, 1):
                            x_lo("body", b + 1)
                        for what, n in order.get(u, []):
                            if what == "m" and i < 7:
                                negated_max(i + 1, n, b)
                            if what == "lo" and i <= 5:
                                lo("body", n, i + 2, b)
                            if what == "r" and i >= 2:
                                reciprocals(i - 2, b)
                        if i == 0:
                            for v in VALUES_AT.get(u, ()):
                                if v % 2 == 1:
                                    value_copy(v, b)
                        if not first and (i, u) == (2, 1):
                            routing.normalise(dve, b - 1, TILES * (b - 1))
                        if not first and (i, u) == (3, 3):
                            routing.mean_square(dve, b - 1)
                        if not first and (i, u) == (5, 6):
                            routing.rows_lo(dve, bank("body", "rT", 0, b), (xT_hi, xT_lo), b - 1)
                        if not first and (i, u) == (6, 4):
                            routing.route(dve, bank("body", "dots", 0, b), b - 1)
                        if not first and (i, u) == (7, 5):
                            routing.rows_of_tokens(dve, bank("body", "places", 0, b), bank("body", "totals", 0, b), b - 1)
                    if first and i == 2:
                        routing.constants(dve)
                    if not first and i == 0:
                        dve.wait_ge(s["x1_done"], v_sum("x1_done", b))
                        routing.norm_stats(dve, b - 1, TILES * (b - 1))
                    if not first and i == 4:
                        routing.rms_norm(dve, b - 1)
                    if i == 3:
                        layer_norm("body", b + 1, nxt)
                    if i == 5:
                        normalise("body", b + 1, nxt)
                for p in (0, 1):
                    for w in "qk":
                        lo("body", w, p, b + 1)
                    if p == 0:
                        reciprocals(6, b)
                for j in range(8):
                    negated_max(0, j, b + 1)
                    if j == 3:
                        last_reciprocals(b)
                        last_scale(b)
                dve.wait_ge(s["x1T_done"], b + 1)
                xb = x[:, bass.ds(TILES * b, TILES), :].rearrange("p t d -> p (t d)")
                nc.vector.tensor_tensor(xb, xb, bank("body", "x1T", 0, b)[:, :], ALU.add).then_inc(s["x1_done"], 1)

            batch(0, first=True)
            with dve.Fori(1, NB) as b:
                batch(b)

        @block.gpsimd
        def _(pool):
            for n in ("sums_done", "scaled"):
                pool.sem_inc(s[n], CR[n])
            nc.gpsimd.memset(power[:, :], -0.5).then_inc(s["setup"], 1)
            nc.gpsimd.memset(ident[:, :], 0.0).then_inc(s["ident_step"], 1)
            pool.wait_ge(s["ident_step"], 1)
            nc.gpsimd.affine_select(out=ident[:, :], in_=ident[:, :], compare_op=ALU.not_equal, fill=1.0, base=0,
                                    pattern=[[-1, P]], channel_multiplier=1).then_inc(s["ident_step"], 1)

            def inverse_std(bb):
                pool.wait_ge(s["ln_step"], 3 * bb + 3)
                nc.gpsimd.tensor_tensor(rstd[:, :], varps[:, :], power[:, :], ALU.pow).then_inc(s["rstd_ready"], 1)

            def sums(p, hh, b):
                pool.wait_ge(s["exp_done"], v_sum("exp_done", 64 * b + 8 * p + 4 * hh + 4))
                pool.wait_ge(s["sums_done"], v_sum("sums_done", 16 * b + 2 * p + hh))
                pr = probs[:, p % 2, hh]
                nc.gpsimd.tensor_tensor(half_sums[:, :, :], pr[:, 0:2, :], pr[:, 2:4, :], ALU.add
                                        ).then_inc(s["sums_step"], 1)
                pool.wait_ge(s["sums_step"], 16 * b + 2 * p + hh + 1)
                if hh == 0:
                    pool.wait_ge(s["den_done"], v_sum("den_done", 8 * b + p - 1))
                nc.gpsimd.tensor_tensor(prob_sums[:, p % 2, hh, :], half_sums[:, 0, :], half_sums[:, 1, :], ALU.add
                                        ).then_inc(s["sums_done"], 1)

            def scale(p, b):
                pool.wait_ge(s["o_done"], v_sum("o_done", 8 * b + p + 1))
                pool.wait_ge(s_n3[p % 2], 32 * of_parity(p) * b + 32 * (p // 2) + 32)
                nc.gpsimd.tensor_tensor(out_T[:, p, :], out_T[:, p, :], rden_rows[:, p % 2, :], ALU.mult
                                        ).then_inc(s["scaled"], 1)

            pool.wait_ge(s["ident_step"], 2)
            nc.gpsimd.memset(T2q[64:P].bitcast(F32), 0.0).then_inc(s["setup"], 1)
            pool.wait_ge(s["setup"], SETUP)
            inverse_std(0)
            def batch(b, first=False):
                for i in range(8):
                    if not first and i == 1:
                        routing.inverse_std(pool, b - 1)
                    if not first and i == 4:
                        routing.inverse_rms(pool, b - 1)
                    sums(i, 0, b)
                    if i >= 2:
                        scale(i - 2, b)
                    if i == 4:
                        inverse_std(b + 1)
                    if first and i == 1:
                        pool.wait_ge(s["w_lo_done"], 3)
                        routing.patterns(pool)
                    if not first and i == 3:
                        routing.residual(pool, b - 1, TILES * (b - 1))
                    sums(i, 1, b)
                scale(6, b)
                if not first:
                    routing.send(pool, b - 1)
                    routing.sent(pool, b - 1)

            batch(0, first=True)
            with pool.Fori(1, NB) as b:
                batch(b)




def feed_forward(nc, t, dram, sh, routing):
    NB, NE, TILES, N, D = sh.B, sh.NE, sh.TILES, sh.N, sh.D
    CH = sh.F // P
    bl = Blocks(sh)
    RUNS = bl.COUNT // RUN
    I32 = mybir.dt.int32

    with ExitStack() as ctx:
        def sb(name, shape, dt=F32):
            return ctx.enter_context(nc.sbuf_tensor(name, shape, dt))

        def pb(name):
            return ctx.enter_context(nc.psum_tensor(name, [P, 512], F32))

        def sem(name):
            return ctx.enter_context(nc.semaphore(name))

        ident = t["ident"]
        along_tile, across = routing.along_tile, routing.across
        up_raw = sb("up_raw", [P, NE * sh.F2])
        up_hi = sb("up_hi", [P, NE * sh.F2], F32R)
        up_lo = sb("up_lo", [P, NE * sh.F2], F32R)
        down_raw = sb("down_raw", [P, NE * CH * P])
        down_hi = sb("down_hi", [P, NE * CH * P], F32R)
        down_lo = sb("down_lo", [P, NE * CH * P], F32R)
        block_no_int = sb("block_no_int", [P, bl.COUNT], I32)
        block_no = sb("block_no", [P, bl.COUNT])
        filling = sb("filling", [P, bl.WIDTH])
        hold = sb("hold2", [P, 1])
        power = sb("power3", [P, 1])
        next_row_int = sb("next_row_int", [P, NE], I32)
        tokens = sb("tokens", [P, NE])
        over = sb("over", [P, NE, bl.TOKEN_TILES])
        PAD = NE
        ends = [sb(f"ends{i}", [P, PAD + NE]) for i in range(4)]
        skip = sb("skip", [P, NE])
        past = sb("past", [P, bl.COUNT, NE])
        skipped = sb("skipped", [P, bl.COUNT, NE])
        BEHIND = 2
        expert_f = sb("expert_f", [P, bl.COUNT])
        expert = sb("expert", [P, BEHIND + bl.COUNT + RUN - BEHIND])
        weights_at = sb("weights_at", [P, RUNS + 1, 2 * RUN], I32)
        start_f = sb("start_f", [P, bl.COUNT])
        start = sb("start", [P, bl.COUNT], I32)
        xb = sb("xb", [P, RUN, P])
        rest = sb("rest", [P, RUN, P + 1])
        xbT_hi = sb("xbT_hi", [P, 2, P], F32R)
        xbT_lo = sb("xbT_lo", [P, 2, P], F32R)
        gate = sb("gate", [P, 2, sh.F])
        act_f = sb("act_f", [P, 2, sh.F])
        act_hi = sb("act_hi", [P, 2, sh.F], F32R)
        act_lo = sb("act_lo", [P, 2, sh.F], F32R)

        xT = [sb("x2T_hi", [P, N], F32R), sb("x2T_lo", [P, N], F32R)]

        turn = [pb("turn0"), pb("turn1")]
        hidden = [pb("hidden0"), pb("hidden1")]
        actT = [pb("actT0"), pb("actT1")]
        yb = [pb("y0"), pb("y1")]

        names = """up_in down_in up_hi_done down_hi_done weights_split held block_no_done fill_done empty_out
            pool_setup tables_step tables_ready fill_out
            xbT_done xbT_hi_done xbT_lo_done up_done gate_done act_done actT_done act_hi_done act_lo_done down_done
            result_ready""".split()
        s = {n: sem("f_" + n) for n in names}
        s_xb = [sem(f"f_xb{i}") for i in range(RUN)]
        s_rest = [sem(f"f_rest{i}") for i in range(RUN)]
        s_out = [sem(f"f_out{i}") for i in range(RUN)]
        CR = {"xbT_done": RUN, "down_done": 2, "xbT_lo_done": 2, "act_done": 2, "act_lo_done": 2,
              "result_ready": 2, "held": 1}
        last = NB - 1
        block = ctx.enter_context(nc.Block())
        out_rows = dram["out"].rearrange("b n d -> (b n) d")
        sorted_rows = dram["sorted"]

        @block.sync
        def _(sp):
            sp.dma_start(up_raw[:, :].rearrange("d (e f) -> d e f", e=NE), dram["up_w"].rearrange("e d f -> d e f")
                         ).then_inc(s["up_in"], 16)
            sp.dma_start(down_raw[:, :].rearrange("f (c d) -> f c d", d=D),
                         dram["down_w"].rearrange("e (c f) d -> f (e c) d", c=CH)).then_inc(s["down_in"], 16)
            sp.wait_ge(s["fill_done"], 2)
            for i in range(bl.EMPTY):
                at = (NE * bl.REGION_BLOCKS + i) * P
                sp.dma_start(sorted_rows[at:at + P, :], filling[:, :]).then_inc(s["empty_out"], 16)
            sp.wait_ge(s["tables_ready"], 5)
            ends_at = [sp.alloc_register(f"end_of_expert{e}") for e in range(NE)]
            sp.load(ends_at, next_row_int[0:1, 0:NE])
            for e in range(NE):
                at = sp.snap(ends_at[e], min_val=0, max_val=NE * bl.REGION_BLOCKS * P - P)
                sp.dma_start(sorted_rows[bass.ds(at, P), :], filling[:, :]).then_inc(s["fill_out"], 16)
            sp.wait_ge(s["empty_out"], 16 * bl.EMPTY)
            sp.wait_ge(s["fill_out"], 16 * NE)
            routing.sent(sp, last)

            starts = [[sp.alloc_register(f"start_of_block{i}{u}") for u in range(RUN)] for i in range(2)]

            def load_starts(i, r):
                sp.load(starts[i], start[0:1, bass.ds(RUN * r, RUN)])

            def row_of_block(i, u):
                return sp.snap(starts[i][u], min_val=0, max_val=bl.ROWS - P)

            def load_x(r, u, first=False):
                at = row_of_block(1, u)
                if not first:
                    sp.wait_ge(s["xbT_done"], RUN * r + u - RUN + 1 + CR["xbT_done"])
                sp.dma_start(xb[:, u, :], sorted_rows[bass.ds(at, P), 0:P]).then_inc(s_xb[u], 16)

            def load_rest(r, u, first=False):
                at = row_of_block(0, u)
                if not first:
                    sp.wait_ge(s_out[u], 16 * r)
                sp.dma_start(rest[:, u, :], sorted_rows[bass.ds(at, P), P:bl.WIDTH]).then_inc(s_rest[u], 16)

            load_starts(1, 0)
            for u in range(RUN):
                load_x(0, u, first=True)
            load_starts(0, 0)
            load_starts(1, 1)
            for u in range(RUN):
                load_rest(0, u, first=True)
                load_x(1, u)
            with sp.Fori(2, RUNS) as r:
                load_starts(0, r - 1)
                load_starts(1, r)
                for u in range(RUN):
                    load_rest(r - 1, u)
                    load_x(r, u)
            load_starts(0, RUNS - 1)
            for u in range(RUN):
                load_rest(RUNS - 1, u)

        @block.tensor
        def _(pe):
            for n in ("xbT_done", "down_done"):
                pe.sem_inc(s[n], CR[n])
            routing.transpose_rows(pe, turn[0], last)
            routing.centroid_products(pe, turn[1], xT, last)
            routing.places(pe, hidden[0], hidden[1], last)
            pe.wait_ge(s["tables_ready"], 5)

            def transpose_block(r, u):
                q, u = u // RUN, u % RUN
                j = RUN * (r + q) + u
                pe.wait_ge(s_xb[u], 16 * (r + q) + 16)
                pe.wait_ge(s["xbT_lo_done"], j - 1 + CR["xbT_lo_done"])
                pe.transpose(turn[u % 2][:, 0:P], xb[:, u, :], ident[:, :]).then_inc(s["xbT_done"], 1)

            def up(r, u):
                j = RUN * r + u
                pe.wait_ge(s["xbT_lo_done"], j + 1 + CR["xbT_lo_done"])
                pe.wait_ge(s["act_done"], j - 1 + CR["act_done"])
                w = bass.ds(place(RUN + u), sh.F2)
                pe.matmul(hidden[u % 2][:, :], xbT_hi[:, u % 2, :], up_hi[:, w], start=True, stop=False)
                pe.matmul(hidden[u % 2][:, :], xbT_hi[:, u % 2, :], up_lo[:, w], start=False, stop=False)
                pe.matmul(hidden[u % 2][:, :], xbT_lo[:, u % 2, :], up_hi[:, w], start=False, stop=True
                          ).then_inc(s["up_done"], 1)

            def transpose_hidden(r, u):
                j = RUN * r + u
                pe.wait_ge(s["act_done"], j + 1 + CR["act_done"])
                pe.wait_ge(s["act_lo_done"], j - 1 + CR["act_lo_done"])
                for c in range(CH):
                    mm = pe.transpose(actT[u % 2][:, c * P:(c + 1) * P], act_f[:, u % 2, c * P:(c + 1) * P], ident[:, :])
                mm.then_inc(s["actT_done"], 1)

            def down(r, u):
                j = RUN * r + u - BEHIND
                first = place(u)
                pe.wait_ge(s["act_lo_done"], j + 1 + CR["act_lo_done"])
                pe.wait_ge(s["result_ready"], j - 1 + CR["result_ready"])
                for c in range(CH):
                    rows_c, w = slice(c * P, (c + 1) * P), bass.ds(first + c * P, P)
                    pe.matmul(yb[u % 2][:, 0:P], act_hi[:, u % 2, rows_c], down_hi[:, w], start=(c == 0), stop=False)
                    pe.matmul(yb[u % 2][:, 0:P], act_hi[:, u % 2, rows_c], down_lo[:, w], start=False, stop=False)
                    mm = pe.matmul(yb[u % 2][:, 0:P], act_lo[:, u % 2, rows_c], down_hi[:, w], start=False,
                                   stop=(c == CH - 1))
                mm.then_inc(s["down_done"], 1)

            at = [pe.alloc_register(f"weights_at{i}") for i in range(2 * RUN)]

            def load_places(r):
                pe.load(at, weights_at[0:1, bass.ds(r, 1), :].rearrange("p o n -> p (o n)"))

            def place(i):
                most = (NE - 1) * (CH * P if i < RUN else sh.F2)
                return pe.snap(at[i], min_val=0, max_val=most)

            def run(r, first=False, last=False):
                load_places(r)
                for u in range(RUN):
                    up(r, u)
                    if not (first and u < 1):
                        transpose_hidden(r, u - 1)
                    if not (last and u >= RUN - 2):
                        transpose_block(r, u + 2)
                    if not (first and u < BEHIND):
                        down(r, u)

            transpose_block(0, 0)
            transpose_block(0, 1)
            pe.wait_ge(s["weights_split"], 2)
            run(0, first=True)
            with pe.Fori(1, RUNS - 1) as r:
                run(r)
            run(RUNS - 1, last=True)
            load_places(RUNS)
            transpose_hidden(RUNS - 1, RUN - 1)
            down(RUNS, 0)
            down(RUNS, 1)

        @block.scalar
        def _(act):
            routing.squares_n(act, last)
            routing.rows_hi(act, turn[0], xT, last)
            routing.squares_r(act, last)
            routing.rows_x(act, last)
            act.wait_ge(s["up_in"], 16)
            nc.scalar.activation(up_hi[:, :], up_raw[:, :], ACT.Copy).then_inc(s["up_hi_done"], 1)
            act.wait_ge(s["down_in"], 16)
            nc.scalar.activation(down_hi[:, :], down_raw[:, :], ACT.Copy).then_inc(s["down_hi_done"], 1)

            act.sem_inc(s["act_hi_done"], 1)

            def xb_hi(r, u):
                q, u = u // RUN, u % RUN
                act.wait_ge(s["xbT_done"], RUN * (r + q) + u + 1 + CR["xbT_done"])
                nc.scalar.activation(xbT_hi[:, u % 2, :], turn[u % 2][:, 0:P], ACT.Copy).then_inc(s["xbT_hi_done"], 1)

            def gates(r, u):
                j = RUN * r + u
                act.wait_ge(s["act_done"], j - 1 + CR["act_done"])
                act.wait_ge(s["up_done"], j + 1)
                nc.scalar.activation(gate[:, u % 2, :], hidden[u % 2][:, sh.F:sh.F2], ACT.Silu).then_inc(s["gate_done"], 1)

            def hidden_hi(r, u):
                act.wait_ge(s["actT_done"], RUN * r + u + 1)
                nc.scalar.activation(act_hi[:, u % 2, :], actT[u % 2][:, 0:sh.F], ACT.Copy).then_inc(s["act_hi_done"], 1)

            def run(r, first=False, last=False):
                for u in range(RUN):
                    gates(r, u)
                    if not (first and u < 1):
                        hidden_hi(r, u - 1)
                    if not (last and u >= RUN - 2):
                        xb_hi(r, u + 2)

            xb_hi(0, 0)
            xb_hi(0, 1)
            run(0, first=True)
            with act.Fori(1, RUNS - 1) as r:
                run(r)
            run(RUNS - 1, last=True)
            hidden_hi(RUNS - 1, RUN - 1)

        @block.vector
        def _(dve):
            for n in ("xbT_lo_done", "act_done", "act_lo_done", "result_ready"):
                dve.sem_inc(s[n], CR[n])
            at = TILES * last
            routing.norm_stats(dve, last, at)
            nc.vector.memset(filling[:, 0:2 * D], 0.0).then_inc(s["fill_done"], 1)
            nc.vector.memset(filling[:, 2 * D:bl.WIDTH].bitcast(I32), 2 * bl.TOKEN_TILES * P).then_inc(s["fill_done"], 1)
            for sums in ends:
                nc.vector.memset(sums[:, 0:PAD], 0.0)
            nc.vector.memset(expert[:, 0:BEHIND], 0.0)
            nc.vector.memset(expert[:, BEHIND + bl.COUNT:], 0.0)
            routing.normalise(dve, last, at)
            routing.mean_square(dve, last)
            routing.rms_norm(dve, last)
            dve.wait_ge(s["block_no_done"], 1)
            nc.vector.tensor_copy(block_no[:, :], block_no_int[:, :]).then_inc(s["block_no_done"], 1)
            routing.rows_lo(dve, turn[0], xT, last)
            routing.route(dve, turn[1], last)
            routing.rows_of_tokens(dve, hidden[0], hidden[1], last)
            dve.wait_ge(s["block_no_done"], 2)

            n = 0

            def table(ins):
                nonlocal n
                n += 1
                ins.then_inc(s["tables_step"], 1)
                dve.wait_ge(s["tables_step"], n)

            table(nc.vector.tensor_tensor(tokens[:, :], routing.next_row[:, :], routing.region[:, :], ALU.subtract))
            nc.vector.tensor_copy(next_row_int[:, :], routing.next_row[:, :]).then_inc(s["tables_ready"], 1)
            table(nc.vector.tensor_scalar(tokens[:, :], tokens[:, :], 1.0 / P, None, ALU.mult))
            table(nc.vector.tensor_tensor(over[:, :, :], along_tile(tokens[:, :], bl.TOKEN_TILES),
                                          across(block_no[:, 0:bl.TOKEN_TILES], NE), ALU.is_gt))
            table(nc.vector.tensor_reduce(ends[0][:, PAD:PAD + NE], over[:, :, :], AX.X, ALU.add))
            nc.vector.tensor_scalar(skip[:, :], ends[0][:, PAD:PAD + NE], -1.0, float(bl.REGION_BLOCKS), ALU.mult, ALU.add)
            for i in range(3):
                back = PAD - 2 ** i
                table(nc.vector.tensor_tensor(ends[i + 1][:, PAD:PAD + NE], ends[i][:, PAD:PAD + NE],
                                              ends[i][:, back:back + NE], ALU.add))
            table(nc.vector.tensor_tensor(past[:, :, :], along_tile(block_no[:, :], NE),
                                          across(ends[3][:, PAD:PAD + NE], bl.COUNT), ALU.is_ge))
            table(nc.vector.tensor_reduce(expert_f[:, :], past[:, :, :], AX.X, ALU.add))
            table(nc.vector.tensor_scalar(expert[:, BEHIND:BEHIND + bl.COUNT], expert_f[:, :], float(NE - 1), None, ALU.min))
            for part, (back, size) in enumerate(((0, CH * P), (BEHIND, sh.F2))):
                runs = RUNS + 1 - part
                nc.vector.tensor_scalar(weights_at[:, 0:runs, part * RUN:(part + 1) * RUN],
                                        expert[:, back:back + runs * RUN].rearrange("p (r u) -> p r u", u=RUN),
                                        float(size), None, ALU.mult).then_inc(s["tables_ready"], 1)
            nc.vector.memset(weights_at[:, RUNS, RUN:2 * RUN], 0).then_inc(s["tables_ready"], 1)
            table(nc.vector.tensor_tensor(skipped[:, :, :], past[:, :, :], across(skip[:, :], bl.COUNT), ALU.mult))
            table(nc.vector.tensor_reduce(start_f[:, :], skipped[:, :, :], AX.X, ALU.add))
            table(nc.vector.tensor_tensor(start_f[:, :], start_f[:, :], block_no[:, :], ALU.add))
            nc.vector.tensor_scalar(start[:, :], start_f[:, :], float(P), None, ALU.mult).then_inc(s["tables_ready"], 1)

            dve.wait_ge(s["up_hi_done"], 1)
            nc.vector.tensor_tensor(up_lo[:, :], up_raw[:, :], up_hi[:, :].bitcast(F32), ALU.subtract
                                    ).then_inc(s["weights_split"], 1)

            def xb_lo(r, u):
                q, u = u // RUN, u % RUN
                dve.wait_ge(s["xbT_hi_done"], RUN * (r + q) + u + 1)
                nc.vector.tensor_tensor(xbT_lo[:, u % 2, :], turn[u % 2][:, 0:P], xbT_hi[:, u % 2, :].bitcast(F32),
                                        ALU.subtract).then_inc(s["xbT_lo_done"], 1)

            def gated(r, u):
                dve.wait_ge(s["gate_done"], RUN * r + u + 1)
                nc.vector.tensor_tensor(act_f[:, u % 2, :], hidden[u % 2][:, 0:sh.F], gate[:, u % 2, :], ALU.mult
                                        ).then_inc(s["act_done"], 1)

            def hidden_lo(r, u):
                dve.wait_ge(s["act_hi_done"], RUN * r + u + 1 + 1)
                nc.vector.tensor_tensor(act_lo[:, u % 2, :], actT[u % 2][:, 0:sh.F], act_hi[:, u % 2, :].bitcast(F32),
                                        ALU.subtract).then_inc(s["act_lo_done"], 1)

            def result(r, u):
                q, u = u // RUN, u % RUN
                dve.wait_ge(s_rest[u], 16 * (r + q) + 16)
                dve.wait_ge(s["down_done"], RUN * (r + q) + u + 1 + CR["down_done"])
                nc.vector.tensor_tensor(rest[:, u, 0:D], rest[:, u, 0:D], yb[u % 2][:, 0:D], ALU.add
                                        ).then_inc(s["result_ready"], 1)

            def run(r, first=False, last=False):
                for u in range(RUN):
                    gated(r, u)
                    if not (first and u < 1):
                        hidden_lo(r, u - 1)
                    if not (last and u >= RUN - 2):
                        xb_lo(r, u + 2)
                    if not (first and u < BEHIND):
                        result(r, u - BEHIND)

            xb_lo(0, 0)
            xb_lo(0, 1)
            run(0, first=True)
            with dve.Fori(1, RUNS - 1) as r:
                run(r)
            run(RUNS - 1, last=True)
            hidden_lo(RUNS - 1, RUN - 1)
            result(RUNS - 1, RUN - 2)
            result(RUNS - 1, RUN - 1)

        @block.gpsimd
        def _(pool):
            nc.gpsimd.memset(power[:, :], -0.5).then_inc(s["pool_setup"], 1)
            nc.gpsimd.iota(block_no_int[:, :], pattern=[[1, bl.COUNT]], base=0, channel_multiplier=0
                           ).then_inc(s["block_no_done"], 1)
            pool.wait_ge(s["pool_setup"], 1)
            routing.inverse_std(pool, last)
            routing.residual(pool, last, TILES * last)
            routing.inverse_rms(pool, last)
            routing.send(pool, last)
            pool.wait_ge(s["down_hi_done"], 1)
            nc.gpsimd.tensor_tensor(down_lo[:, :], down_raw[:, :], down_hi[:, :].bitcast(F32), ALU.subtract
                                    ).then_inc(s["weights_split"], 1)

            pool.sem_inc(s["held"], CR["held"])
            last_token = pool.to_reg(bl.TOKEN_TILES * P - 1)
            with pool.Fori(0, RUNS) as r:
                for u in range(RUN):
                    pool.wait_ge(s["result_ready"], RUN * r + u + 1 + CR["result_ready"])
                    pool.wait_ge(s["held"], RUN * r + u + CR["held"])
                    nc.gpsimd.tensor_tensor(hold[:, :], power[:, :], power[:, :], ALU.add).then_inc(s["held"], 1)
                    nc.gpsimd.indirect_dma_start(
                        out_rows, bass.IndirectOffsetOnAxis(ap=rest[:, u, D:D + 1].bitcast(I32), axis=0),
                        rest[:, u, 0:D], None, bounds_check=last_token, oob_is_err=False
                    ).then_inc(s_out[u], 16)
            for u in range(RUN):
                pool.wait_ge(s_out[u], 16 * RUNS)




def _sorted_shape(dram):
    bl = Blocks(Shapes(dram["x"], dram["Wq"], dram["up_w"]))
    return [bl.ROWS, bl.WIDTH]


def build(nc, dram):
    sh = Shapes(dram["x"], dram["Wq"], dram["up_w"])
    with ExitStack() as ctx:
        x = ctx.enter_context(nc.sbuf_tensor("x_all", [P, sh.B * sh.TILES, P], F32))
        ident = ctx.enter_context(nc.sbuf_tensor("ident", [P, P], F32))
        staging = ctx.enter_context(nc.sbuf_tensor("staging", [P, 3, 1024], F32))
        t = {"x": x, "ident": ident, "staging": staging}
        routing = make_routing(nc, ctx, t, dram, sh)
        attention(nc, t, dram, sh, routing)
        feed_forward(nc, t, dram, sh, routing)


_INS = {
    "x": "L0_attn_query", "Wq": "L0_attn_Wq", "Wk": "L0_attn_Wk", "Wv": "L0_attn_Wv", "Wp": "L0_attn_Wp",
    "bp": "L0_attn_bp", "scale": "L0_ffn_scale", "centroids": "L0_ffn_centroids", "up_w": "L0_ffn_up_w",
    "down_w": "L0_ffn_down_w",
}


def kernel(**inputs):
    import numpy as _np
    import concourse.bacc as _bacc
    from concourse.bass_utils import run_bass_kernel_spmd as _run

    nc = _bacc.Bacc("TRN2", target_bir_lowering=False, num_devices=1)
    arrays, dram = {}, {}
    for name, given in _INS.items():
        a = _np.ascontiguousarray(inputs[given])
        arrays[f"in_{name}"] = a
        dram[name] = nc.dram_tensor(f"in_{name}", a.shape, mybir.dt.from_np(a.dtype), kind="ExternalInput").ap()
    shape = arrays["in_x"].shape
    dram["out"] = nc.dram_tensor("out_x", shape, F32, kind="ExternalOutput").ap()
    dram["rden"] = nc.dram_tensor("rden_rows_dram", [2, 2 * shape[1]], F32, kind="Internal").ap()
    sorted_shape = _sorted_shape(dram)
    dram["sorted"] = nc.dram_tensor("sorted_rows_dram", sorted_shape, F32, kind="Internal").ap()
    build(nc, dram)
    return _run(nc, [arrays], core_ids=[0]).results[0]["out_x"]
```
